# Optimizing a Trainium2 kernel written in Bass

```python
import numpy as np
import jax
import jax.numpy as jnp

def _softmax(x, axis=-1):
    return jax.nn.softmax(x, axis=axis)

def _gelu(x):
    return jax.nn.gelu(x, approximate=True)

def _silu(x):
    return jax.nn.silu(x)

def _sigmoid(x):
    return jax.nn.sigmoid(x)

def _layernorm(x, axis=-1, eps=1e-05):
    m = jnp.mean(x, axis=axis, keepdims=True)
    v = jnp.var(x, axis=axis, keepdims=True)
    return (x - m) / jnp.sqrt(v + eps)

def _scatter_add(tgt, idx, src, axis=0):
    return tgt.at[idx].add(src)

def _segment_sum(src, seg, n):
    return jax.ops.segment_sum(src, seg, n)
kernel_name = 'mk_hybrid_d2_jaxref_r8_84f127'

def setup_inputs(seed: int=0):
    np.random.seed(seed)
    _w = jnp.asarray

    def _L0_attn_a_setup():
        import jax, jax.numpy as jnp
        import numpy as np
        D_MODEL = 128
        NHEAD = 16
        HEAD_DIM = D_MODEL // NHEAD
        GN_EPS = 0.00064
        NORM_EPS = 1e-06
        B, T = (4, 128)

        def _xavier(key, shape):
            lim = float(np.sqrt(6.0 / (shape[0] + shape[1])))
            return jax.random.uniform(key, shape, jnp.float32, -lim, lim)

        def _l2norm(t):
            n = jnp.linalg.norm(t, axis=-1, keepdims=True)
            return t / jnp.maximum(n, NORM_EPS)
        key = jax.random.key(seed)
        ks = jax.random.split(key, 10)
        D = D_MODEL
        ddd = jnp.linspace(0.0, 1.0, D, dtype=jnp.float32)
        inp = {'x': jax.random.normal(ks[0], (B, T, D), jnp.float32), 'x_r': 1.0 - ddd ** 0.2, 'x_w': 1.0 - ddd ** 0.9, 'x_k': 1.0 - ddd ** 0.7, 'x_v': 1.0 - ddd ** 0.7, 'x_a': 1.0 - ddd ** 0.9, 'x_b': 1.0 - ddd ** 0.9, 'x_g': 1.0 - ddd ** 0.2, 'W_r': _xavier(ks[1], (D, D)), 'W_w': _xavier(ks[2], (D, D)), 'W_k': _xavier(ks[3], (D, D)), 'W_v': _xavier(ks[4], (D, D)), 'W_a': _xavier(ks[5], (D, D)), 'W_b': _xavier(ks[6], (D, D)), 'W_g': _xavier(ks[7], (D, D)), 'W_o': _xavier(ks[8], (D, D)) * 0.1, 'b_o': jnp.zeros((D,), jnp.float32), 'gn_w': jnp.ones((D,), jnp.float32), 'gn_b': jnp.zeros((D,), jnp.float32)}
        return inp
    _L0_attn_a_in = _L0_attn_a_setup()

    def _L0_attn_b_setup():
        import jax, jax.numpy as jnp
        import numpy as np
        EPS_LN = 1e-06
        STAB = 0.001

        def layer_norm(x, gamma, beta):
            mu = jnp.mean(x, axis=-1, keepdims=True)
            var = jnp.mean(jnp.square(x - mu), axis=-1, keepdims=True)
            return (x - mu) * jax.lax.rsqrt(var + EPS_LN) * gamma + beta
        key = jax.random.key(seed)
        B, L, E, H, F = (8, 256, 128, 16, 512)
        dh = E // H
        ks = jax.random.split(key, 12)
        s_attn = 1.0 / np.sqrt(E)
        s_ffn1 = 1.0 / np.sqrt(E)
        s_ffn2 = 1.0 / np.sqrt(F)
        return {'x': jax.random.normal(ks[0], (B, L, E), jnp.float32), 'gamma1': jnp.ones((E,), jnp.float32), 'beta1': jnp.zeros((E,), jnp.float32), 'wq': jax.random.normal(ks[1], (E, H, dh), jnp.float32) * s_attn, 'wk': jax.random.normal(ks[2], (E, H, dh), jnp.float32) * s_attn, 'wv': jax.random.normal(ks[3], (E, H, dh), jnp.float32) * s_attn, 'wo': jax.random.normal(ks[4], (H, dh, E), jnp.float32) * s_attn, 'w1': jax.random.normal(ks[5], (E, F), jnp.float32) * s_ffn1, 'b1': jnp.zeros((F,), jnp.float32), 'w2': jax.random.normal(ks[6], (F, E), jnp.float32) * s_ffn2, 'b2': jnp.zeros((E,), jnp.float32)}
    _L0_attn_b_in = _L0_attn_b_setup()

    def _L0_ffn_setup():
        import jax, jax.numpy as jnp
        import numpy as np
        H = 128
        I = 512
        E = 4
        LN_EPS = 1e-12

        def _layer_norm(x, gamma, beta, eps=LN_EPS):
            mu = jnp.mean(x, axis=-1, keepdims=True)
            var = jnp.mean(jnp.square(x - mu), axis=-1, keepdims=True)
            return (x - mu) * jax.lax.rsqrt(var + eps) * gamma + beta
        key = jax.random.key(seed)
        ks = jax.random.split(key, 8)
        B, S = (4, 64)
        scale = 0.02
        return {'hidden_states': jax.random.normal(ks[0], (B, S, H), jnp.float32), 'W_router': jax.random.normal(ks[1], (H, E), jnp.float32) * scale, 'W1': jax.random.normal(ks[2], (E, H, I), jnp.float32) * scale, 'b1': jax.random.normal(ks[3], (E, I), jnp.float32) * scale, 'Wo': jax.random.normal(ks[4], (I, H), jnp.float32) * scale, 'bo': jax.random.normal(ks[5], (H,), jnp.float32) * scale, 'ln_gamma': jnp.ones((H,), jnp.float32), 'ln_beta': jnp.zeros((H,), jnp.float32)}
    _L0_ffn_in = _L0_ffn_setup()

    def _L1_attn_a_setup():
        import math
        import jax, jax.numpy as jnp
        import numpy as np
        NUM_HEADS = 16
        HEAD_SIZE = 64
        HIDDEN = 128
        ROPE_BASE = 10000.0

        def _rope_cos_sin(seq_len, dim, dtype):
            inv_freq = 1.0 / ROPE_BASE ** (jnp.arange(0, dim, 2, dtype=jnp.float32) / dim)
            t = jnp.arange(seq_len, dtype=jnp.float32)
            freqs = jnp.einsum('s,d->sd', t, inv_freq)
            emb = jnp.concatenate([freqs, freqs], axis=-1)
            return (jnp.cos(emb).astype(dtype), jnp.sin(emb).astype(dtype))

        def _rotate_half(x):
            half = x.shape[-1] // 2
            return jnp.concatenate([-x[..., half:], x[..., :half]], axis=-1)

        def _apply_rope(q, k):
            cos, sin = _rope_cos_sin(q.shape[-2], q.shape[-1], q.dtype)
            q = q * cos + _rotate_half(q) * sin
            k = k * cos + _rotate_half(k) * sin
            return (q, k)
        key = jax.random.key(seed)
        ks = jax.random.split(key, 9)
        B, S = (2, 512)
        dt = jnp.bfloat16
        lim_in = 1.0 / math.sqrt(HIDDEN)
        inp = {'input_embeds': jax.random.normal(ks[0], (B, S, HIDDEN), dtype=dt), 'Wq': jax.random.uniform(ks[1], (NUM_HEADS * HEAD_SIZE, HIDDEN), dtype=dt, minval=-lim_in, maxval=lim_in), 'bq': jnp.zeros((NUM_HEADS * HEAD_SIZE,), dtype=dt), 'Wk': jax.random.uniform(ks[2], (NUM_HEADS * HEAD_SIZE, HIDDEN), dtype=dt, minval=-lim_in, maxval=lim_in), 'bk': jnp.zeros((NUM_HEADS * HEAD_SIZE,), dtype=dt), 'Wv': jax.random.uniform(ks[3], (NUM_HEADS * HEAD_SIZE, HIDDEN), dtype=dt, minval=-lim_in, maxval=lim_in), 'bv': jnp.zeros((NUM_HEADS * HEAD_SIZE,), dtype=dt), 'Wo': jax.random.uniform(ks[4], (HIDDEN, NUM_HEADS * HEAD_SIZE), dtype=dt, minval=-lim_in, maxval=lim_in), 'bo': jnp.zeros((HIDDEN,), dtype=dt)}
        return inp
    _L1_attn_a_in = _L1_attn_a_setup()

    def _L1_attn_b_setup():
        import jax, jax.numpy as jnp
        import numpy as np
        B, L, D = (2, 512, 128)
        EXPAND = 2
        D_INNER = D * EXPAND
        K, M = (32, 1)
        H = D_INNER // K
        KS = 4
        NA = 4
        ND = K - NA
        C = 2 * D_INNER + K
        SD = H * M
        key = jax.random.key(seed)
        ks = jax.random.split(key, 8)
        x = jax.random.normal(ks[0], (B, L, D), jnp.float32)
        in_proj_w = jax.random.normal(ks[1], (D, C), jnp.float32) * (1.0 / np.sqrt(D))
        conv_k = jax.random.normal(ks[2], (KS, 1, C), jnp.float32) * 0.3
        conv_b = jnp.zeros((C,), jnp.float32)
        grid = np.linspace(0.1, 1.5, K * H).reshape(1, 1, K, H, 1)
        signs = np.resize([1.0, -1.0], grid.shape)
        theta = jnp.asarray(grid * signs, jnp.float32)
        decay_slopes = jnp.asarray(np.log(np.exp(np.geomspace(0.001, 0.1, ND)) - 1.0), jnp.float32)
        anchor_slopes = jnp.asarray(np.log(np.exp(np.geomspace(0.01, 0.1, NA)) - 1.0), jnp.float32)
        score_scale = jnp.ones((K,), jnp.float32)
        deriv_logits = jnp.asarray([5.0, 0.0, 0.0], jnp.float32)
        glorot = np.sqrt(2.0 / (SD + H))
        W_re = jax.random.normal(ks[3], (SD, H), jnp.float32) * glorot
        W_im = jax.random.normal(ks[4], (SD, H), jnp.float32) * glorot
        norm_scale = jnp.ones((2 * SD,), jnp.float32)
        out_proj_w = jax.random.normal(ks[5], (D_INNER, D), jnp.float32) * (1.0 / np.sqrt(D_INNER))
        return dict(x=x, in_proj_w=in_proj_w, conv_k=conv_k, conv_b=conv_b, theta=theta, decay_slopes=decay_slopes, anchor_slopes=anchor_slopes, score_scale=score_scale, deriv_logits=deriv_logits, W_re=W_re, W_im=W_im, norm_scale=norm_scale, out_proj_w=out_proj_w)
    _L1_attn_b_in = _L1_attn_b_setup()

    def _L1_ffn_setup():
        import jax, jax.numpy as jnp
        import numpy as np
        B, T, DIM = (4, 128, 128)
        H, E, DH, K = (8, 5, 64, 3)

        def _topk_mask(s, k):
            idx = jax.lax.top_k(s, k)[1]
            return jnp.sum(jax.nn.one_hot(idx, s.shape[-1], dtype=s.dtype), axis=-2)
        key = jax.random.key(seed)
        ks = jax.random.split(key, 6)
        w = lambda k, shape: jax.random.normal(k, shape, jnp.float32) * 0.02
        return {'x': jax.random.normal(ks[0], (B, T, DIM), jnp.float32), 'Wq': w(ks[1], (DIM, H * E * DH)), 'Wkv': w(ks[2], (DIM, 2 * H * E * DH)), 'Ws': w(ks[3], (DIM, H * E)), 'Wd': w(ks[4], (DIM, H * E)), 'Wo': w(ks[5], (DH, E * DIM))}
    _L1_ffn_in = _L1_ffn_setup()
    _d = {'L0_attn_a_x': _L0_attn_a_in['x'], 'L0_attn_a_x_r': _L0_attn_a_in['x_r'], 'L0_attn_a_x_w': _L0_attn_a_in['x_w'], 'L0_attn_a_x_k': _L0_attn_a_in['x_k'], 'L0_attn_a_x_v': _L0_attn_a_in['x_v'], 'L0_attn_a_x_a': _L0_attn_a_in['x_a'], 'L0_attn_a_x_b': _L0_attn_a_in['x_b'], 'L0_attn_a_x_g': _L0_attn_a_in['x_g'], 'L0_attn_a_W_r': _L0_attn_a_in['W_r'], 'L0_attn_a_W_w': _L0_attn_a_in['W_w'], 'L0_attn_a_W_k': _L0_attn_a_in['W_k'], 'L0_attn_a_W_v': _L0_attn_a_in['W_v'], 'L0_attn_a_W_a': _L0_attn_a_in['W_a'], 'L0_attn_a_W_b': _L0_attn_a_in['W_b'], 'L0_attn_a_W_g': _L0_attn_a_in['W_g'], 'L0_attn_a_W_o': _L0_attn_a_in['W_o'], 'L0_attn_a_b_o': _L0_attn_a_in['b_o'], 'L0_attn_a_gn_w': _L0_attn_a_in['gn_w'], 'L0_attn_a_gn_b': _L0_attn_a_in['gn_b'], 'L0_attn_b_gamma1': _L0_attn_b_in['gamma1'], 'L0_attn_b_beta1': _L0_attn_b_in['beta1'], 'L0_attn_b_wq': _L0_attn_b_in['wq'], 'L0_attn_b_wk': _L0_attn_b_in['wk'], 'L0_attn_b_wv': _L0_attn_b_in['wv'], 'L0_attn_b_wo': _L0_attn_b_in['wo'], 'L0_attn_b_w1': _L0_attn_b_in['w1'], 'L0_attn_b_b1': _L0_attn_b_in['b1'], 'L0_attn_b_w2': _L0_attn_b_in['w2'], 'L0_attn_b_b2': _L0_attn_b_in['b2'], 'L0_ffn_W_router': _L0_ffn_in['W_router'], 'L0_ffn_W1': _L0_ffn_in['W1'], 'L0_ffn_b1': _L0_ffn_in['b1'], 'L0_ffn_Wo': _L0_ffn_in['Wo'], 'L0_ffn_bo': _L0_ffn_in['bo'], 'L0_ffn_ln_gamma': _L0_ffn_in['ln_gamma'], 'L0_ffn_ln_beta': _L0_ffn_in['ln_beta'], 'L1_attn_a_Wq': _L1_attn_a_in['Wq'], 'L1_attn_a_bq': _L1_attn_a_in['bq'], 'L1_attn_a_Wk': _L1_attn_a_in['Wk'], 'L1_attn_a_bk': _L1_attn_a_in['bk'], 'L1_attn_a_Wv': _L1_attn_a_in['Wv'], 'L1_attn_a_bv': _L1_attn_a_in['bv'], 'L1_attn_a_Wo': _L1_attn_a_in['Wo'], 'L1_attn_a_bo': _L1_attn_a_in['bo'], 'L1_attn_b_in_proj_w': _L1_attn_b_in['in_proj_w'], 'L1_attn_b_conv_k': _L1_attn_b_in['conv_k'], 'L1_attn_b_conv_b': _L1_attn_b_in['conv_b'], 'L1_attn_b_theta': _L1_attn_b_in['theta'], 'L1_attn_b_decay_slopes': _L1_attn_b_in['decay_slopes'], 'L1_attn_b_anchor_slopes': _L1_attn_b_in['anchor_slopes'], 'L1_attn_b_score_scale': _L1_attn_b_in['score_scale'], 'L1_attn_b_deriv_logits': _L1_attn_b_in['deriv_logits'], 'L1_attn_b_W_re': _L1_attn_b_in['W_re'], 'L1_attn_b_W_im': _L1_attn_b_in['W_im'], 'L1_attn_b_norm_scale': _L1_attn_b_in['norm_scale'], 'L1_attn_b_out_proj_w': _L1_attn_b_in['out_proj_w'], 'L1_ffn_Wq': _L1_ffn_in['Wq'], 'L1_ffn_Wkv': _L1_ffn_in['Wkv'], 'L1_ffn_Ws': _L1_ffn_in['Ws'], 'L1_ffn_Wd': _L1_ffn_in['Wd'], 'L1_ffn_Wo': _L1_ffn_in['Wo']}
    _x0 = _d['L0_attn_a_x']
    _d['L0_attn_a_x'] = jax.random.normal(jax.random.fold_in(jax.random.key(seed), 1), (2, 1024, 128), dtype=_x0.dtype)
    del _x0
    return _d

def reference(L0_attn_a_x, L0_attn_a_x_r, L0_attn_a_x_w, L0_attn_a_x_k, L0_attn_a_x_v, L0_attn_a_x_a, L0_attn_a_x_b, L0_attn_a_x_g, L0_attn_a_W_r, L0_attn_a_W_w, L0_attn_a_W_k, L0_attn_a_W_v, L0_attn_a_W_a, L0_attn_a_W_b, L0_attn_a_W_g, L0_attn_a_W_o, L0_attn_a_b_o, L0_attn_a_gn_w, L0_attn_a_gn_b, L0_attn_b_gamma1, L0_attn_b_beta1, L0_attn_b_wq, L0_attn_b_wk, L0_attn_b_wv, L0_attn_b_wo, L0_attn_b_w1, L0_attn_b_b1, L0_attn_b_w2, L0_attn_b_b2, L0_ffn_W_router, L0_ffn_W1, L0_ffn_b1, L0_ffn_Wo, L0_ffn_bo, L0_ffn_ln_gamma, L0_ffn_ln_beta, L1_attn_a_Wq, L1_attn_a_bq, L1_attn_a_Wk, L1_attn_a_bk, L1_attn_a_Wv, L1_attn_a_bv, L1_attn_a_Wo, L1_attn_a_bo, L1_attn_b_in_proj_w, L1_attn_b_conv_k, L1_attn_b_conv_b, L1_attn_b_theta, L1_attn_b_decay_slopes, L1_attn_b_anchor_slopes, L1_attn_b_score_scale, L1_attn_b_deriv_logits, L1_attn_b_W_re, L1_attn_b_W_im, L1_attn_b_norm_scale, L1_attn_b_out_proj_w, L1_ffn_Wq, L1_ffn_Wkv, L1_ffn_Ws, L1_ffn_Wd, L1_ffn_Wo):

    def _L0_attn_a_ref(x, x_r, x_w, x_k, x_v, x_a, x_b, x_g, W_r, W_w, W_k, W_v, W_a, W_b, W_g, W_o, b_o, gn_w, gn_b):
        import jax, jax.numpy as jnp
        import numpy as np
        D_MODEL = 128
        NHEAD = 16
        HEAD_DIM = D_MODEL // NHEAD
        GN_EPS = 0.00064
        NORM_EPS = 1e-06
        B, T = (4, 128)

        def _xavier(key, shape):
            lim = float(np.sqrt(6.0 / (shape[0] + shape[1])))
            return jax.random.uniform(key, shape, jnp.float32, -lim, lim)

        def _l2norm(t):
            n = jnp.linalg.norm(t, axis=-1, keepdims=True)
            return t / jnp.maximum(n, NORM_EPS)
        Bs, Ts, D = x.shape
        H, K = (NHEAD, HEAD_DIM)
        prev = jnp.concatenate([jnp.zeros_like(x[:, :1]), x[:, :-1]], axis=1)
        xx = prev - x

        def proj(mix, W):
            return jnp.einsum('btd,ed->bte', x + xx * mix, W)
        heads = lambda t: t.reshape(Bs, Ts, H, K)
        r = heads(proj(x_r, W_r))
        w = -jax.nn.softplus(heads(proj(x_w, W_w)))
        k = jnp.tanh(heads(proj(x_k, W_k)))
        v = heads(proj(x_v, W_v))
        a = _l2norm(heads(proj(x_a, W_a)))
        b = _l2norm(heads(proj(x_b, W_b)))
        g = jax.nn.sigmoid(proj(x_g, W_g))

        def step(S, ins):
            r_t, w_t, k_t, v_t, a_t, b_t = ins
            Sa = jnp.einsum('bhvk,bhk->bhv', S, a_t)
            S = S * jnp.exp(w_t)[:, :, None, :] + Sa[..., None] * b_t[:, :, None, :] + v_t[..., None] * k_t[:, :, None, :]
            o = jnp.einsum('bhvk,bhk->bhv', S, r_t)
            return (S, o)
        tm = lambda t: jnp.moveaxis(t, 1, 0)
        S0 = jnp.zeros((Bs, H, K, K), jnp.float32)
        _, o = jax.lax.scan(step, S0, (tm(r), tm(w), tm(k), tm(v), tm(a), tm(b)))
        mixed = jnp.moveaxis(o, 0, 1).reshape(Bs, Ts, D)
        gm = mixed.reshape(Bs * Ts, H, K)
        mu = gm.mean(-1, keepdims=True)
        var = gm.var(-1, keepdims=True)
        normed = ((gm - mu) * jax.lax.rsqrt(var + GN_EPS)).reshape(Bs * Ts, D)
        normed = (normed * gn_w + gn_b).reshape(Bs, Ts, D)
        return jnp.einsum('btd,ed->bte', normed * g, W_o) + b_o

    def _L0_attn_b_ref(x, gamma1, beta1, wq, wk, wv, wo, w1, b1, w2, b2):
        import jax, jax.numpy as jnp
        import numpy as np
        EPS_LN = 1e-06
        STAB = 0.001

        def layer_norm(x, gamma, beta):
            mu = jnp.mean(x, axis=-1, keepdims=True)
            var = jnp.mean(jnp.square(x - mu), axis=-1, keepdims=True)
            return (x - mu) * jax.lax.rsqrt(var + EPS_LN) * gamma + beta
        ln1 = layer_norm(x, gamma1, beta1)
        q = jnp.einsum('ble,ehd->blhd', ln1, wq)
        k = jnp.einsum('ble,ehd->blhd', ln1, wk)
        v = jnp.einsum('ble,ehd->blhd', ln1, wv)
        qp = jax.nn.relu(q) + STAB
        kp = jax.nn.relu(k) + STAB
        kvs = jnp.einsum('blhm,blhd->bhmd', kp, v)
        num = jnp.einsum('blhm,bhmd->blhd', qp, kvs)
        ksum = jnp.sum(kp, axis=1)
        den = jnp.einsum('blhm,bhm->blh', qp, ksum)
        att = num / den[..., None]
        attn_out = jnp.einsum('blhd,hde->ble', att, wo)
        add1 = attn_out + x
        ln2 = layer_norm(add1, gamma1, beta1)
        h = jax.nn.gelu(jnp.einsum('ble,ef->blf', ln2, w1) + b1, approximate=False)
        out2 = jax.nn.gelu(jnp.einsum('blf,fe->ble', h, w2) + b2, approximate=False)
        return out2 + add1

    def _L0_ffn_ref(hidden_states, W_router, W1, b1, Wo, bo, ln_gamma, ln_beta):
        import jax, jax.numpy as jnp
        import numpy as np
        H = 128
        I = 512
        E = 4
        LN_EPS = 1e-12

        def _layer_norm(x, gamma, beta, eps=LN_EPS):
            mu = jnp.mean(x, axis=-1, keepdims=True)
            var = jnp.mean(jnp.square(x - mu), axis=-1, keepdims=True)
            return (x - mu) * jax.lax.rsqrt(var + eps) * gamma + beta
        B, S, _ = hidden_states.shape
        x = hidden_states.reshape(-1, H)
        logits = x @ W_router
        expert_idx = jnp.argmax(logits, axis=-1)
        h = jnp.einsum('th,ehi->tei', x, W1) + b1
        h = jax.nn.gelu(h, approximate=False)
        onehot = jax.nn.one_hot(expert_idx, E, dtype=x.dtype)
        intermediate = jnp.einsum('te,tei->ti', onehot, h)
        y = intermediate @ Wo + bo + x
        y = _layer_norm(y, ln_gamma, ln_beta)
        return y.reshape(B, S, H)

    def _L1_attn_a_ref(input_embeds, Wq, bq, Wk, bk, Wv, bv, Wo, bo):
        import math
        import jax, jax.numpy as jnp
        import numpy as np
        NUM_HEADS = 16
        HEAD_SIZE = 64
        HIDDEN = 128
        ROPE_BASE = 10000.0

        def _rope_cos_sin(seq_len, dim, dtype):
            inv_freq = 1.0 / ROPE_BASE ** (jnp.arange(0, dim, 2, dtype=jnp.float32) / dim)
            t = jnp.arange(seq_len, dtype=jnp.float32)
            freqs = jnp.einsum('s,d->sd', t, inv_freq)
            emb = jnp.concatenate([freqs, freqs], axis=-1)
            return (jnp.cos(emb).astype(dtype), jnp.sin(emb).astype(dtype))

        def _rotate_half(x):
            half = x.shape[-1] // 2
            return jnp.concatenate([-x[..., half:], x[..., :half]], axis=-1)

        def _apply_rope(q, k):
            cos, sin = _rope_cos_sin(q.shape[-2], q.shape[-1], q.dtype)
            q = q * cos + _rotate_half(q) * sin
            k = k * cos + _rotate_half(k) * sin
            return (q, k)
        B, S, _ = input_embeds.shape
        q = input_embeds @ Wq.T + bq
        k = input_embeds @ Wk.T + bk
        v = input_embeds @ Wv.T + bv

        def split_heads(x):
            return x.reshape(B, S, NUM_HEADS, HEAD_SIZE).transpose(0, 2, 1, 3)
        q, k, v = (split_heads(q), split_heads(k), split_heads(v))
        q, k = _apply_rope(q, k)
        scale = 1.0 / math.sqrt(HEAD_SIZE)
        scores = jnp.einsum('bhqd,bhkd->bhqk', q, k) * scale
        attn = jax.nn.softmax(scores, axis=-1)
        out = jnp.einsum('bhqk,bhkd->bhqd', attn, v)
        out = out.transpose(0, 2, 1, 3).reshape(B, S, NUM_HEADS * HEAD_SIZE)
        return out @ Wo.T + bo

    def _L1_attn_b_ref(x, in_proj_w, conv_k, conv_b, theta, decay_slopes, anchor_slopes, score_scale, deriv_logits, W_re, W_im, norm_scale, out_proj_w):
        import jax, jax.numpy as jnp
        import numpy as np
        B, L, D = (2, 512, 128)
        EXPAND = 2
        D_INNER = D * EXPAND
        K, M = (32, 1)
        H = D_INNER // K
        KS = 4
        NA = 4
        ND = K - NA
        C = 2 * D_INNER + K
        SD = H * M
        b, l, _ = x.shape
        z = x @ in_proj_w
        zp = jnp.pad(z, ((0, 0), (KS - 1, 0), (0, 0)))
        z = jax.lax.conv_general_dilated(zp, conv_k, (1,), 'VALID', dimension_numbers=('NWC', 'WIO', 'NWC'), feature_group_count=C) + conv_b
        x_val = z[..., :D_INNER].reshape(b, l, K, H)
        x_gate = jax.nn.silu(z[..., D_INNER:2 * D_INNER])
        s_raw = z[..., -K:].reshape(b, l, K, 1)
        pos = jnp.arange(l, dtype=jnp.float32)
        slopes_d = jax.nn.softplus(decay_slopes).reshape(1, 1, -1, 1)
        dist = jnp.maximum(jnp.float32(l - 1) - pos, 0.0)
        w_d = jnp.exp(-slopes_d * dist[None, :, None, None])
        slopes_a = jax.nn.softplus(anchor_slopes).reshape(1, 1, -1, 1)
        w_a = jnp.exp(-slopes_a * pos[None, :, None, None])
        time_weight = jnp.concatenate([w_d, w_a], axis=2)
        p = jnp.exp(jnp.clip(score_scale[None, None, :, None] * s_raw, -20.0, 20.0))
        p_w = (p * time_weight).reshape(b, l, K, 1, 1)
        xv = x_val[..., None]
        phi = xv * theta
        cos_b, sin_b = (jnp.cos(phi), jnp.sin(phi))
        w = jax.nn.softmax(deriv_logits)
        poly = w[0] + w[1] * xv - w[2] * jnp.square(xv)
        re_m, im_m = (poly * cos_b, poly * sin_b)
        den = jnp.cumsum(p_w, axis=1)
        num_re = jnp.cumsum(p_w * re_m, axis=1)
        num_im = jnp.cumsum(p_w * im_m, axis=1)
        inv_den = 1.0 / jnp.maximum(den, 0.0001)
        re_flat = (num_re * inv_den).reshape(b, l, K, SD)
        im_flat = (num_im * inv_den).reshape(b, l, K, SD)
        mean_sq = (jnp.sum(jnp.square(re_flat), -1) + jnp.sum(jnp.square(im_flat), -1)) / (2 * SD)
        rs = jax.lax.rsqrt(mean_sq[..., None] + 1e-05)
        y = (jnp.dot(re_flat * rs * norm_scale[:SD], W_re) + jnp.dot(im_flat * rs * norm_scale[SD:], W_im)).reshape(b, l, D_INNER)
        return y * x_gate @ out_proj_w

    def _L1_ffn_ref(x, Wq, Wkv, Ws, Wd, Wo):
        import jax, jax.numpy as jnp
        import numpy as np
        B, T, DIM = (4, 128, 128)
        H, E, DH, K = (8, 5, 64, 3)

        def _topk_mask(s, k):
            idx = jax.lax.top_k(s, k)[1]
            return jnp.sum(jax.nn.one_hot(idx, s.shape[-1], dtype=s.dtype), axis=-2)
        b, t, _ = x.shape
        scale = DH ** (-0.5)
        ss = jax.nn.sigmoid(x @ Ws).reshape(b, t, H, E)
        sd = jax.nn.sigmoid(x @ Wd).reshape(b, t, H, E)
        ms = _topk_mask(ss, K)
        md = _topk_mask(sd, K)
        ss_g = ss * ms
        sd_g = sd * md
        q5 = (x @ Wq).reshape(b, t, H, E, DH)
        kv = (x @ Wkv).reshape(b, t, 2, H, E, DH)
        k5, v5 = (kv[:, :, 0], kv[:, :, 1])
        q = jnp.einsum('bthed,bthe->bhtd', q5, sd_g)
        k = jnp.einsum('bthed,bthe->bhtd', k5, ss_g)
        v = jnp.einsum('bthed,bthe->bhtd', v5, ss_g)
        attn = jax.nn.softmax(jnp.einsum('bhid,bhjd->bhij', q * scale, k), axis=-1)
        out = jnp.einsum('bhij,bhjd->bihd', attn, v)
        o5 = jnp.einsum('bthd,dm->bthm', out, Wo).reshape(b, t, H, E, DIM)
        return jnp.einsum('bthem,bthe->btm', o5, md)
    x = L0_attn_a_x
    x = x + _L0_attn_a_ref(_layernorm(x, axis=-1), L0_attn_a_x_r, L0_attn_a_x_w, L0_attn_a_x_k, L0_attn_a_x_v, L0_attn_a_x_a, L0_attn_a_x_b, L0_attn_a_x_g, L0_attn_a_W_r, L0_attn_a_W_w, L0_attn_a_W_k, L0_attn_a_W_v, L0_attn_a_W_a, L0_attn_a_W_b, L0_attn_a_W_g, L0_attn_a_W_o, L0_attn_a_b_o, L0_attn_a_gn_w, L0_attn_a_gn_b)
    x = x + _L0_ffn_ref(_layernorm(x, axis=-1), L0_ffn_W_router, L0_ffn_W1, L0_ffn_b1, L0_ffn_Wo, L0_ffn_bo, L0_ffn_ln_gamma, L0_ffn_ln_beta)
    x = x + _L0_attn_b_ref(_layernorm(x, axis=-1), L0_attn_b_gamma1, L0_attn_b_beta1, L0_attn_b_wq, L0_attn_b_wk, L0_attn_b_wv, L0_attn_b_wo, L0_attn_b_w1, L0_attn_b_b1, L0_attn_b_w2, L0_attn_b_b2)
    x = x + _L0_ffn_ref(_layernorm(x, axis=-1), L0_ffn_W_router, L0_ffn_W1, L0_ffn_b1, L0_ffn_Wo, L0_ffn_bo, L0_ffn_ln_gamma, L0_ffn_ln_beta)
    x = x + _L1_attn_a_ref(_layernorm(x, axis=-1), L1_attn_a_Wq, L1_attn_a_bq, L1_attn_a_Wk, L1_attn_a_bk, L1_attn_a_Wv, L1_attn_a_bv, L1_attn_a_Wo, L1_attn_a_bo)
    x = x + _L1_ffn_ref(_layernorm(x, axis=-1), L1_ffn_Wq, L1_ffn_Wkv, L1_ffn_Ws, L1_ffn_Wd, L1_ffn_Wo)
    x = x + _L1_attn_b_ref(_layernorm(x, axis=-1), L1_attn_b_in_proj_w, L1_attn_b_conv_k, L1_attn_b_conv_b, L1_attn_b_theta, L1_attn_b_decay_slopes, L1_attn_b_anchor_slopes, L1_attn_b_score_scale, L1_attn_b_deriv_logits, L1_attn_b_W_re, L1_attn_b_W_im, L1_attn_b_norm_scale, L1_attn_b_out_proj_w)
    x = x + _L1_ffn_ref(_layernorm(x, axis=-1), L1_ffn_Wq, L1_ffn_Wkv, L1_ffn_Ws, L1_ffn_Wd, L1_ffn_Wo)
    return x

_drawn_inputs = setup_inputs


def setup_inputs(seed=0):
    import zlib

    import numpy as np

    out = dict(_drawn_inputs(seed))
    spreads = {'L0_attn_a_b_o': (0.0, 0.1),
     'L0_attn_a_gn_w': (1.0, 0.6),
     'L0_attn_a_gn_b': (0.0, 0.8),
     'L0_attn_b_gamma1': (1.0, 0.2),
     'L0_attn_b_beta1': (0.0, 0.1),
     'L0_attn_b_b1': (0.0, 0.528),
     'L0_attn_b_b2': (0.0, 0.342),
     'L0_ffn_ln_gamma': (1.0, 0.2),
     'L0_ffn_ln_beta': (0.0, 0.1),
     'L1_attn_a_bq': (0.0, 0.8),
     'L1_attn_a_bk': (0.0, 0.8),
     'L1_attn_a_bv': (0.0, 0.1),
     'L1_attn_a_bo': (0.0, 0.302),
     'L1_attn_b_conv_b': (0.0, 0.368),
     'L1_attn_b_score_scale': (1.0, 0.6),
     'L1_attn_b_norm_scale': (1.0, 0.6)}
    factors = {'L0_attn_a_x_r': 2.732,
     'L0_attn_a_x_w': 6.286,
     'L0_attn_a_x_a': 3.125,
     'L0_attn_a_x_b': 3.039,
     'L0_attn_a_x_g': 8.0,
     'L0_attn_a_W_w': 3.137,
     'L0_attn_a_W_g': 2.826,
     'L0_ffn_b1': 8.0,
     'L0_ffn_bo': 3.124,
     'L1_attn_a_Wq': 8.0,
     'L1_attn_a_Wk': 8.0,
     'L1_attn_b_theta': 3.781,
     'L1_attn_b_anchor_slopes': 64.0,
     'L1_attn_b_W_im': 3.288,
     'L1_ffn_Wq': 8.0,
     'L1_ffn_Wkv': 5.692,
     'L1_ffn_Ws': 8.0,
     'L1_ffn_Wd': 8.0,
     'L1_ffn_Wo': 6.063}
    for name, (base, spread) in spreads.items():
        noise = np.random.default_rng([zlib.crc32(name.encode()), seed]).standard_normal(out[name].shape)
        drawn = base * np.exp(spread * noise) if base else spread * noise
        out[name] = jnp.asarray(drawn.astype(out[name].dtype))
    for name, factor in factors.items():
        out[name] = (out[name] * factor).astype(out[name].dtype)
    return out
```

```python
from contextlib import ExitStack, contextmanager

import concourse.bass as bass
import numpy as np
from concourse import mybir

F32 = mybir.dt.float32
BF16 = mybir.dt.bfloat16
ALU = mybir.AluOpType
ACT = mybir.ActivationFunctionType
AX = mybir.AxisListType

P = 128
BATCH = 2
SEQ = 1024
TOKENS = BATCH * SEQ
TILES = TOKENS // P
CHUNK = 512
CHUNKS = TOKENS // CHUNK


class Chain:

    def __init__(self, eng, sem):
        self.eng, self.sem, self.n, self.at = eng, sem, 0, 0

    def __call__(self, ins):
        self.n += 1
        ins.then_inc(self.sem, 1)
        self.eng.wait_ge(self.sem, self.at + self.n)

    @contextmanager
    def loop(self, rounds, steps):
        before = self.n
        with self.eng.Fori(0, rounds) as i:
            self.at = i * steps
            yield i
        assert self.n == before + steps, (self.n - before, steps)
        self.n = before + rounds * steps
        self.at = 0


class Core:

    def __init__(self, nc, dram, ctx):
        self.nc, self.dram = nc, dram
        self.in_use = []
        sb = lambda name, shape, dt=F32: ctx.enter_context(nc.sbuf_tensor(name, shape, dt))
        self.x = sb("residual", [P, TILES, P])
        self.xn = sb("normed", [P, TILES, P])
        self.xt = sb("normed_t", [P, TOKENS])
        self.ident = sb("identity", [P, P])
        self.banks = ctx.enter_context(nc.psum_tensor("banks", [P, 8, CHUNK], F32))
        self.ps = [self.banks[:, i, :] for i in range(8)]

    def semaphore(self, ctx, name):
        handle = ctx.enter_context(self.nc.semaphore(name))
        self.in_use.append(handle)
        return handle

    def block(self, ctx):
        ctx.callback(self.clear)
        return ctx.enter_context(self.nc.Block())

    def clear(self):
        for handle in self.in_use:
            self.nc.gpsimd.sem_clear(handle)
        self.in_use = []
        self.nc.all_engine_barrier()

    def row(self, ap, tiles=TILES):
        return ap.unsqueeze(1).to_broadcast([P, tiles, ap.shape[-1]])

    def col(self, ap, n=P):
        return ap.unsqueeze(2).to_broadcast([P, ap.shape[1], n])


def dve_norm(core, step, src, dst, square, stat, eps, var_ready, rstd_ready, turn):
    v = core.nc.vector
    step(v.tensor_reduce(stat[:, 0], src[:], AX.X, ALU.add))
    step(v.tensor_scalar(stat[:, 0], stat[:, 0], 1.0 / P, None, ALU.mult))
    step(v.tensor_tensor(dst[:], src[:], core.col(stat[:, 0]), ALU.subtract))
    step(v.tensor_tensor(square[:], dst[:], dst[:], ALU.mult))
    step(v.tensor_reduce(stat[:, 1], square[:], AX.X, ALU.add))
    step(v.tensor_scalar(stat[:, 1], stat[:, 1], 1.0 / P, eps, ALU.mult, ALU.add))
    v.reciprocal(stat[:, 2], stat[:, 1]).then_inc(var_ready, 1)
    step.eng.wait_ge(rstd_ready, turn)
    return v.tensor_tensor(dst[:], dst[:], core.col(stat[:, 3]), ALU.mult)


def act_rstd(core, act, stat, var_ready, rstd_ready, turn):
    act.wait_ge(var_ready, turn)
    core.nc.scalar.activation(stat[:, 3], stat[:, 2], ACT.Sqrt).then_inc(rstd_ready, 1)


def pe_transpose_tiles(core, pe, src, ready, full, empty):
    pe.wait_ge(*ready)
    for g in range(CHUNKS):
        if g >= 2:
            pe.wait_ge(empty[0], empty[1] + g - 1)
        for t in range(4):
            ins = core.nc.tensor.transpose(core.ps[g % 2][:, t * P:(t + 1) * P], src[:, 4 * g + t, :],
                                           core.ident[:])
        ins.then_inc(full, 1)


def act_copy_transposed(core, act, dst, full, empty, turn=0):
    for g in range(CHUNKS):
        act.wait_ge(full, turn + g + 1)
        core.nc.scalar.copy(dst[:, g * CHUNK:(g + 1) * CHUNK], core.ps[g % 2][:]).then_inc(empty, 1)


def load_stage(core):
    nc = core.nc
    with ExitStack() as ctx:
        loaded = core.semaphore(ctx, "residual_in")
        block = core.block(ctx)

        @block.sync
        def _(sp):
            sp.dma_start(core.x[:], core.dram["x"].rearrange("b (t p) c -> p (b t) c", p=P)).then_inc(loaded, 16)
            sp.dma_start(core.ident[:], core.dram["identity"]).then_inc(loaded, 16)
            sp.wait_ge(loaded, 32)


def store_stage(core):
    nc = core.nc
    with nc.semaphore("result_out") as stored, nc.Block() as block:
        @block.sync
        def _(sp):
            sp.dma_start(core.dram["out"].rearrange("b (t p) c -> p (b t) c", p=P), core.x[:]).then_inc(stored, 16)
            sp.wait_ge(stored, 16)


def rwkv_stage(core):
    nc, d = core.nc, core.dram
    H, K = 16, 8
    STEPS = 64
    PER = SEQ // STEPS
    COLS = BATCH * PER
    ROWS = 2 * K
    BLOCK = 8
    PAD = STEPS + BLOCK
    SCAN = ("w", "k", "v", "a", "b", "r")
    ORDER = ("r", "w", "k", "v", "a", "b", "g")
    tag = "rw_"
    with ExitStack() as ctx:
        sb = lambda name, shape, dt=F32: ctx.enter_context(nc.sbuf_tensor(tag + name, shape, dt))
        sem = lambda name: core.semaphore(ctx, tag + name)
        weights = sb("weights", [P, 8, P])
        mix = sb("mix", [P, 7])
        bo, gn = sb("bo", [P, P]), sb("gn", [P, 2])
        head = sb("head", [P, H])
        same = sb("same", [P, P])
        pick = sb("pick", [P, K, P])
        give = sb("give", [P, K, P])
        pool2 = sb("pool2", [P, 2, 2 * H])
        spread2 = sb("spread2", [P, 2, P])
        eye = sb("eye", [P, K])
        seq = {n: sb(n, [P, COLS, PAD]) for n in SCAN}
        g_t = sb("g_t", [P, TOKENS])
        state = sb("state", [P, 2, COLS, ROWS])
        yr = sb("yr", [P, 2, BLOCK, COLS, ROWS])
        kv = sb("kv", [P, 2, K, COLS * BLOCK])
        ya, ub, x1 = sb("ya", [P, 2, PER, ROWS]), sb("ub", [P, 2, PER, ROWS]), sb("x1", [P, 2, PER, ROWS])
        o, yc = sb("o", [P, COLS, PAD]), sb("yc", [P, COLS, PAD])
        borders = sb("borders", [P, COLS, K])
        stat = sb("stat", [P, 4, TILES])
        inv = sb("inv", [P, CHUNK])
        flat_yr = yr[:].rearrange("p i s c r -> p (i s c r)")
        square = flat_yr[:, 0:2048].rearrange("p (t c) -> p t c", c=P)
        diff, mixed = flat_yr[:, 2048:4096], [flat_yr[:, 4096:6144], flat_yr[:, 6144:8192]]
        wide = flat_yr[:, 0:4096].rearrange("p (n c) -> p n c", c=P)
        tight = flat_yr[:, 4096:8192].rearrange("p (n c) -> p n c", c=P)

        loads = sem("loads")
        var_ready, rstd_ready, normed = sem("var_ready"), sem("rstd_ready"), sem("normed")
        xt_full, xt_copied = sem("xt_full"), sem("xt_copied")
        mixed_ready, proj_full, proj_ready = sem("mixed_ready"), sem("proj_full"), sem("proj_ready")
        sq_ready, sq_full, len_ready, inv_ready, inv_full, unit_ready = (sem(n) for n in (
            "sq_ready", "sq_full", "len_ready", "inv_ready", "inv_full", "unit_ready"))
        y_ready, u_full, x1_ready, x_ready = sem("y_ready"), sem("u_full"), sem("x1_ready"), sem("x_ready")
        yr_ready, v_full, kv_ready, o_full, o_copied = (sem(n) for n in ("yr_ready", "v_full", "kv_ready", "o_full", "o_copied"))
        wide_ready, wide_full, wide_copied, border_full, border_ready = (sem(n) for n in (
            "wide_ready", "wide_full", "wide_copied", "border_full", "border_ready"))
        fix_ready, fix_full = sem("fix_ready"), sem("fix_full")
        gn_in, gn_full = sem("gn_in"), sem("gn_full")
        res_ready, res_full = sem("res_ready"), sem("res_full")
        dve_step, pool_step = sem("dve_step"), sem("pool_step")
        LOADS = 13
        banks0 = core.banks[:, 0:4, :].rearrange("p k n -> p (k n)")
        banks4 = core.banks[:, 4:8, :].rearrange("p k n -> p (k n)")
        cols = lambda t, off: t[:, :, off:off + STEPS]
        block = core.block(ctx)

        @block.sync
        def _(sp):
            pairs = ((weights[:], d["rw_w"].rearrange("k c n -> c k n")), (mix[:], d["rw_mix"]), (bo[:], d["rw_bo"].partition_broadcast(P)),
                     (gn[:], d["rw_gn"]), (head[:], d["head_mask"]), (same[:], d["rw_same"]), (pick[:], d["rw_pick"]),
                     (give[:], d["rw_give"]), (pool2[:], d["rw_pool2"]), (spread2[:], d["rw_spread2"]), (eye[:], d["rw_eye"]))
            for dst, src in pairs:
                sp.dma_start(dst, src).then_inc(loads, 16)

        @block.tensor
        def _(pe):
            mm = nc.tensor.matmul
            pe_transpose_tiles(core, pe, core.xn, (normed, 1), xt_full, (xt_copied, 0))
            pe.wait_ge(loads, 11 * 16)
            pe.wait_ge(xt_copied, CHUNKS)
            for i in range(7):
                pe.wait_ge(mixed_ready, i + 1)
                for c in range(CHUNKS):
                    if i >= 2:
                        pe.wait_ge(proj_ready, (i - 2) * CHUNKS + c + 1)
                    mm(core.ps[4 * (i % 2) + c], weights[:, i, :], mixed[i % 2][:, c * CHUNK:(c + 1) * CHUNK], start=True,
                       stop=True).then_inc(proj_full, 1)
            pe.wait_ge(proj_ready, 7 * CHUNKS)
            for i, n in enumerate("ab"):
                pe.wait_ge(sq_ready, i + 1)
                for c in range(CHUNKS):
                    ins = mm(core.ps[0][32 * c:32 * c + 32, :], pool2[:, i, :], mixed[i][:, c * CHUNK:(c + 1) * CHUNK],
                             start=(i == 0), stop=(i == 1), tile_position=(0, 32 * c), skip_group_check=True)
            ins.then_inc(sq_full, 1)
            pe.wait_ge(inv_ready, 1)
            for i in range(2):
                if i:
                    pe.wait_ge(unit_ready, 1)
                for c in range(CHUNKS):
                    ins = mm(core.ps[4 + c], spread2[32 * c:32 * c + 32, i, :], inv[32 * c:32 * c + 32, :], start=True, stop=True)
                ins.then_inc(inv_full, 1)
            pe.wait_ge(unit_ready, 2)

            def spread_v(q, s):
                r = s // 2
                ins = mm(core.ps[2 + r % 2][:, (s % 2) * 256:(s % 2 + 1) * 256], give[:, s, :], seq["v"][:, :, bass.ds(q * BLOCK, BLOCK)],
                         start=True, stop=True)
                if s % 2:
                    ins.then_inc(v_full, 1)

            def output(i, row):
                ins = mm(core.ps[4 + row // K][:, 0:256], pick[:, row % K, :], yr[:, i, :, :, row].rearrange("p s c -> p c s"),
                         start=(row % K == 0), stop=(row % K == K - 1))
                if row % K == K - 1:
                    ins.then_inc(o_full, 1)

            for s in range(K):
                if s in (4, 6):
                    pe.wait_ge(kv_ready, s // 2 - 1)
                spread_v(0, s)
            pe.sem_inc(o_full, 4)
            with pe.Fori(0, STEPS // BLOCK // 2) as qq:
                for i in range(2):
                    q = qq * 2 + i
                    todo = list(range(ROWS))
                    for s in range(BLOCK):
                        n = q * BLOCK + s
                        for b in range(BATCH):
                            pe.wait_ge(y_ready, n * 2 + b + 1)
                            mm(core.ps[b][:, 0:256], same[:], ya[:, b].rearrange("p c r -> p (c r)"), start=True, stop=True).then_inc(u_full, 1)
                            if b == 0:
                                if s % 2 == 0:
                                    pe.wait_ge(kv_ready, q * 4 + s // 2 + 3)
                                spread_v(q + 1, s)
                            elif s:
                                if s == 1:
                                    pe.wait_ge(yr_ready, q * BLOCK + 1)
                                    pe.wait_ge(o_copied, q * 2 + 2)
                                for row in todo[:3 if s <= 2 else 2]:
                                    output(1 - i, row)
                                    todo.remove(row)
            pe.wait_ge(yr_ready, STEPS + 1)
            pe.wait_ge(o_copied, STEPS // BLOCK * 2 + 2)
            for row in range(ROWS):
                output(1, row)
            pe.wait_ge(wide_ready, 1)
            for m in range(COLS // 4):
                if m >= 2:
                    pe.wait_ge(wide_copied, m - 1)
                for t in range(4):
                    ins = nc.tensor.transpose(core.ps[m % 2][:, t * P:(t + 1) * P], wide[:, 4 * m + t, :], core.ident[:])
                ins.then_inc(wide_full, 1)
            pe.wait_ge(wide_copied, COLS // 4)
            for c in range(PER - 1):
                pe.wait_ge(border_ready, c + 1)
                for b in range(BATCH):
                    ins = mm(core.ps[2 + c % 2][:, b * K:(b + 1) * K], tight[:, b * PER + c, :], borders[:, b * PER + c, :],
                             start=True, stop=True)
                ins.then_inc(border_full, 1)
            pe.wait_ge(fix_ready, 1)
            pe.wait_ge(o_copied, STEPS // BLOCK * 2 + 4)
            for c in range(COLS):
                ins = mm(core.ps[4 + c // 8][:, (c % 8) * STEPS:(c % 8 + 1) * STEPS], wide[:, c, :], yc[:, c, BLOCK:BLOCK + STEPS],
                         start=True, stop=True)
            ins.then_inc(fix_full, 1)
            pe.wait_ge(gn_in, 1)
            for c in range(CHUNKS):
                ins = mm(core.ps[c], same[:], mixed[0][:, c * CHUNK:(c + 1) * CHUNK], start=True, stop=True)
            ins.then_inc(gn_full, 1)
            pe.wait_ge(gn_in, 2)
            for c in range(CHUNKS):
                ins = mm(core.ps[0][32 * c:32 * c + 32, :], pool2[:, 0, :], mixed[1][:, c * CHUNK:(c + 1) * CHUNK],
                         start=True, stop=True, tile_position=(0, 32 * c), skip_group_check=True)
            ins.then_inc(gn_full, 1)
            pe.wait_ge(inv_ready, 2)
            for c in range(CHUNKS):
                ins = mm(core.ps[4 + c], spread2[32 * c:32 * c + 32, 0, :], inv[32 * c:32 * c + 32, :], start=True, stop=True)
            ins.then_inc(gn_full, 1)
            pe.wait_ge(res_ready, 1)
            for t in range(TILES):
                ins = mm(core.ps[t // 4][:, (t % 4) * P:(t % 4 + 1) * P], mixed[0][:, t * P:(t + 1) * P], weights[:, 7, :],
                         start=True, stop=True)
            ins.then_inc(res_full, 1)

        @block.scalar
        def _(act):
            act_rstd(core, act, stat, var_ready, rstd_ready, 1)
            act_copy_transposed(core, act, core.xt, xt_full, xt_copied)
            func = {"w": (ACT.Sigmoid, -1.0), "k": (ACT.Tanh, 1.0), "g": (ACT.Sigmoid, 1.0)}
            for i, n in enumerate(ORDER):
                for c in range(CHUNKS):
                    act.wait_ge(proj_full, i * CHUNKS + c + 1)
                    src = core.ps[4 * (i % 2) + c]
                    if n == "g":
                        dst = g_t[:, c * CHUNK:(c + 1) * CHUNK]
                    else:
                        off = 1 if n == "r" else 0
                        dst = seq[n][:, 8 * c:8 * c + 8, off:off + STEPS]
                        src = src.rearrange("p (c s) -> p c s", s=STEPS)
                    f, scale = func.get(n, (ACT.Copy, 1.0))
                    nc.scalar.activation(dst, src, f, scale=scale).then_inc(proj_ready, 1)
            act.wait_ge(sq_full, 1)
            nc.scalar.activation(inv[:], core.ps[0], ACT.Sqrt).then_inc(len_ready, 1)
            act.sem_inc(o_copied, 2)

            def copy_outputs(q):
                for i, dst in enumerate((o, yc)):
                    act.wait_ge(o_full, q * 2 + i + 5)
                    nc.scalar.copy(dst[:, :, bass.ds(q * BLOCK, BLOCK)], core.ps[4 + i][:, 0:256].rearrange("p (c s) -> p c s", s=BLOCK)).then_inc(o_copied, 1)

            with act.Fori(0, STEPS // BLOCK) as q:
                copy_outputs(q)
            copy_outputs(STEPS // BLOCK)
            for m in range(COLS // 4):
                act.wait_ge(wide_full, m + 1)
                nc.scalar.copy(tight[:, 4 * m:4 * m + 4, :], core.ps[m % 2].rearrange("p (t c) -> p t c", c=P)).then_inc(wide_copied, 1)
            act.wait_ge(len_ready, 2)
            nc.scalar.activation(inv[:], inv[:], ACT.Sqrt).then_inc(inv_ready, 1)

        @block.gpsimd
        def _(pool):
            g = nc.gpsimd
            pool.wait_ge(inv_ready, 1)
            step = Chain(pool, pool_step)
            with step.loop(STEPS // BLOCK // 2, 2 * BLOCK * 2) as qq:
                for i in range(2):
                    q = qq * 2 + i
                    pool.wait_ge(kv_ready, q * 4 + 4)
                    for s in range(BLOCK):
                        n = q * BLOCK + s
                        before = state[:, 1 - s % 2]
                        for b in range(BATCH):
                            mine = slice(b * PER, (b + 1) * PER)
                            pool.wait_ge(x_ready, n * 2 + b + 1)
                            step(g.tensor_tensor(x1[:, b], before[:, mine], seq["w"][:, mine, bass.ds(n, 1)].to_broadcast([P, PER, ROWS]), ALU.mult))
                            g.tensor_tensor(x1[:, b, :, 0:K], x1[:, b, :, 0:K],
                                            kv[:, i].rearrange("p v (c s) -> p c v s", s=BLOCK)[:, mine, :, s], ALU.add).then_inc(x1_ready, 1)
                        if s == 1:
                            pool.wait_ge(o_full, q * 2 + 2)
                        j, slot = (i, s - 1) if s else (1 - i, BLOCK - 1)
                        g.tensor_tensor(yr[:, j, slot], before, seq["r"][:, :, bass.ds(n, 1)].to_broadcast([P, COLS, ROWS]),
                                        ALU.mult).then_inc(yr_ready, 1)
            pool.wait_ge(x_ready, STEPS * 2 + 2)
            g.tensor_tensor(yr[:, 1, BLOCK - 1], state[:, 1], seq["r"][:, :, STEPS:STEPS + 1].to_broadcast([P, COLS, ROWS]),
                            ALU.mult).then_inc(yr_ready, 1)

        @block.vector
        def _(dve):
            v = nc.vector
            step = Chain(dve, dve_step)
            step(dve_norm(core, step, core.x, core.xn, square, stat, 1e-5, var_ready, rstd_ready, 1))
            dve.sem_inc(normed, 1)
            dve.wait_ge(xt_copied, CHUNKS)
            dve.wait_ge(loads, 11 * 16)
            x_t = core.xt[:].rearrange("p (b s) -> p b s", b=BATCH)
            df = diff.rearrange("p (b s) -> p b s", b=BATCH)
            step(v.tensor_tensor(df[:, :, 1:SEQ], x_t[:, :, 0:SEQ - 1], x_t[:, :, 1:SEQ], ALU.subtract))
            step(v.tensor_scalar(df[:, :, 0:1], x_t[:, :, 0:1], -1.0, None, ALU.mult))
            for i in range(7):
                if i >= 2:
                    dve.wait_ge(proj_full, (i - 1) * CHUNKS)
                v.scalar_tensor_tensor(out=mixed[i % 2], in0=diff, scalar=mix[:, i:i + 1], in1=core.xt[:], op0=ALU.mult,
                                       op1=ALU.add).then_inc(mixed_ready, 1)
            for n in ("k", "v", "a"):
                step(v.memset(seq[n][:, :, STEPS:PAD], 0.0))
            step(v.memset(seq["r"][:, :, 0:1], 0.0))
            step(v.memset(state[:, 1, :, 0:K], 0.0))
            step(v.tensor_copy(state[:, 1, :, K:ROWS], eye[:].unsqueeze(1).to_broadcast([P, COLS, K])))
            dve.wait_ge(proj_ready, 7 * CHUNKS)
            for i, n in enumerate("ab"):
                step(v.tensor_tensor(mixed[i].rearrange("p (c s) -> p c s", s=STEPS), cols(seq[n], 0), cols(seq[n], 0), ALU.mult))
                dve.sem_inc(sq_ready, 1)
            dve.wait_ge(len_ready, 1)
            step(v.tensor_scalar(inv[:], inv[:], 1e-6, None, ALU.max))
            step(v.reciprocal(inv[:], inv[:]))
            dve.sem_inc(inv_ready, 1)
            for i, n in enumerate("ab"):
                dve.wait_ge(inv_full, i + 1)
                step(v.tensor_tensor(cols(seq[n], 0), cols(seq[n], 0), banks4.rearrange("p (c s) -> p c s", s=STEPS), ALU.mult))
                dve.sem_inc(unit_ready, 1)
            step(v.memset(yr[:, 1], 0.0))

            def key_values(q, r, i):
                v.tensor_tensor(kv[:, i, 2 * r:2 * r + 2].rearrange("p v (c s) -> p v c s", s=BLOCK),
                                core.ps[2 + r % 2].rearrange("p (v c s) -> p v c s", v=2, s=BLOCK),
                                seq["k"][:, :, bass.ds(q * BLOCK, BLOCK)].unsqueeze(1).to_broadcast([P, 2, COLS, BLOCK]),
                                ALU.mult).then_inc(kv_ready, 1)

            def times_a(n, b, src):
                mine = slice(b * PER, (b + 1) * PER)
                v.tensor_tensor(ya[:, b], src[:, mine], seq["a"][:, mine, bass.ds(n, 1)].to_broadcast([P, PER, ROWS]),
                                ALU.mult).then_inc(y_ready, 1)

            for r in range(4):
                dve.wait_ge(v_full, r + 1)
                key_values(0, r, 0)
            for b in range(BATCH):
                times_a(0, b, state[:, 1])
            dve.sem_inc(x_ready, 2)
            with step.loop(STEPS // BLOCK // 2, 2 * BLOCK * 2) as qq:
                for i in range(2):
                    q = qq * 2 + i
                    for s in range(BLOCK):
                        n = q * BLOCK + s
                        for b in range(BATCH):
                            mine = slice(b * PER, (b + 1) * PER)
                            dve.wait_ge(u_full, n * 2 + b + 1)
                            step(v.tensor_tensor(ub[:, b], core.ps[b][:, 0:256].rearrange("p (c r) -> p c r", r=ROWS),
                                                 seq["b"][:, mine, bass.ds(n, 1)].to_broadcast([P, PER, ROWS]), ALU.mult))
                            dve.wait_ge(x1_ready, n * 2 + b + 1)
                            v.tensor_tensor(state[:, s % 2, mine], ub[:, b], x1[:, b], ALU.add).then_inc(x_ready, 1)
                            dve.wait_ge(x_ready, n * 2 + b + 3)
                            times_a(n + 1, b, state[:, s % 2])
                        if s % 2:
                            dve.wait_ge(v_full, q * 4 + s // 2 + 5)
                            key_values(q + 1, s // 2, 1 - i)
            last = state[:, 1]
            dve.wait_ge(o_full, STEPS // BLOCK * 2 + 6)
            step(v.tensor_tensor(wide.rearrange("p n (h k) -> p n h k", k=K), last[:, :, K:ROWS].unsqueeze(2).to_broadcast([P, COLS, H, K]),
                                 head[:].unsqueeze(1).unsqueeze(3).to_broadcast([P, COLS, H, K]), ALU.mult))
            dve.sem_inc(wide_ready, 1)
            border = borders[:].rearrange("p (b c) k -> p b c k", b=BATCH)
            own = last.rearrange("p (b c) r -> p b c r", b=BATCH)
            step(v.memset(border[:, :, 0], 0.0))
            dve.sem_inc(border_ready, 1)
            for c in range(PER - 1):
                dve.wait_ge(border_full, c + 1)
                v.tensor_tensor(border[:, :, c + 1], core.ps[2 + c % 2][:, 0:BATCH * K].rearrange("p (b k) -> p b k", b=BATCH),
                                own[:, :, c, 0:K], ALU.add).then_inc(border_ready, 1)
            dve.wait_ge(border_ready, PER)
            step(v.tensor_tensor(wide.rearrange("p n (h k) -> p n h k", k=K), borders[:].unsqueeze(2).to_broadcast([P, COLS, H, K]),
                                 head[:].unsqueeze(1).unsqueeze(3).to_broadcast([P, COLS, H, K]), ALU.mult))
            dve.sem_inc(fix_ready, 1)
            dve.wait_ge(fix_full, 1)
            out, dev = mixed
            step(v.tensor_tensor(out.rearrange("p (c s) -> p c s", s=STEPS), cols(o, BLOCK), banks4.rearrange("p (c s) -> p c s", s=STEPS), ALU.add))
            dve.sem_inc(gn_in, 1)
            dve.wait_ge(gn_full, 1)
            step(v.scalar_tensor_tensor(out=out, in0=banks0, scalar=-1.0 / K, in1=out, op0=ALU.mult, op1=ALU.add))
            step(v.tensor_tensor(dev, out, out, ALU.mult))
            dve.sem_inc(gn_in, 1)
            dve.wait_ge(gn_full, 2)
            step(v.tensor_scalar(inv[:], core.ps[0], 1.0 / K, 0.00064, ALU.mult, ALU.add))
            step(v.reciprocal(inv[:], inv[:]))
            dve.sem_inc(len_ready, 1)
            dve.wait_ge(gn_full, 3)
            step(v.tensor_tensor(out, out, banks4, ALU.mult))
            step(v.tensor_scalar(out, out, gn[:, 0:1], gn[:, 1:2], ALU.mult, ALU.add))
            step(v.tensor_tensor(out, out, g_t[:], ALU.mult))
            dve.sem_inc(res_ready, 1)
            step(v.tensor_tensor(core.x[:], core.x[:], core.row(bo[:]), ALU.add))
            dve.wait_ge(res_full, 1)
            step(v.tensor_tensor(core.x[:], core.x[:], banks0.rearrange("p (t c) -> p t c", c=P), ALU.add))


def routed_ffn_stage(core, tag):
    nc, d = core.nc, core.dram
    E, I = 4, 512
    IB = I // P
    with ExitStack() as ctx:
        sb = lambda name, shape, dt=F32: ctx.enter_context(nc.sbuf_tensor(tag + name, shape, dt))
        sem = lambda name: core.semaphore(ctx, tag + name)
        w_router = sb("w_router", [P, E])
        w1 = sb("w1", [P, E, I])
        b1 = sb("b1", [E, I])
        wo = sb("wo", [P, IB, P])
        bo, gamma, beta = sb("bo", [P, P]), sb("gamma", [P, P]), sb("beta", [P, P])
        square = sb("square", [P, TILES, P])
        stat = sb("stat", [P, 4, TILES])
        best, left = sb("best", [P, TILES]), sb("left", [P, TILES])
        hot = sb("hot", [P, TILES, E])
        hot_t = sb("hot_t", [E, TOKENS])
        xe = [sb(f"xe{e}", [P, TILES, P]) for e in range(E)]
        xe_t = sb("xe_t", [P, E, TOKENS])
        hidden = sb("hidden", [P, IB, CHUNK])
        y = sb("y", [P, TILES, P])

        loads = sem("loads")
        var_ready, rstd_ready, normed = sem("var_ready"), sem("rstd_ready"), sem("normed")
        xt_full, xt_copied = sem("xt_full"), sem("xt_copied")
        logits_full, hot_ready, hot_full, hot_copied = sem("logits_full"), sem("hot_ready"), sem("hot_full"), sem("hot_copied")
        xe_ready = [sem(f"xe_ready{e}") for e in range(E)]
        h_full, h_free, hidden_free = sem("h_full"), sem("h_free"), sem("hidden_free")
        y_full, y_free = sem("y_full"), sem("y_free")
        dve_step, act_step, pool_step = sem("dve_step"), sem("act_step"), sem("pool_step")
        logits, hot_ps, y_ps = core.ps[2], core.ps[3], core.ps[4]

        block = core.block(ctx)

        @block.sync
        def _(sp):
            for dst, src in ((w_router[:], d["W_router"]), (w1[:], d["W1"].rearrange("e c i -> c e i")), (b1[:], d["b1"]),
                             (wo[:], d["Wo"].rearrange("(j p) c -> p j c", p=P)), (bo[:], d["bo"].partition_broadcast(P)),
                             (gamma[:], d["gamma"].partition_broadcast(P)), (beta[:], d["beta"].partition_broadcast(P))):
                sp.dma_start(dst, src).then_inc(loads, 16)

        @block.tensor
        def _(pe):
            pe_transpose_tiles(core, pe, core.xn, (normed, 1), xt_full, (xt_copied, 0))
            pe.wait_ge(loads, 7 * 16)
            pe.wait_ge(xt_copied, CHUNKS)
            for t in range(TILES):
                ins = nc.tensor.matmul(logits[:, t * E:(t + 1) * E], core.xt[:, t * P:(t + 1) * P], w_router[:],
                                       start=True, stop=True)
            ins.then_inc(logits_full, 1)
            pe.wait_ge(hot_ready, 1)
            for g in range(CHUNKS):
                if g:
                    pe.wait_ge(hot_copied, g)
                for t in range(4):
                    ins = nc.tensor.transpose(hot_ps[0:E, t * P:(t + 1) * P], hot[:, 4 * g + t, :], core.ident[:])
                ins.then_inc(hot_full, 1)
            for e in range(E):
                pe_transpose_tiles(core, pe, xe[e], (xe_ready[e], 1), xt_full, (xt_copied, CHUNKS * (e + 1)))
                pe.wait_ge(xt_copied, CHUNKS * (e + 2))
            with pe.Fori(0, CHUNKS) as c:
                for j in range(IB):
                    pe.wait_ge(h_free, c * IB + j + 1)
                    h = core.ps[j % 2]
                    for e in range(E):
                        nc.tensor.matmul(h[:], w1[:, e, j * P:(j + 1) * P], xe_t[:, e, bass.ds(c * CHUNK, CHUNK)],
                                         start=(e == 0), stop=False)
                    nc.tensor.matmul(h[:], b1[:, j * P:(j + 1) * P], hot_t[:, bass.ds(c * CHUNK, CHUNK)],
                                     start=False, stop=True).then_inc(h_full, 1)
                pe.wait_ge(y_free, c + 1)
                pe.wait_ge(act_step, c * IB + IB)
                for t in range(4):
                    for j in range(IB):
                        ins = nc.tensor.matmul(y_ps[:, t * P:(t + 1) * P], hidden[:, j, t * P:(t + 1) * P], wo[:, j, :],
                                               start=(j == 0), stop=(j == IB - 1))
                ins.then_inc(y_full, 1)

        @block.scalar
        def _(act):
            act_rstd(core, act, stat, var_ready, rstd_ready, 1)
            act_copy_transposed(core, act, core.xt, xt_full, xt_copied)
            for g in range(CHUNKS):
                act.wait_ge(hot_full, g + 1)
                nc.scalar.copy(hot_t[:, g * CHUNK:(g + 1) * CHUNK], hot_ps[0:E, :]).then_inc(hot_copied, 1)
            for e in range(E):
                act_copy_transposed(core, act, xe_t[:, e], xt_full, xt_copied, CHUNKS * (e + 1))
            act.sem_inc(h_free, 2)
            with act.Fori(0, CHUNKS) as c:
                for j in range(IB):
                    act.wait_ge(h_full, c * IB + j + 1)
                    if j == 0:
                        act.wait_ge(hidden_free, c + 1)
                    nc.scalar.activation(hidden[:, j, :], core.ps[j % 2][:], ACT.Gelu).then_inc(act_step, 1)
                    act.wait_ge(act_step, c * IB + j + 1)
                    act.sem_inc(h_free, 1)
            act_rstd(core, act, stat, var_ready, rstd_ready, 2)

        @block.gpsimd
        def _(pool):
            pool.wait_ge(hot_ready, 1)
            for e in (2, 3):
                nc.gpsimd.tensor_tensor(xe[e][:], core.xn[:], core.col(hot[:, :, e]), ALU.mult).then_inc(xe_ready[e], 1)

        @block.vector
        def _(dve):
            v = nc.vector
            step = Chain(dve, dve_step)
            step(dve_norm(core, step, core.x, core.xn, square, stat, 1e-5, var_ready, rstd_ready, 1))
            dve.sem_inc(normed, 1)
            dve.wait_ge(logits_full, 1)
            scores = logits[:, 0:TILES * E].rearrange("p (t e) -> p t e", e=E)
            step(v.tensor_reduce(best[:], scores, AX.X, ALU.max))
            step(v.tensor_tensor(hot[:], scores, core.col(best[:], E), ALU.is_equal))
            step(v.tensor_scalar(left[:], hot[:, :, 0], -1.0, 1.0, ALU.mult, ALU.add))
            for e in range(1, E):
                step(v.tensor_tensor(hot[:, :, e], hot[:, :, e], left[:], ALU.mult))
                step(v.tensor_tensor(left[:], left[:], hot[:, :, e], ALU.subtract))
            dve.sem_inc(hot_ready, 1)
            for e in (0, 1):
                v.tensor_tensor(xe[e][:], core.xn[:], core.col(hot[:, :, e]), ALU.mult).then_inc(xe_ready[e], 1)
            dve.wait_ge(loads, 7 * 16)
            dve.sem_inc(y_free, 1)
            dve.sem_inc(hidden_free, 1)
            with step.loop(CHUNKS, 2) as c:
                dve.wait_ge(y_full, c + 1)
                part = y[:, bass.ds(c * 4, 4), :]
                step(v.tensor_tensor(part, y_ps[:].rearrange("p (t c) -> p t c", c=P), core.xn[:, bass.ds(c * 4, 4), :],
                                     ALU.add))
                dve.sem_inc(y_free, 1)
                dve.sem_inc(hidden_free, 1)
                step(v.tensor_tensor(part, part, core.row(bo[:], 4), ALU.add))
            step(dve_norm(core, step, y, y, square, stat, 1e-12, var_ready, rstd_ready, 2))
            step(v.tensor_tensor(y[:], y[:], core.row(gamma[:]), ALU.mult))
            step(v.tensor_tensor(y[:], y[:], core.row(beta[:]), ALU.add))
            step(v.tensor_tensor(core.x[:], core.x[:], y[:], ALU.add))


def linear_attention_stage(core):
    nc, d = core.nc, core.dram
    H, M, F = 16, 8, 512
    FB = F // P
    STAB = 0.001
    KV = P + H
    tag = "la_"
    with ExitStack() as ctx:
        sb = lambda name, shape, dt=F32: ctx.enter_context(nc.sbuf_tensor(tag + name, shape, dt))
        sem = lambda name: core.semaphore(ctx, tag + name)
        wq, wkv, wo = sb("wq", [P, P]), sb("wkv", [P, 2 * P]), sb("wo", [P, P])
        w1, b1, w2, b2 = sb("w1", [P, F]), sb("b1", [P, FB]), sb("w2", [P, FB, P]), sb("b2", [P, P])
        gamma, beta, head = sb("gamma", [P, P]), sb("beta", [P, P]), sb("head", [P, H])
        square = sb("square", [P, TILES, P])
        stat = sb("stat", [P, 4, TILES])
        ln = sb("ln", [P, TILES, P])
        q_t = sb("q_t", [P, TOKENS])
        k = sb("k", [P, TILES, P])
        v1 = sb("v1", [P, TILES, P + 1])
        kv = sb("kv", [P, BATCH, KV])
        recip = sb("recip", [P, TILES, H])
        att = sb("att", [P, TILES, P])
        add1 = sb("add1", [P, TILES, P])
        hidden = sb("hidden", [P, FB, CHUNK])
        y = sb("y", [P, TILES, P])

        loads = sem("loads")
        var_ready, rstd_ready, ln_ready = sem("var_ready"), sem("rstd_ready"), sem("ln_ready")
        xt_full, xt_copied = sem("xt_full"), sem("xt_copied")
        q_full, q_ready = sem("q_full"), sem("q_ready")
        kv_full, k_ready, v_ready = sem("kv_full"), sem("k_ready"), sem("v_ready")
        sums_full, sums_ready = sem("sums_full"), sem("sums_ready")
        att_full, att_ready = sem("att_full"), sem("att_ready")
        out_full, add_ready = sem("out_full"), sem("add_ready")
        h_full, h_ready = sem("h_full"), sem("h_ready")
        y_full, y_ready, y_read = sem("y_full"), sem("y_ready"), sem("y_read")
        dve_step, out_gelu = sem("dve_step"), sem("out_gelu")
        block = core.block(ctx)

        @block.sync
        def _(sp):
            for dst, src in ((wq[:], d["la_wq"]), (wkv[:, 0:P], d["la_wk"]), (wkv[:, P:2 * P], d["la_wv"]), (wo[:], d["la_wo"]),
                             (w1[:], d["la_w1"]), (b1[:], d["la_b1"].rearrange("(j p) -> p j", p=P)),
                             (w2[:], d["la_w2"].rearrange("(j p) c -> p j c", p=P)), (b2[:], d["la_b2"].partition_broadcast(P)),
                             (gamma[:], d["la_gamma"].partition_broadcast(P)), (beta[:], d["la_beta"].partition_broadcast(P)),
                             (head[:], d["head_mask"])):
                with nc.allow_non_contiguous_dma("a bias per partition"):
                    sp.dma_start(dst, src).then_inc(loads, 16)

        @block.tensor
        def _(pe):
            pe_transpose_tiles(core, pe, ln, (ln_ready, 1), xt_full, (xt_copied, 0))
            pe.wait_ge(xt_copied, CHUNKS)
            pe.wait_ge(loads, 11 * 16)
            for g in range(CHUNKS):
                if g >= 2:
                    pe.wait_ge(q_ready, g - 1)
                nc.tensor.matmul(core.ps[2 + g % 2], wq[:], core.xt[:, g * CHUNK:(g + 1) * CHUNK], start=True,
                                 stop=True).then_inc(q_full, 1)
            for g in range(TILES // 2):
                if g >= 2:
                    pe.wait_ge(k_ready, g - 1)
                    pe.wait_ge(v_ready, g - 1)
                for t in range(2):
                    at = (2 * g + t) * P
                    ins = nc.tensor.matmul(core.ps[4 + g % 2][:, t * 2 * P:(t + 1) * 2 * P], core.xt[:, at:at + P], wkv[:],
                                           start=True, stop=True)
                ins.then_inc(kv_full, 1)
            for b in range(BATCH):
                pe.wait_ge(k_ready, (b + 1) * TILES // 4)
                pe.wait_ge(v_ready, (b + 1) * TILES // 4)
                for t in range(TILES // 2):
                    ins = nc.tensor.matmul(core.ps[6 + b][:, 0:P + 1], k[:, b * 8 + t, :], v1[:, b * 8 + t, :],
                                           start=(t == 0), stop=(t == 7))
                ins.then_inc(sums_full, 1)
            pe.wait_ge(q_ready, CHUNKS)
            for g in range(TILES // 2):
                pe.wait_ge(sums_ready, g // 4 + 1)
                if g >= 2:
                    pe.wait_ge(att_ready, g - 1)
                for t in range(2):
                    at = (2 * g + t) * P
                    ins = nc.tensor.matmul(core.ps[2 + g % 2][:, t * KV:(t + 1) * KV], q_t[:, at:at + P], kv[:, g // 4, :],
                                           start=True, stop=True)
                ins.then_inc(att_full, 1)
            pe_transpose_tiles(core, pe, att, (att_ready, TILES // 2), xt_full, (xt_copied, CHUNKS))
            pe.wait_ge(xt_copied, 2 * CHUNKS)
            for g in range(CHUNKS):
                if g >= 2:
                    pe.wait_ge(add_ready, g - 1)
                for t in range(4):
                    at = (4 * g + t) * P
                    ins = nc.tensor.matmul(core.ps[4 + g % 2][:, t * P:(t + 1) * P], core.xt[:, at:at + P], wo[:],
                                           start=True, stop=True)
                ins.then_inc(out_full, 1)
            pe_transpose_tiles(core, pe, ln, (ln_ready, 2), xt_full, (xt_copied, 2 * CHUNKS))
            pe.wait_ge(xt_copied, 3 * CHUNKS)
            with pe.Fori(0, CHUNKS) as c:
                for j in range(FB):
                    pe.wait_ge(h_ready, c * FB + j + 1)
                    nc.tensor.matmul(core.ps[j % 2], w1[:, j * P:(j + 1) * P], core.xt[:, bass.ds(c * CHUNK, CHUNK)],
                                     start=True, stop=True).then_inc(h_full, 1)
                pe.wait_ge(h_ready, c * FB + FB + 2)
                pe.wait_ge(y_read, c + 1)
                for t in range(4):
                    for j in range(FB):
                        ins = nc.tensor.matmul(core.ps[2][:, t * P:(t + 1) * P], hidden[:, j, t * P:(t + 1) * P], w2[:, j, :],
                                               start=(j == 0), stop=(j == FB - 1))
                ins.then_inc(y_full, 1)

        @block.scalar
        def _(act):
            act_rstd(core, act, stat, var_ready, rstd_ready, 1)
            act_rstd(core, act, stat, var_ready, rstd_ready, 2)
            act_copy_transposed(core, act, core.xt, xt_full, xt_copied)
            for g in range(TILES // 2):
                act.wait_ge(kv_full, g + 1)
                nc.scalar.copy(v1[:, 2 * g:2 * g + 2, 0:P],
                               core.ps[4 + g % 2].rearrange("p (t k c) -> p t k c", t=2, k=2)[:, :, 1]).then_inc(v_ready, 1)
            act_copy_transposed(core, act, core.xt, xt_full, xt_copied, CHUNKS)
            act_rstd(core, act, stat, var_ready, rstd_ready, 3)
            act_copy_transposed(core, act, core.xt, xt_full, xt_copied, 2 * CHUNKS)
            act.sem_inc(h_ready, 2)
            with act.Fori(0, CHUNKS) as c:
                act.wait_ge(y_read, c + 1)
                for j in range(FB):
                    act.wait_ge(h_full, c * FB + j + 1)
                    nc.scalar.activation(hidden[:, j, :], core.ps[j % 2], ACT.Gelu, bias=b1[:, j:j + 1]).then_inc(h_ready, 1)
            for g in range(CHUNKS):
                act.wait_ge(y_ready, g + 1)
                part = y[:, 4 * g:4 * g + 4, :]
                nc.scalar.activation(part, part, ACT.Gelu).then_inc(out_gelu, 1)

        @block.vector
        def _(dve):
            v = nc.vector
            step = Chain(dve, dve_step)
            step(v.memset(v1[:, :, P:P + 1], 1.0))
            step(dve_norm(core, step, core.x, core.xn, square, stat, 1e-5, var_ready, rstd_ready, 1))
            step(dve_norm(core, step, core.xn, ln, square, stat, 1e-6, var_ready, rstd_ready, 2))
            dve.wait_ge(loads, 11 * 16)
            step(v.tensor_tensor(ln[:], ln[:], core.row(gamma[:]), ALU.mult))
            step(v.tensor_tensor(ln[:], ln[:], core.row(beta[:]), ALU.add))
            dve.sem_inc(ln_ready, 1)
            for g in range(CHUNKS):
                dve.wait_ge(q_full, g + 1)
                v.tensor_scalar(q_t[:, g * CHUNK:(g + 1) * CHUNK], core.ps[2 + g % 2], 0.0, STAB, ALU.max, ALU.add).then_inc(q_ready, 1)
            for g in range(TILES // 2):
                dve.wait_ge(v_ready, g + 1)
                v.tensor_scalar(k[:, 2 * g:2 * g + 2, :], core.ps[4 + g % 2].rearrange("p (t k c) -> p t k c", t=2, k=2)[:, :, 0],
                                0.0, STAB, ALU.max, ALU.add).then_inc(k_ready, 1)
            for b in range(BATCH):
                dve.wait_ge(sums_full, b + 1)
                step(v.tensor_tensor(kv[:, b, 0:P].rearrange("p (h c) -> p h c", c=M), core.ps[6 + b][:, 0:P].rearrange("p (h c) -> p h c", c=M),
                                     head[:].unsqueeze(2).to_broadcast([P, H, M]), ALU.mult))
                step(v.tensor_tensor(kv[:, b, P:KV], head[:], core.ps[6 + b][:, P:P + 1].to_broadcast([P, H]), ALU.mult))
                dve.sem_inc(sums_ready, 1)
            for g in range(TILES // 2):
                dve.wait_ge(att_full, g + 1)
                part = core.ps[2 + g % 2][:, 0:2 * KV].rearrange("p (t n) -> p t n", t=2)
                step(v.reciprocal(recip[:, 2 * g:2 * g + 2], part[:, :, P:KV]))
                v.tensor_tensor(att[:, 2 * g:2 * g + 2, :].rearrange("p t (h c) -> p t h c", c=M), part[:, :, 0:P].rearrange("p t (h c) -> p t h c", c=M),
                                recip[:, 2 * g:2 * g + 2].unsqueeze(3).to_broadcast([P, 2, H, M]), ALU.mult).then_inc(att_ready, 1)
            for g in range(CHUNKS):
                dve.wait_ge(out_full, g + 1)
                v.tensor_tensor(add1[:, 4 * g:4 * g + 4, :], core.ps[4 + g % 2].rearrange("p (t c) -> p t c", c=P),
                                core.xn[:, 4 * g:4 * g + 4, :], ALU.add).then_inc(add_ready, 1)
            dve.wait_ge(add_ready, CHUNKS)
            step(dve_norm(core, step, add1, ln, square, stat, 1e-6, var_ready, rstd_ready, 3))
            step(v.tensor_tensor(ln[:], ln[:], core.row(gamma[:]), ALU.mult))
            step(v.tensor_tensor(ln[:], ln[:], core.row(beta[:]), ALU.add))
            dve.sem_inc(ln_ready, 1)
            step(v.tensor_tensor(core.x[:], core.x[:], add1[:], ALU.add))
            dve.sem_inc(y_read, 1)
            for g in range(CHUNKS):
                dve.wait_ge(y_full, g + 1)
                part = y[:, 4 * g:4 * g + 4, :]
                v.tensor_tensor(part, core.ps[2].rearrange("p (t c) -> p t c", c=P), core.row(b2[:], 4), ALU.add).then_inc(y_read, 1)
                dve.wait_ge(y_read, g + 2)
                dve.sem_inc(y_ready, 1)
            for g in range(CHUNKS):
                dve.wait_ge(out_gelu, g + 1)
                part = slice(4 * g, 4 * g + 4)
                step(v.tensor_tensor(core.x[:, part], core.x[:, part], y[:, part], ALU.add))


class HeadPair:
    T = SEQ // P
    SLOTS = 2 * T

    def __init__(self, core, ctx, tag):
        nc = self.nc = core.nc
        self.core = core
        sb = lambda name, shape, dt=F32: ctx.enter_context(nc.sbuf_tensor(tag + name, shape, dt))
        sem = lambda name: core.semaphore(ctx, tag + name)
        self.qz, self.kt = sb("q_z", [P, 2, SEQ]), sb("k_t", [P, SEQ])
        self.v = sb("v", [P, self.T, 2, 65])
        self.v_hi, self.v_lo = sb("v_hi", [P, self.T, 2, 65], BF16), sb("v_lo", [P, self.T, 2, 65], BF16)
        self.negmax = sb("negmax", [P, 2])
        self.p = sb("p", [P, 2, SEQ])
        self.p_hi, self.p_lo = sb("p_hi", [P, 2, SEQ], BF16), sb("p_lo", [P, 2, SEQ], BF16)
        self.recip = sb("recip", [P, 2])
        self.o = sb("o", [P, self.T, 2, 64])
        self.s_full = sem("s_full")
        self.max_ready = sem("max_ready")
        self.exp_done = sem("exp_done")
        self.pt_full = sem("pt_full")
        self.hi_ready = sem("hi_ready")
        self.lo_ready = sem("lo_ready")
        self.v_split = sem("v_split")
        self.v_split_hi = sem("v_split_hi")
        self.av_done = sem("av_done")
        self.o_ready = sem("o_ready")
        self.recip_ready = sem("recip_ready")

    def pe_seed(self, pe):
        pe.sem_inc(self.pt_full, 4)
        pe.sem_inc(self.av_done, 2)

    def act_seed(self, act):
        act.sem_inc(self.exp_done, 2)

    def dve_seed(self, dve):
        dve.sem_inc(self.lo_ready, 2)
        dve.sem_inc(self.o_ready, 2)

    def pe_wait_pair(self, pe, pair, slot0, tile0):
        if pair == 0:
            pe.wait_ge(self.exp_done, slot0 + 2)
        elif pair == 2:
            pe.wait_ge(self.lo_ready, slot0 * 2 + 2)
        elif pair == 3:
            pe.wait_ge(self.o_ready, tile0 + 2)

    def pe(self, pe, slot0, tile0, unit, banks_free=None):
        nc, core = self.nc, self.core

        def scores(i):
            t, h = i // 2, i % 2
            pe.wait_ge(self.exp_done, slot0 + i + 1)
            for half in range(2):
                ins = nc.tensor.matmul(core.ps[2 * h + half], self.qz[:, h, t * P:(t + 1) * P],
                                       self.kt[:, half * CHUNK:(half + 1) * CHUNK], start=True, stop=True)
            ins.then_inc(self.s_full, 1)

        def transpose(i):
            pe.wait_ge(self.exp_done, slot0 + i + 3)
            for g in range(2):
                pe.wait_ge(self.lo_ready, (slot0 + i) * 2 + g + 1)
                for j in range(4):
                    k = 4 * g + j
                    ins = nc.tensor.transpose(core.ps[4 + g][:, j * P:(j + 1) * P], self.p[:, i % 2, k * P:(k + 1) * P],
                                              core.ident[:])
                ins.then_inc(self.pt_full, 1)

        def values(i):
            t, h = i // 2, i % 2
            pe.wait_ge(self.lo_ready, (slot0 + i) * 2 + 4)
            if h == 0:
                pe.wait_ge(self.o_ready, tile0 + t + 1)
            out = core.ps[6 + t % 2][:, h * 65:(h + 1) * 65]
            for k in range(self.T):
                block = slice(k * P, (k + 1) * P)
                for n, (p, v) in enumerate(((self.p_hi, self.v_hi), (self.p_hi, self.v_lo), (self.p_lo, self.v_hi))):
                    ins = nc.tensor.matmul(out, p[:, h, block], v[:, k, h, :], start=(k == 0 and n == 0),
                                           stop=(k == self.T - 1 and n == 2))
            ins.then_inc(self.av_done, 1)

        for i in range(self.SLOTS + 2):
            if i < self.SLOTS:
                scores(i)
            if i == 1 and banks_free:
                pe.wait_ge(*banks_free)
            if 1 <= i <= self.SLOTS:
                transpose(i - 1)
            if i >= 2:
                if i == 2:
                    pe.wait_ge(self.v_split, unit + 1)
                values(i - 2)

    def act(self, act, slot0):
        nc, core = self.nc, self.core
        for i in range(self.SLOTS + 1):
            if i >= 1:
                h = (i - 1) % 2
                act.wait_ge(self.av_done, slot0 + i)
                for g in range(2):
                    act.wait_ge(self.pt_full, (slot0 + i - 1) * 2 + g + 5)
                    nc.scalar.copy(self.p_hi[:, h, g * CHUNK:(g + 1) * CHUNK], core.ps[4 + g]).then_inc(self.hi_ready, 1)
            if i < self.SLOTS:
                h = i % 2
                act.wait_ge(self.max_ready, slot0 + i + 1)
                act.wait_ge(self.pt_full, (slot0 + i) * 2 + 2)
                nc.scalar.activation(self.p[:, h, :], core.banks[:, 2 * h:2 * h + 2, :], ACT.Exp,
                                     bias=self.negmax[:, h:h + 1]).then_inc(self.exp_done, 1)

    def dve(self, dve, slot0, tile0):
        nc, core = self.nc, self.core
        for i in range(self.SLOTS + 2):
            if i < self.SLOTS:
                h = i % 2
                dve.wait_ge(self.s_full, slot0 + i + 1)
                nc.vector.tensor_reduce(self.negmax[:, h:h + 1], core.banks[:, 2 * h:2 * h + 2, :], AX.XY, ALU.max,
                                        negate=True).then_inc(self.max_ready, 1)
            if 1 <= i <= self.SLOTS:
                h = (i - 1) % 2
                for g in range(2):
                    part = slice(g * CHUNK, (g + 1) * CHUNK)
                    dve.wait_ge(self.hi_ready, (slot0 + i - 1) * 2 + g + 1)
                    nc.vector.tensor_tensor(self.p_lo[:, h, part], core.ps[4 + g], self.p_hi[:, h, part],
                                            ALU.subtract).then_inc(self.lo_ready, 1)
            if i >= 3 and i % 2:
                t = (i - 3) // 2
                dve.wait_ge(self.av_done, slot0 + 2 * t + 4)
                o = core.ps[6 + t % 2][:, 0:130].rearrange("p (h c) -> p h c", h=2)
                nc.vector.reciprocal(self.recip[:], o[:, :, 64]).then_inc(self.recip_ready, 1)
                dve.wait_ge(self.recip_ready, tile0 + t + 1)
                nc.vector.tensor_tensor(self.o[:, t], o[:, :, 0:64], core.col(self.recip[:], 64),
                                        ALU.mult).then_inc(self.o_ready, 1)

    def act_split_values(self, act, slot0, ready):
        act.wait_ge(*ready)
        act.wait_ge(self.av_done, slot0 + 2)
        self.nc.scalar.copy(self.v_hi[:], self.v[:]).then_inc(self.v_split_hi, 1)

    def pool_split_values(self, pool, unit):
        pool.wait_ge(self.v_split_hi, unit + 1)
        self.nc.gpsimd.tensor_tensor(self.v_lo[:], self.v[:], self.v_hi[:], ALU.subtract).then_inc(self.v_split, 1)


class HeadStream:
    T = SEQ // P
    SLOTS = 2 * T

    def __init__(self, core, ctx, tag):
        nc = self.nc = core.nc
        self.core = core
        sb = lambda name, shape, dt=F32: ctx.enter_context(nc.sbuf_tensor(tag + name, shape, dt))
        sem = lambda name: core.semaphore(ctx, tag + name)
        self.qz, self.kt = sb("q_z", [P, 2, 2, SEQ]), sb("k_t", [P, 2, SEQ])
        self.v = sb("v", [P, self.T, 2, 65])
        self.v_hi, self.v_lo = sb("v_hi", [P, 2, self.T, 2, 65], BF16), sb("v_lo", [P, 2, self.T, 2, 65], BF16)
        self.negmax = sb("negmax", [P, 2])
        self.p = sb("p", [P, 2, SEQ])
        self.p_hi, self.p_lo = sb("p_hi", [P, 2, SEQ], BF16), sb("p_lo", [P, 2, SEQ], BF16)
        self.recip = sb("recip", [P, 2])
        self.o = sb("o", [P, 2, self.T, 2, 64])
        self.filled = sem("filled")
        self.s_full = sem("s_full")
        self.max_ready = sem("max_ready")
        self.exp_done = sem("exp_done")
        self.pt_full = sem("pt_full")
        self.hi_ready = sem("hi_ready")
        self.lo_ready = sem("lo_ready")
        self.av_done = sem("av_done")
        self.o_ready = sem("o_ready")
        self.recip_ready = sem("recip_ready")
        self.v_split_hi = sem("v_split_hi")
        self.v_split = sem("v_split")

    def fill(self, pool):
        g = self.nc.gpsimd
        for ap, value in ((self.v[:, :, :, 64:65], 1.0), (self.qz[:], 0.0), (self.o[:], 0.0), (self.p[:], 1.0),
                          (self.p_hi[:], 1.0), (self.p_lo[:], 0.0), (self.v_hi[:, 1, :, :, 0:64], 0.0),
                          (self.v_hi[:, 1, :, :, 64:65], 1.0), (self.v_lo[:, 1], 0.0)):
            g.memset(ap, value).then_inc(self.filled, 1)
    FILLS = 9

    def pe_seed(self, pe):
        pe.wait_ge(self.filled, self.FILLS)
        pe.sem_inc(self.pt_full, 2)
        pe.sem_inc(self.av_done, 1)

    def act_seed(self, act):
        act.wait_ge(self.filled, self.FILLS)
        act.sem_inc(self.exp_done, 2)

    def dve_seed(self, dve):
        dve.wait_ge(self.filled, self.FILLS)
        dve.sem_inc(self.lo_ready, 2)
        dve.sem_inc(self.o_ready, 1)

    def scores(self, pe, unit, b, i):
        s, t, h = unit * self.SLOTS + i, i // 2, i % 2
        pe.wait_ge(self.exp_done, s + 1)
        for half in range(2):
            ins = self.nc.tensor.matmul(self.core.ps[2 * h + half], self.qz[:, b, h, t * P:(t + 1) * P],
                                        self.kt[:, b, half * CHUNK:(half + 1) * CHUNK], start=True, stop=True)
        ins.then_inc(self.s_full, 1)

    def transpose(self, pe, unit, i, g):
        s, h = unit * self.SLOTS + i, (i - 1) % 2
        if g == 0:
            pe.wait_ge(self.exp_done, s + 2)
        pe.wait_ge(self.lo_ready, s * 2 + g + 1)
        for j in range(4):
            k = 4 * g + j
            ins = self.nc.tensor.transpose(self.core.ps[4 + g][:, j * P:(j + 1) * P], self.p[:, h, k * P:(k + 1) * P],
                                           self.core.ident[:])
        ins.then_inc(self.pt_full, 1)

    def values(self, pe, unit, b, i):
        s, t, h = unit * self.SLOTS + i, (i - 2) // 2, i % 2
        own = b if i >= 2 else 1 - b
        pe.wait_ge(self.lo_ready, s * 2 + 2)
        if h == 0:
            pe.wait_ge(self.o_ready, unit * self.T + i // 2 + 1)
        if i == 2:
            pe.wait_ge(self.v_split, unit + 1)
        at = (t % 2) * 130 + h * 65
        for k in range(self.T):
            block = slice(k * P, (k + 1) * P)
            for n, (p, v) in enumerate(((self.p_hi, self.v_hi), (self.p_hi, self.v_lo), (self.p_lo, self.v_hi))):
                ins = self.nc.tensor.matmul(self.core.ps[6][:, at:at + 65], p[:, h, block], v[:, own, k, h, :],
                                            start=(k == 0 and n == 0), stop=(k == self.T - 1 and n == 2))
        ins.then_inc(self.av_done, 1)

    def act_hi(self, act, unit, i):
        s, h = unit * self.SLOTS + i, (i - 1) % 2
        act.wait_ge(self.av_done, s + 1)
        for g in range(2):
            act.wait_ge(self.pt_full, s * 2 + g + 3)
            self.nc.scalar.copy(self.p_hi[:, h, g * CHUNK:(g + 1) * CHUNK], self.core.ps[4 + g]).then_inc(self.hi_ready, 1)

    def act_exp(self, act, unit, i):
        s, h = unit * self.SLOTS + i, i % 2
        act.wait_ge(self.max_ready, s + 1)
        act.wait_ge(self.pt_full, s * 2 + 2)
        self.nc.scalar.activation(self.p[:, h, :], self.core.banks[:, 2 * h:2 * h + 2, :], ACT.Exp,
                                  bias=self.negmax[:, h:h + 1]).then_inc(self.exp_done, 1)

    def dve_max(self, dve, unit, i):
        h = i % 2
        dve.wait_ge(self.s_full, unit * self.SLOTS + i + 1)
        self.nc.vector.tensor_reduce(self.negmax[:, h:h + 1], self.core.banks[:, 2 * h:2 * h + 2, :], AX.XY, ALU.max,
                                     negate=True).then_inc(self.max_ready, 1)

    def dve_lo(self, dve, unit, i):
        s, h = unit * self.SLOTS + i, (i - 1) % 2
        for g in range(2):
            part = slice(g * CHUNK, (g + 1) * CHUNK)
            dve.wait_ge(self.hi_ready, s * 2 + g + 1)
            self.nc.vector.tensor_tensor(self.p_lo[:, h, part], self.core.ps[4 + g], self.p_hi[:, h, part],
                                         ALU.subtract).then_inc(self.lo_ready, 1)

    def dve_normalise(self, dve, unit, b, i):
        t = (i - 3) // 2
        own = b if i >= 3 else 1 - b
        dve.wait_ge(self.av_done, unit * self.SLOTS + i + 2)
        o = self.core.ps[6][:, (t % 2) * 130:(t % 2 + 1) * 130].rearrange("p (h c) -> p h c", h=2)
        self.nc.vector.reciprocal(self.recip[:], o[:, :, 64]).then_inc(self.recip_ready, 1)
        dve.wait_ge(self.recip_ready, unit * self.T + t + 2)
        self.nc.vector.tensor_tensor(self.o[:, own, t % self.T], o[:, :, 0:64], self.core.col(self.recip[:], 64),
                                     ALU.mult).then_inc(self.o_ready, 1)

    def act_split_values(self, act, unit, b, ready):
        act.wait_ge(*ready)
        self.nc.scalar.copy(self.v_hi[:, b], self.v[:]).then_inc(self.v_split_hi, 1)

    def pool_split_values(self, pool, unit, b):
        pool.wait_ge(self.v_split_hi, unit + 1)
        self.nc.gpsimd.tensor_tensor(self.v_lo[:, b], self.v[:], self.v_hi[:, b], ALU.subtract).then_inc(self.v_split, 1)


def attention_stage(core):
    nc, d = core.nc, core.dram
    PAIRS = 8
    UNITS = PAIRS * BATCH
    tag = "at_"
    with ExitStack() as ctx:
        sb = lambda name, shape, dt=F32: ctx.enter_context(nc.sbuf_tensor(tag + name, shape, dt))
        sem = lambda name: core.semaphore(ctx, tag + name)
        w = sb("w", [P, 5, (PAIRS + 1) * P], BF16)
        bias_all, bias = sb("bias_all", [P, PAIRS + 1, 4], BF16), sb("bias", [P, 4])
        bv = sb("bv", [P, (PAIRS + 1) * P], BF16)
        wo_all = sb("wo_all", [P, PAIRS, P], BF16)
        wo = sb("wo", [P, PAIRS + 1, P])
        bo = sb("bo", [P, P], BF16)
        rope = sb("rope", [P, 4, SEQ])
        xt_parts = sb("xt_parts", [P, 3, TOKENS], BF16)
        turned = sb("turned", [P, 2, CHUNK])
        o_t = sb("o_t", [P, SEQ])
        stat = sb("stat", [P, 4, TILES])
        square = sb("square", [P, TILES, P])
        rest = square[:].rearrange("p t c -> p (t c)")
        hs = HeadStream(core, ctx, tag)

        loads, padded = sem("loads"), sem("padded")
        var_ready, rstd_ready, normed = sem("var_ready"), sem("rstd_ready"), sem("normed")
        xt_full, xt_copied = sem("xt_full"), sem("xt_copied")
        part_ready, rest_ready = sem("part_ready"), sem("rest_ready")
        proj_full = sem("proj_full")
        terms_ready = sem("terms_ready")
        bias_ready = sem("bias_ready")
        qk_ready = sem("qk_ready")
        v_full, v_ready = sem("v_full"), sem("v_ready")
        ot_full, ot_ready = sem("ot_full"), sem("ot_ready")
        y_full, y_added = sem("y_full"), sem("y_added")
        dve_step = sem("dve_step")
        spare = core.ps[7]
        LOADS = 9
        block = core.block(ctx)

        @block.sync
        def _(sp):
            biases = tuple((bias_all[:, 0:PAIRS, k], d["at_bias"][k].rearrange("g p -> p g")) for k in range(4))
            for dst, src in ((w[:, :, 0:PAIRS * P], d["at_w"].rearrange("k c n -> c k n")),
                             (bv[:, 0:PAIRS * P], d["at_bv"].partition_broadcast(P)), (wo_all[:], d["at_wo"].rearrange("(g p) c -> p g c", p=P)),
                             (bo[:], d["at_bo"].partition_broadcast(P)), (rope[:], d["rope"].rearrange("k p s -> p k s"))) + biases:
                with nc.allow_non_contiguous_dma("head-major weights"):
                    sp.dma_start(dst, src).then_inc(loads, 16)

        @block.tensor
        def _(pe):
            pe_transpose_tiles(core, pe, core.xn, (normed, 1), xt_full, (xt_copied, 0))
            pe.wait_ge(loads, LOADS * 16)
            pe.wait_ge(padded, 5)
            pe.wait_ge(part_ready, 2)
            pe.wait_ge(rest_ready, 2)

            def project(unit, pair, b, n, first=False):
                if n == 0:
                    if not first:
                        pe.wait_ge(v_ready, unit * 2)
                        pe.wait_ge(y_added, unit * 2 - 1)
                elif n <= 8:
                    pe.wait_ge(terms_ready, unit * 8 + n)
                else:
                    pe.wait_ge(v_ready, unit * 2 + 1)
                if n < 8:
                    kind, at = 2 * (n // 4) + n % 2, b * SEQ + (n // 2 % 2) * CHUNK
                    for j in range(3):
                        ins = nc.tensor.matmul(spare, w[:, kind, bass.ds(pair * P, P)], xt_parts[:, j, at:at + CHUNK],
                                               start=(j == 0), stop=(j == 2))
                    ins.then_inc(proj_full, 1)
                else:
                    for t in range(4):
                        at = b * SEQ + (4 * (n - 8) + t) * P
                        for j in range(3):
                            ins = nc.tensor.matmul(spare[:, t * P:(t + 1) * P], xt_parts[:, j, at:at + P],
                                                   w[:, 4, bass.ds(pair * P, P)], start=(j == 0), stop=(j == 2))
                    ins.then_inc(v_full, 1)

            def output(unit, b, at, n, v_count):
                if n == 0:
                    pe.wait_ge(v_ready, v_count)
                    pe.wait_ge(hs.o_ready, unit * hs.T + 2)
                else:
                    pe.wait_ge(ot_ready, unit * 2 + min(n, 2))
                if n == 3:
                    pe.wait_ge(y_added, unit * 2 + 2)
                for t in range(4):
                    tile = 4 * (n % 2) + t
                    if n < 2:
                        ins = nc.tensor.transpose(spare[:, t * P:(t + 1) * P], hs.o[:, 1 - b, tile].rearrange("p h c -> p (h c)"),
                                                  core.ident[:])
                    else:
                        ins = nc.tensor.matmul(spare[:, t * P:(t + 1) * P], o_t[:, tile * P:(tile + 1) * P],
                                               wo[:, bass.ds(at, 1), :].rearrange("p a b -> p (a b)"), start=True, stop=True)
                ins.then_inc(ot_full if n < 2 else y_full, 1)

            for n in range(10):
                project(0, 0, 0, n, True)
            hs.pe_seed(pe)
            with pe.Fori(0, PAIRS) as pair:
                for b in range(BATCH):
                    u = pair * BATCH + b
                    for i in range(hs.SLOTS):
                        if i == 0:
                            pe.wait_ge(qk_ready, u * 4 + 5)
                        hs.scores(pe, u, b, i)
                        for g in range(2):
                            hs.transpose(pe, u, i, g)
                        hs.values(pe, u, b, i)
                        if i < 10:
                            project(u + 1, pair + b, 1 - b, i)
                        elif i < 14:
                            output(u, b, pair + b, i - 10, u * 2 + 4)
            for g in range(2):
                hs.transpose(pe, UNITS, 0, g)
            hs.values(pe, UNITS, 0, 0)
            hs.values(pe, UNITS, 0, 1)
            for n in range(4):
                output(UNITS, 0, PAIRS, n, UNITS * 2 + 2)

        @block.scalar
        def _(act):
            act_rstd(core, act, stat, var_ready, rstd_ready, 1)
            act_copy_transposed(core, act, core.xt, xt_full, xt_copied)
            act.wait_ge(xt_copied, CHUNKS)
            nc.scalar.copy(xt_parts[:, 0, :], core.xt[:]).then_inc(part_ready, 1)
            act.wait_ge(rest_ready, 1)
            nc.scalar.copy(xt_parts[:, 1, :], rest).then_inc(part_ready, 1)
            hs.act_seed(act)

            def copy_outputs(u, n):
                act.wait_ge(ot_full, u * 2 + n + 1)
                nc.scalar.copy(o_t[:, n * CHUNK:(n + 1) * CHUNK], spare).then_inc(ot_ready, 1)

            hs.act_split_values(act, 0, 0, (v_ready, 2))
            with act.Fori(0, PAIRS) as pair:
                for b in range(BATCH):
                    u = pair * BATCH + b
                    for i in range(hs.SLOTS):
                        hs.act_hi(act, u, i)
                        hs.act_exp(act, u, i)
                        if i in (10, 11):
                            copy_outputs(u, i - 10)
                        if i == 12:
                            hs.act_split_values(act, u + 1, 1 - b, (v_ready, u * 2 + 4))
            hs.act_hi(act, UNITS, 0)
            for n in range(2):
                copy_outputs(UNITS, n)

        @block.gpsimd
        def _(pool):
            g = nc.gpsimd
            hs.fill(pool)
            for ap in (w[:, :, PAIRS * P:], bias_all[:, PAIRS, :], bv[:, PAIRS * P:], wo[:, 0]):
                g.memset(ap, 0.0).then_inc(padded, 1)
            pool.wait_ge(loads, LOADS * 16)
            g.tensor_copy(wo[:, 1:], wo_all[:]).then_inc(padded, 1)

            def sum_keys(unit, b):
                for c in range(2):
                    pool.wait_ge(terms_ready, unit * 8 + 2 * c + 6)
                    g.tensor_tensor(hs.kt[:, b, c * CHUNK:(c + 1) * CHUNK], turned[:, 0, :], turned[:, 1, :],
                                    ALU.add).then_inc(qk_ready, 1)
                hs.pool_split_values(pool, unit, b)

            sum_keys(0, 0)
            with pool.Fori(0, PAIRS) as pair:
                for b in range(BATCH):
                    sum_keys(pair * BATCH + b + 1, 1 - b)

        @block.vector
        def _(dve):
            v = nc.vector
            step = Chain(dve, dve_step)
            step(dve_norm(core, step, core.x, core.xn, square, stat, 1e-5, var_ready, rstd_ready, 1))
            dve.sem_inc(normed, 1)
            dve.wait_ge(loads, LOADS * 16)
            step(v.tensor_tensor(core.x[:], core.x[:], core.row(bo[:]), ALU.add))
            dve.wait_ge(part_ready, 1)
            v.tensor_tensor(rest, core.xt[:], xt_parts[:, 0, :], ALU.subtract).then_inc(rest_ready, 1)
            dve.wait_ge(part_ready, 2)
            v.tensor_tensor(xt_parts[:, 2, :], rest, xt_parts[:, 1, :], ALU.subtract).then_inc(rest_ready, 1)
            dve.wait_ge(padded, 5)

            def rotate(unit, pair, b, n, first=False):
                if n < 8:
                    g, term = n // 2, n % 2
                    kind, chunk = 2 * (g // 2) + term, slice((g % 2) * CHUNK, (g % 2 + 1) * CHUNK)
                    dve.wait_ge(proj_full, unit * 8 + n + 1)
                    if term == 0:
                        dve.wait_ge(qk_ready, unit * 4 + g + 1)
                    if n == 0:
                        v.tensor_copy(bias[:], bias_all[:, bass.ds(pair, 1), :].rearrange("p a b -> p (a b)")).then_inc(bias_ready, 1)
                        dve.wait_ge(bias_ready, unit + 1)
                    v.scalar_tensor_tensor(out=turned[:, term, :], in0=spare, scalar=bias[:, kind:kind + 1],
                                           in1=rope[:, kind, chunk], op0=ALU.add, op1=ALU.mult).then_inc(terms_ready, 1)
                    if n in (1, 3):
                        dve.wait_ge(terms_ready, unit * 8 + n + 1)
                        for h in range(2):
                            rows = slice(64 * h, 64 * h + 64)
                            ins = v.tensor_tensor(hs.qz[rows, b, h, chunk], turned[rows, 0, :], turned[rows, 1, :], ALU.add)
                        ins.then_inc(qk_ready, 1)
                    return
                if n == 8 and not first:
                    dve.wait_ge(hs.v_split, unit)
                dve.wait_ge(v_full, unit * 2 + n - 7)
                v.tensor_tensor(hs.v[:, 4 * (n - 8):4 * (n - 7), :, 0:64], spare.rearrange("p (t h c) -> p t h c", t=4, h=2),
                                bv[:, bass.ds(pair * P, P)].rearrange("p (h c) -> p h c", h=2).unsqueeze(1).to_broadcast([P, 4, 2, 64]),
                                ALU.add).then_inc(v_ready, 1)

            def add_outputs(u, b, n):
                dve.wait_ge(y_full, u * 2 + n + 1)
                at = b * hs.T + 4 * n
                v.tensor_tensor(core.x[:, at:at + 4, :], core.x[:, at:at + 4, :], spare.rearrange("p (t c) -> p t c", c=P),
                                ALU.add).then_inc(y_added, 1)

            dve.sem_inc(qk_ready, 1)
            dve.sem_inc(y_added, 1)
            hs.dve_seed(dve)
            for n in range(10):
                rotate(0, 0, 0, n, True)
            with dve.Fori(0, PAIRS) as pair:
                for b in range(BATCH):
                    u = pair * BATCH + b
                    for i in range(hs.SLOTS):
                        hs.dve_max(dve, u, i)
                        hs.dve_lo(dve, u, i)
                        if i % 2:
                            hs.dve_normalise(dve, u, b, i)
                        if i < 10:
                            rotate(u + 1, pair + b, 1 - b, i)
                        elif 12 <= i < 14:
                            add_outputs(u, 1 - b, i - 12)
            hs.dve_lo(dve, UNITS, 0)
            hs.dve_normalise(dve, UNITS, 0, 1)
            for n in range(2):
                add_outputs(UNITS, 1, n)


def expert_attention_stage(core, tag):
    nc, d = core.nc, core.dram
    H, E, D, TOP = 8, 5, 64, 3
    PAIRS = H // 2
    ED = E * D
    ROWS_OUT = (P, P, ED - 2 * P)
    with ExitStack() as ctx:
        sb = lambda name, shape, dt=F32: ctx.enter_context(nc.sbuf_tensor(tag + name, shape, dt))
        sem = lambda name: core.semaphore(ctx, tag + name)
        w = sb("w", [P, 3, H, ED])
        w_gate = sb("w_gate", [P, 2 * H * E])
        wo = sb("wo", [P, 3, P])
        stat = sb("stat", [P, 4, TILES])
        gate = sb("gate", [P, 2, TILES, H, E])
        mask = sb("mask", [P, 2, TILES, H, E])
        scratch = sb("scratch", [P, 8 * ED])
        square = scratch[:, 0:TILES * P].rearrange("p (t c) -> p t c", c=P)
        beats = scratch[:, 0:2 * TILES * H * E].rearrange("p (n e) -> p n e", e=E)
        lost = sb("lost", [P, 2 * TILES * H])
        qk_product, v_product = sb("qk_product", [P, 2, 2, 2, E, D]), sb("v_product", [P, 2, 2, E, D])
        tok = sb("tok", [P, 2, 8, 2, D])
        routed = sb("routed", [P, 2, E, D])
        z = sb("z", [P, TILES, 3 * P])
        z_t = sb("z_t", [P, 2, 3, P])
        hp = HeadPair(core, ctx, tag)

        loads = sem("loads")
        var_ready, rstd_ready, normed = sem("var_ready"), sem("rstd_ready"), sem("normed")
        xt_full, xt_copied = sem("xt_full"), sem("xt_copied")
        gates_full, gates_ready = sem("gates_full"), sem("gates_ready")
        proj_full = sem("proj_full")
        product_ready = sem("product_ready")
        tok_ready = sem("tok_ready")
        v_ready = sem("v_ready")
        qk_full, qk_ready = sem("qk_full"), sem("qk_ready")
        zt_full, zt_ready = sem("zt_full"), sem("zt_ready")
        y_full, y_added = sem("y_full"), sem("y_added")
        dve_step, pool_step, z_ready = sem("dve_step"), sem("pool_step"), sem("z_ready")
        GB = 6
        block = core.block(ctx)

        @block.sync
        def _(sp):
            for dst, src in ((w[:].rearrange("p k h n -> p k (h n)"), d["ex_w"].rearrange("k c n -> c k n")), (w_gate[:], d["ex_gate"]),
                             (wo[:, 0:2, :], d["ex_wo"][0:256, :].rearrange("(j p) c -> p j c", p=P)),
                             (wo[0:64, 2, :], d["ex_wo"][256:320, :])):
                sp.dma_start(dst, src).then_inc(loads, 16)

        @block.tensor
        def _(pe):
            pe_transpose_tiles(core, pe, core.xn, (normed, 1), xt_full, (xt_copied, 0))
            pe.wait_ge(xt_copied, CHUNKS)
            pe.wait_ge(loads, 4 * 16)
            for t in range(TILES):
                ins = nc.tensor.matmul(core.ps[2 + t // GB][:, (t % GB) * 80:(t % GB + 1) * 80], core.xt[:, t * P:(t + 1) * P],
                                       w_gate[:], start=True, stop=True)
            ins.then_inc(gates_full, 1)
            pe.wait_ge(gates_ready, 3)
            hp.pe_seed(pe)
            with pe.Fori(0, PAIRS) as pair:
                for b in range(BATCH):
                    u = pair * BATCH + b
                    turn = u * hp.T
                    for t in range(hp.T):
                        for kind in range(3):
                            n = t * 3 + kind
                            if n < 4:
                                hp.pe_wait_pair(pe, n, turn * 2, turn)
                            pe.wait_ge(product_ready, u * 24 + n + 1)
                            for h in range(2):
                                ins = nc.tensor.matmul(core.ps[2 * (n % 4) + h][:, 0:ED],
                                                       core.xt[:, b * SEQ + t * P:b * SEQ + (t + 1) * P],
                                                       w[:, kind, bass.ds(pair * 2 + h, 1), :].rearrange("p a n -> p (a n)"),
                                                       start=True, stop=True)
                            ins.then_inc(proj_full, 1)
                    pe.wait_ge(product_ready, u * 24 + 28)
                    pe.wait_ge(tok_ready, u * 16 + 16)
                    for g in range(4):
                        for t in range(4):
                            ins = nc.tensor.transpose(core.ps[2 * g][:, t * P:(t + 1) * P],
                                                      tok[:, g // 2, 4 * (g % 2) + t].rearrange("p h c -> p (h c)"),
                                                      core.ident[:])
                        ins.then_inc(qk_full, 1)
                    pe.wait_ge(qk_ready, u * 4 + 4)
                    hp.pe(pe, turn * 2, turn, u)
            pe.wait_ge(z_ready, 1)
            for t in range(TILES + 1):
                if t < TILES:
                    if t >= 2:
                        pe.wait_ge(zt_ready, t - 1)
                    for j in range(3):
                        ins = nc.tensor.transpose(core.ps[t % 2][:, j * P:(j + 1) * P], z[:, t, j * P:(j + 1) * P], core.ident[:])
                    ins.then_inc(zt_full, 1)
                if t >= 1:
                    pe.wait_ge(zt_ready, t)
                    if t >= 3:
                        pe.wait_ge(y_added, t - 2)
                    for j, n in enumerate(ROWS_OUT):
                        ins = nc.tensor.matmul(core.ps[2 + (t - 1) % 2][:, 0:P], z_t[0:n, (t - 1) % 2, j, :], wo[0:n, j, :],
                                               start=(j == 0), stop=(j == 2))
                    ins.then_inc(y_full, 1)

        @block.scalar
        def _(act):
            act_rstd(core, act, stat, var_ready, rstd_ready, 1)
            act_copy_transposed(core, act, core.xt, xt_full, xt_copied)
            act.wait_ge(gates_full, 1)
            for i in range(3):
                n = min(GB, TILES - i * GB)
                for which in range(2):
                    ins = nc.scalar.activation(gate[:, which, i * GB:i * GB + n],
                                               core.ps[2 + i][:, 0:n * 80].rearrange("p (t w h e) -> p t w h e", w=2, h=H, e=E)[:, :, which],
                                               ACT.Sigmoid)
                ins.then_inc(gates_ready, 1)
            hp.act_seed(act)
            with act.Fori(0, PAIRS) as pair:
                for b in range(BATCH):
                    u = pair * BATCH + b
                    for g in range(4):
                        act.wait_ge(qk_full, u * 4 + g + 1)
                        chunk = slice((g % 2) * CHUNK, (g % 2 + 1) * CHUNK)
                        if g < 2:
                            for h in range(2):
                                rows = slice(64 * h, 64 * h + 64)
                                ins = nc.scalar.copy(hp.qz[rows, h, chunk], core.ps[2 * g][rows, :])
                        else:
                            ins = nc.scalar.copy(hp.kt[:, chunk], core.ps[2 * g])
                        ins.then_inc(qk_ready, 1)
                    hp.act_split_values(act, u * hp.SLOTS, (v_ready, u * 8 + 8))
                    hp.act(act, u * hp.SLOTS)
            for t in range(TILES):
                act.wait_ge(zt_full, t + 1)
                if t >= 2:
                    act.wait_ge(y_full, t - 1)
                nc.scalar.copy(z_t[:, t % 2].rearrange("p j c -> p (j c)"), core.ps[t % 2][:, 0:3 * P]).then_inc(zt_ready, 1)

        @block.gpsimd
        def _(pool):
            g = nc.gpsimd
            step = Chain(pool, pool_step)
            with step.loop(PAIRS, BATCH * (16 * 2 + 3 * hp.T)) as pair:
                for b in range(BATCH):
                    u = pair * BATCH + b
                    for t in range(hp.T):
                        for kind in range(2):
                            i = t * 3 + kind
                            pool.wait_ge(product_ready, u * 24 + i + 5)
                            part = qk_product[:, t % 2, kind]
                            step(g.tensor_tensor(part[:, :, 0:2], part[:, :, 0:2], part[:, :, 2:4], ALU.add))
                            step(g.tensor_tensor(part[:, :, 0], part[:, :, 0], part[:, :, 1], ALU.add))
                            g.tensor_tensor(tok[:, kind, t], part[:, :, 0], part[:, :, 4], ALU.add).then_inc(tok_ready, 1)
                    hp.pool_split_values(pool, u)
                    for t in range(hp.T):
                        tile = b * hp.T + t
                        pool.wait_ge(hp.o_ready, u * hp.T + t + 3)
                        step(g.tensor_tensor(routed[:], hp.o[:, t].unsqueeze(2).to_broadcast([P, 2, E, D]),
                                             mask[:, 1, tile, bass.ds(pair * 2, 2), :].unsqueeze(3).to_broadcast([P, 2, E, D]),
                                             ALU.mult))
                        for h in range(2):
                            step(g.tensor_tensor(z[:, tile, 0:ED], z[:, tile, 0:ED], routed[:, h].rearrange("p e c -> p (e c)"), ALU.add))
            pool.sem_inc(z_ready, 1)

        @block.vector
        def _(dve):
            v = nc.vector
            step = Chain(dve, dve_step)
            step(v.memset(hp.v[:, :, :, 64:65], 1.0))
            step(v.memset(hp.qz[:], 0.0))
            step(v.memset(z[:], 0.0))
            step(dve_norm(core, step, core.x, core.xn, square, stat, 1e-5, var_ready, rstd_ready, 1))
            dve.sem_inc(normed, 1)
            g3 = gate[:].rearrange("p w t h e -> p (w t h) e")
            m3 = mask[:].rearrange("p w t h e -> p (w t h) e")
            for e in range(E):
                step(v.memset(m3[:, :, e], float(E - 1 - e)))
            dve.wait_ge(gates_ready, 3)
            n = 2 * TILES * H
            for e in range(E - 1):
                rest = E - 1 - e
                step(v.tensor_tensor(beats[:, :, 0:rest], g3[:, :, e].unsqueeze(2).to_broadcast([P, n, rest]), g3[:, :, e + 1:E],
                                     ALU.is_ge))
                step(v.tensor_tensor(m3[:, :, e + 1:E], m3[:, :, e + 1:E], beats[:, :, 0:rest], ALU.add))
                step(v.tensor_reduce(lost[:], beats[:, :, 0:rest], AX.X, ALU.add))
                step(v.tensor_tensor(m3[:, :, e], m3[:, :, e], lost[:], ALU.subtract))
            step(v.tensor_scalar(m3, m3, float(TOP), None, ALU.is_lt))
            step(v.tensor_tensor(gate[:], gate[:], mask[:], ALU.mult))
            step(v.tensor_scalar(gate[:, 1], gate[:, 1], float(D) ** -0.5, None, ALU.mult))
            hp.dve_seed(dve)
            dve.sem_inc(product_ready, 4)
            with dve.Fori(0, PAIRS) as pair:
                for b in range(BATCH):
                    u = pair * BATCH + b

                    def sum_values(t):
                        dve.wait_ge(product_ready, u * 24 + t * 3 + 7)
                        v.tensor_reduce(hp.v[:, t, :, 0:D], v_product[:, t % 2].rearrange("p h e c -> p h c e"), AX.X,
                                        ALU.add).then_inc(v_ready, 1)

                    for t in range(hp.T):
                        for kind in range(3):
                            i = t * 3 + kind
                            dve.wait_ge(proj_full, u * 24 + i + 1)
                            which = 1 if kind == 0 else 0
                            gates = gate[:, which, b * hp.T + t, bass.ds(pair * 2, 2), :]
                            if kind < 2 and t >= 2:
                                dve.wait_ge(tok_ready, u * 16 + (t - 2) * 2 + kind + 1)
                            if kind == 2 and t >= 2:
                                dve.wait_ge(v_ready, u * 8 + t - 1)
                            product = qk_product[:, t % 2, kind] if kind < 2 else v_product[:, t % 2]
                            v.tensor_tensor(product, core.banks[:, 2 * (i % 4):2 * (i % 4) + 2, 0:ED].rearrange("p h (e c) -> p h e c", c=D),
                                            gates.unsqueeze(3).to_broadcast([P, 2, E, D]), ALU.mult).then_inc(product_ready, 1)
                        if t:
                            sum_values(t - 1)
                    sum_values(hp.T - 1)
                    hp.dve(dve, u * hp.SLOTS, u * hp.T)
            for t in range(TILES):
                dve.wait_ge(y_full, t + 1)
                v.tensor_tensor(core.x[:, t], core.x[:, t], core.ps[2 + t % 2][:, 0:P], ALU.add).then_inc(y_added, 1)


def ssm_stage(core):
    nc, d = core.nc, core.dram
    K, H = 32, 8
    TAPS = 4
    BLOCKS = 2
    ORDER = (4, 0, 1, 2, 3)
    TURN_HI = 6.28125
    TURN_LO = 2 * np.pi - TURN_HI
    ROUND = 1.5 * 2.0 ** 23
    tag = "ss_"
    with ExitStack() as ctx:
        sb = lambda name, shape, dt=F32: ctx.enter_context(nc.sbuf_tensor(tag + name, shape, dt))
        sem = lambda name: core.semaphore(ctx, tag + name)
        w_in = sb("w_in", [P, 4 * P + K])
        taps, taps_s = sb("taps", [P, 4, TAPS + 1]), sb("taps_s", [K, TAPS + 1])
        theta = sb("theta", [P, BLOCKS])
        slopes, scale, dist = sb("slopes", [K, 8]), sb("scale", [K, 1]), sb("dist", [K, SEQ])
        logits = sb("logits", [P, 3])
        mix = sb("mix", [P, 8])
        w_rep, norm = sb("w_rep", [P, 2, H]), sb("norm", [P, 2])
        w_diag = sb("w_diag", [P, 2, P])
        head = sb("head", [P, 16])
        spread, gather, eps_eye = sb("spread", [P, BLOCKS, P]), sb("gather", [P, BLOCKS, K]), sb("eps_eye", [K, K])
        w_out = sb("w_out", [P, BLOCKS, P])
        square = sb("square", [P, TILES, P])
        stat = sb("stat", [P, 4, TILES])
        raw = [sb(f"raw{i}", [P, BATCH, SEQ + TAPS - 1]) for i in range(2)]
        score = sb("score", [K, BATCH, SEQ])
        weight = sb("weight", [K, SEQ])
        den = sb("den", [K, BATCH, SEQ])
        value = [sb(f"value{j}", [P, BATCH, SEQ]) for j in range(BLOCKS)]
        gate = [sb(f"gate{j}", [P, BATCH, SEQ]) for j in range(BLOCKS)]
        angle, poly = square[:].rearrange("p t c -> p (t c)"), sb("poly", [P, TOKENS])
        sin, cos = sb("sin", [P, TOKENS]), sb("cos", [P, TOKENS])
        num = [[sb(f"num{j}{i}", [P, BATCH, SEQ]) for i in range(2)] for j in range(BLOCKS)]
        factor = sb("factor", [P, CHUNK])
        ones = sb("ones", [P, SEQ])
        flat = lambda t: t[:].rearrange("p b s -> p (b s)")

        loads = sem("loads")
        var_ready, rstd_ready, normed = sem("var_ready"), sem("rstd_ready"), sem("normed")
        xt_full, xt_copied = sem("xt_full"), sem("xt_copied")
        raw_full, raw_ready, conv_done = sem("raw_full"), sem("raw_ready"), sem("conv_done")
        small_ready, small_exp, small_ln = sem("small_ready"), sem("small_exp"), sem("small_ln")
        score_ready, weights_ready, pw_ready = sem("score_ready"), sem("weights_ready"), sem("pw_ready")
        spread_full, spread_used = sem("spread_full"), sem("spread_used")
        angle_ready, waves_ready, num_ready, squares_ready = sem("angle_ready"), sem("waves_ready"), sem("num_ready"), sem("squares_ready")
        squares_used, power_full, power_inv, factor_ready = sem("squares_used"), sem("power_full"), sem("power_inv"), sem("factor_ready")
        gates_ready, mixed_full, mixed_read, gated_ready = sem("gates_ready"), sem("mixed_full"), sem("mixed_read"), sem("gated_ready")
        out_full = sem("out_full")
        dve_step, act_step = sem("dve_step"), sem("act_step")
        banks4 = core.banks[:, 4:8, :].rearrange("p k n -> p (k n)")
        banks0 = core.banks[:, 0:4, :].rearrange("p k n -> p (k n)")
        block = core.block(ctx)
        LOADS = 16

        @block.sync
        def _(sp):
            pairs = ((w_in[:], d["ss_in"]), (taps[:], d["ss_taps"][0:512, :].rearrange("(m p) k -> p m k", p=P)),
                     (taps_s[:], d["ss_taps"][512:544, :]), (theta[:], d["ss_theta"].rearrange("j p -> p j")),
                     (slopes[:, 0:1], d["ss_slopes"].unsqueeze(1)), (scale[:], d["ss_scale"].unsqueeze(1)), (dist[:], d["ss_dist"]),
                     (logits[:], d["ss_logits"].partition_broadcast(P)), (w_rep[:], d["ss_w"].rearrange("i p h -> p i h")),
                     (norm[:], d["ss_norm"].rearrange("i p -> p i")), (head[:], d["head_mask"]),
                     (spread[:], d["ss_spread"]), (gather[:], d["ss_gather"]), (eps_eye[:], d["ss_eps_eye"]),
                     (w_out[:], d["ss_out"].rearrange("(j p) c -> p j c", p=P)), (ones[:], d["ones"].partition_broadcast(P)))
            assert len(pairs) == LOADS
            for dst, src in pairs:
                with nc.allow_non_contiguous_dma("small constants"):
                    sp.dma_start(dst, src).then_inc(loads, 16)

        @block.tensor
        def _(pe):
            pe_transpose_tiles(core, pe, core.xn, (normed, 1), xt_full, (xt_copied, 0))
            pe.wait_ge(xt_copied, CHUNKS)
            pe.wait_ge(loads, LOADS * 16)
            for i, m in enumerate(ORDER):
                n = K if m == 4 else P
                for c in range(CHUNKS):
                    if i:
                        pe.wait_ge(raw_ready, (i - 1) * CHUNKS + c + 1)
                    nc.tensor.matmul(core.ps[c][0:n, :], w_in[:, m * P:m * P + n], core.xt[:, c * CHUNK:(c + 1) * CHUNK],
                                     start=True, stop=True).then_inc(raw_full, 1)
            pe.wait_ge(pw_ready, 1)
            for j in range(BLOCKS):
                if j:
                    pe.wait_ge(spread_used, 1)
                for c in range(CHUNKS):
                    ins = nc.tensor.matmul(core.ps[4 + c], spread[0:K, j, :], flat(score)[:, c * CHUNK:(c + 1) * CHUNK],
                                           start=True, stop=True)
                ins.then_inc(spread_full, 1)
            pe.wait_ge(raw_ready, len(ORDER) * CHUNKS)
            for j in range(BLOCKS):
                pe.wait_ge(squares_ready, j + 1)
                for c in range(CHUNKS):
                    out = core.ps[0][K * c:K * (c + 1), :]
                    for i, sq in enumerate((sin, cos)):
                        ins = nc.tensor.matmul(out, gather[:, j, :], sq[:, c * CHUNK:(c + 1) * CHUNK],
                                               start=(j == 0 and i == 0), stop=False, tile_position=(0, K * c),
                                               skip_group_check=True)
                    if j == BLOCKS - 1:
                        ins = nc.tensor.matmul(out, eps_eye[:], flat(den)[:, c * CHUNK:(c + 1) * CHUNK], start=False, stop=True,
                                               tile_position=(0, K * c), skip_group_check=True)
                ins.then_inc(squares_used, 1)
            pe.wait_ge(factor_ready, 1)
            pe.wait_ge(spread_used, 2)
            for j in range(BLOCKS):
                if j:
                    pe.wait_ge(mixed_read, 1)
                for c in range(CHUNKS):
                    nc.tensor.matmul(core.ps[4 + c], spread[K * c:K * (c + 1), j, :], factor[K * c:K * (c + 1), :], start=True, stop=True)
                    for i in range(2):
                        ins = nc.tensor.matmul(core.ps[c], w_diag[:, i, :], flat(num[j][i])[:, c * CHUNK:(c + 1) * CHUNK],
                                               start=(i == 0), stop=(i == 1))
                ins.then_inc(mixed_full, 1)
            pe.wait_ge(mixed_read, 2)
            for t in range(TILES):
                for j in range(BLOCKS):
                    ins = nc.tensor.matmul(core.ps[4 + t // 4][:, (t % 4) * P:(t % 4 + 1) * P], flat(gate[j])[:, t * P:(t + 1) * P],
                                           w_out[:, j, :], start=(j == 0), stop=(j == 1))
            ins.then_inc(out_full, 1)

        @block.scalar
        def _(act):
            act_rstd(core, act, stat, var_ready, rstd_ready, 1)
            step = Chain(act, act_step)
            act_copy_transposed(core, act, core.xt, xt_full, xt_copied)
            act.wait_ge(small_ready, 1)
            nc.scalar.activation(slopes[:, 2:3], slopes[:, 1:2], ACT.Exp)
            nc.scalar.activation(mix[:, 0:3], mix[:, 0:3], ACT.Exp).then_inc(small_exp, 1)
            act.wait_ge(small_ready, 2)
            nc.scalar.activation(slopes[:, 4:5], slopes[:, 3:4], ACT.Ln).then_inc(small_ln, 1)
            act.wait_ge(small_ready, 3)
            nc.scalar.activation(weight[:], dist[:], ACT.Exp, scale=slopes[:, 7:8]).then_inc(weights_ready, 1)
            for i, m in enumerate(ORDER):
                n = K if m == 4 else P
                if i >= 2:
                    act.wait_ge(conv_done, i - 1)
                for c in range(CHUNKS):
                    act.wait_ge(raw_full, i * CHUNKS + c + 1)
                    at = TAPS - 1 + (c % 2) * CHUNK
                    nc.scalar.copy(raw[i % 2][0:n, c // 2, at:at + CHUNK], core.ps[c][0:n, :]).then_inc(raw_ready, 1)
                if i == 0:
                    act.wait_ge(score_ready, 1)
                    nc.scalar.activation(flat(score), flat(score), ACT.Exp).then_inc(weights_ready, 1)
            for j in range(BLOCKS):
                act.wait_ge(angle_ready, j + 1)
                if j:
                    act.wait_ge(squares_used, 1)
                nc.scalar.activation(sin[:], angle, ACT.Sin)
                step(nc.scalar.activation(cos[:], angle, ACT.Sin, scale=0.5))
                nc.scalar.activation(cos[:], cos[:], ACT.Square).then_inc(waves_ready, 1)
                act.wait_ge(num_ready, j + 1)
                for i, sq in enumerate((sin, cos)):
                    ins = nc.scalar.activation(sq[:], flat(num[j][i]), ACT.Square)
                ins.then_inc(squares_ready, 1)
            act.wait_ge(power_inv, 1)
            nc.scalar.activation(factor[:], factor[:], ACT.Sqrt).then_inc(factor_ready, 1)
            for j in range(BLOCKS):
                act.wait_ge(conv_done, 4 + j)
                nc.scalar.activation(flat(gate[j]), flat(gate[j]), ACT.Silu).then_inc(gates_ready, 1)

        @block.vector
        def _(dve):
            v = nc.vector
            step = Chain(dve, dve_step)
            for i in range(2):
                step(v.memset(raw[i][:, :, 0:TAPS - 1], 0.0))
            step(dve_norm(core, step, core.x, core.xn, square, stat, 1e-5, var_ready, rstd_ready, 1))
            dve.sem_inc(normed, 1)
            dve.wait_ge(loads, LOADS * 16)
            step(v.tensor_scalar(slopes[:, 1:2], slopes[:, 0:1], -1.0, None, ALU.mult))
            step(v.tensor_tensor(slopes[:, 1:2], slopes[:, 1:2], slopes[:, 0:1], ALU.min))
            step(v.tensor_reduce(mix[:, 3:4], logits[:], AX.X, ALU.max))
            step(v.tensor_scalar(mix[:, 0:3], logits[:], mix[:, 3:4], None, ALU.subtract))
            dve.sem_inc(small_ready, 1)
            dve.wait_ge(small_exp, 1)
            step(v.tensor_reduce(mix[:, 3:4], mix[:, 0:3], AX.X, ALU.add))
            step(v.reciprocal(mix[:, 4:5], mix[:, 3:4]))
            step(v.tensor_scalar(mix[:, 0:3], mix[:, 0:3], mix[:, 4:5], None, ALU.mult))
            step(v.tensor_scalar(mix[:, 5:6], mix[:, 2:3], -1.0, None, ALU.mult))
            step(v.tensor_scalar(slopes[:, 3:4], slopes[:, 2:3], 1.0, None, ALU.add))
            dve.sem_inc(small_ready, 1)
            step(v.tensor_scalar(slopes[:, 5:6], slopes[:, 3:4], -1.0, None, ALU.add))
            step(v.tensor_scalar(slopes[:, 6:7], slopes[:, 5:6], 0.0, None, ALU.is_equal))
            step(v.tensor_tensor(slopes[:, 6:7], slopes[:, 6:7], slopes[:, 2:3], ALU.mult))
            step(v.tensor_scalar(slopes[:, 5:6], slopes[:, 5:6], 1e-20, None, ALU.max))
            step(v.reciprocal(slopes[:, 7:8], slopes[:, 5:6]))
            step(v.tensor_tensor(slopes[:, 7:8], slopes[:, 7:8], slopes[:, 2:3], ALU.mult))
            dve.wait_ge(small_ln, 1)
            step(v.tensor_tensor(slopes[:, 7:8], slopes[:, 7:8], slopes[:, 4:5], ALU.mult))
            step(v.tensor_tensor(slopes[:, 7:8], slopes[:, 7:8], slopes[:, 6:7], ALU.add))
            step(v.tensor_scalar(slopes[:, 5:6], slopes[:, 0:1], 0.0, None, ALU.max))
            step(v.tensor_tensor(slopes[:, 7:8], slopes[:, 7:8], slopes[:, 5:6], ALU.add))
            step(v.tensor_scalar(slopes[:, 7:8], slopes[:, 7:8], -1.0, None, ALU.mult))
            dve.sem_inc(small_ready, 1)
            for i in range(2):
                step(v.tensor_tensor(w_diag[:, i].rearrange("p (k h) -> p k h", h=H), head[:].unsqueeze(2).to_broadcast([P, 16, H]),
                                     w_rep[:, i].unsqueeze(1).to_broadcast([P, 16, H]), ALU.mult))
                step(v.tensor_scalar(w_diag[:, i], w_diag[:, i], norm[:, i:i + 1], None, ALU.mult))
            targets = {4: score, 0: value[0], 1: value[1], 2: gate[0], 3: gate[1]}

            def convolve(i):
                m = ORDER[i]
                out, tap = targets[m], (taps_s if m == 4 else taps[:, m])
                n = K if m == 4 else P
                dve.wait_ge(raw_ready, (i + 1) * CHUNKS)
                step(v.tensor_scalar(out[:], raw[i % 2][0:n, :, 0:SEQ], tap[:, 0:1], tap[:, TAPS:TAPS + 1], ALU.mult, ALU.add))
                for k in range(1, TAPS):
                    step(v.scalar_tensor_tensor(out=out[:], in0=raw[i % 2][0:n, :, k:k + SEQ], scalar=tap[:, k:k + 1], in1=out[:],
                                                op0=ALU.mult, op1=ALU.add))
                dve.sem_inc(conv_done, 1)

            convolve(0)
            step(v.tensor_scalar(score[:], score[:], scale[:], -20.0, ALU.mult, ALU.max))
            step(v.tensor_scalar(score[:], score[:], 20.0, None, ALU.min))
            dve.sem_inc(score_ready, 1)
            convolve(1)
            dve.wait_ge(weights_ready, 2)
            step(v.tensor_tensor(score[:], score[:], weight[:].unsqueeze(1).to_broadcast([K, BATCH, SEQ]), ALU.mult))
            dve.sem_inc(pw_ready, 1)
            for b in range(BATCH):
                step(v.tensor_tensor_scan(den[:, b], ones[0:K, :], score[:, b], 0.0, ALU.mult, ALU.add))
            step(v.tensor_scalar(den[:], den[:], 1e-4, None, ALU.max))
            step(v.tensor_tensor(den[:], den[:], den[:], ALU.mult))
            for j in range(BLOCKS):
                x = flat(value[j])
                step(v.tensor_scalar(angle, x, theta[:, j:j + 1], None, ALU.mult))
                step(v.tensor_scalar(poly[:], angle, 1.0 / (2 * np.pi), ROUND, ALU.mult, ALU.add))
                step(v.tensor_scalar(poly[:], poly[:], -ROUND, None, ALU.add))
                step(v.scalar_tensor_tensor(out=angle, in0=poly[:], scalar=-TURN_HI, in1=angle, op0=ALU.mult, op1=ALU.add))
                step(v.scalar_tensor_tensor(out=angle, in0=poly[:], scalar=-TURN_LO, in1=angle, op0=ALU.mult, op1=ALU.add))
                step(v.tensor_scalar(angle, angle, 3.1415925, -3.1415925, ALU.min, ALU.max))
                dve.sem_inc(angle_ready, 1)
                step(v.tensor_scalar(poly[:], x, mix[:, 5:6], mix[:, 1:2], ALU.mult, ALU.add))
                step(v.tensor_tensor(poly[:], poly[:], x, ALU.mult))
                step(v.tensor_scalar(poly[:], poly[:], mix[:, 0:1], None, ALU.add))
                dve.wait_ge(spread_full, j + 1)
                step(v.tensor_tensor(poly[:], poly[:], banks4, ALU.mult))
                dve.sem_inc(spread_used, 1)
                convolve(2 + j)
                dve.wait_ge(waves_ready, j + 1)
                step(v.tensor_scalar(cos[:], cos[:], -2.0, 1.0, ALU.mult, ALU.add))
                step(v.tensor_tensor(cos[:], cos[:], poly[:], ALU.mult))
                step(v.tensor_tensor(sin[:], sin[:], poly[:], ALU.mult))
                for i, wave in enumerate((cos, sin)):
                    for b in range(BATCH):
                        step(v.tensor_tensor_scan(num[j][i][:, b], ones[:], wave[:, b * SEQ:(b + 1) * SEQ], 0.0, ALU.mult, ALU.add))
                dve.sem_inc(num_ready, 1)
            convolve(4)
            dve.wait_ge(squares_used, 2)
            step(v.reciprocal(factor[:], core.ps[0]))
            dve.sem_inc(power_inv, 1)
            for j in range(BLOCKS):
                dve.wait_ge(gates_ready, j + 1)
                dve.wait_ge(mixed_full, j + 1)
                step(v.tensor_tensor(flat(gate[j]), flat(gate[j]), banks4, ALU.mult))
                step(v.tensor_tensor(flat(gate[j]), flat(gate[j]), banks0, ALU.mult))
                dve.sem_inc(mixed_read, 1)
            dve.wait_ge(out_full, 1)
            step(v.tensor_tensor(core.x[:], core.x[:], banks4.rearrange("p (t c) -> p t c", c=P), ALU.add))


def program(nc, dram):
    with ExitStack() as ctx:
        core = Core(nc, dram, ctx)
        load_stage(core)
        rwkv_stage(core)
        routed_ffn_stage(core, "f0_")
        linear_attention_stage(core)
        routed_ffn_stage(core, "f1_")
        attention_stage(core)
        expert_attention_stage(core, "g0_")
        ssm_stage(core)
        expert_attention_stage(core, "g1_")
        store_stage(core)


def kernel(**inputs):
    import numpy as _np
    import concourse.bacc as _bacc
    from concourse import mybir as _mybir
    from concourse.bass_utils import run_bass_kernel_spmd as _run

    nc = _bacc.Bacc("TRN2", target_bir_lowering=False, num_devices=1)
    arrays, dram = {}, {}

    def give(name, a):
        a = _np.ascontiguousarray(a)
        arrays[f"in_{name}"] = a
        dram[name] = nc.dram_tensor(f"in_{name}", a.shape, _mybir.dt.from_np(a.dtype), kind="ExternalInput").ap()

    give("x", inputs["L0_attn_a_x"])
    give("identity", _np.eye(P, dtype=_np.float32))
    for name in ("W_router", "W1", "b1", "Wo", "bo"):
        give(name, inputs["L0_ffn_" + name])
    give("gamma", inputs["L0_ffn_ln_gamma"])
    give("beta", inputs["L0_ffn_ln_beta"])
    def pair_swapped(a):
        return a.reshape((16, 2, 32) + a.shape[1:])[:, ::-1].reshape(a.shape)

    wq, wk, wv = (_np.asarray(inputs["L1_attn_a_W" + n]) for n in "qkv")
    bq, bk = (_np.asarray(inputs["L1_attn_a_b" + n]) for n in "qk")
    give("at_w", _np.stack([a.T for a in (wq, pair_swapped(wq), wk, pair_swapped(wk), wv)]))
    give("at_bias", _np.stack([a.reshape(8, P) for a in (bq, pair_swapped(bq), bk, pair_swapped(bk))]))
    give("at_bv", inputs["L1_attn_a_bv"])
    give("at_wo", _np.asarray(inputs["L1_attn_a_Wo"]).T)
    give("at_bo", inputs["L1_attn_a_bo"])
    freq = (1.0 / _np.float32(10000.0) ** (_np.arange(0, 64, 2, dtype=_np.float32) / _np.float32(64))).astype(_np.float32)
    angle = (freq[:, None] * _np.arange(SEQ, dtype=_np.float32)[None, :]).astype(_np.float32)
    cos = _np.tile(_np.cos(angle), (4, 1)).astype(_np.float32)
    sin = _np.concatenate([-_np.sin(angle), _np.sin(angle)] * 2).astype(_np.float32)
    give("rope", _np.stack([cos / 8, sin / 8, cos, sin]).astype(_np.float32))


    wkv = _np.asarray(inputs["L1_ffn_Wkv"])
    half = wkv.shape[1] // 2
    give("ex_w", _np.stack([_np.asarray(inputs["L1_ffn_Wq"]), wkv[:, :half], wkv[:, half:]]))
    give("ex_gate", _np.concatenate([_np.asarray(inputs["L1_ffn_Ws"]), _np.asarray(inputs["L1_ffn_Wd"])], axis=1))
    give("ex_wo", _np.asarray(inputs["L1_ffn_Wo"]).reshape(64, 5, P).transpose(1, 0, 2).reshape(320, P))
    for name in ("wq", "wk", "wv", "wo"):
        give("la_" + name, _np.asarray(inputs["L0_attn_b_" + name]).reshape(P, P))
    for name in ("w1", "b1", "w2", "b2"):
        give("la_" + name, inputs["L0_attn_b_" + name])
    give("la_gamma", inputs["L0_attn_b_gamma1"])
    give("la_beta", inputs["L0_attn_b_beta1"])
    give("head_mask", (_np.arange(P)[:, None] // 8 == _np.arange(16)[None, :]).astype(_np.float32))
    ssm = lambda name: _np.asarray(inputs["L1_attn_b_" + name])
    give("ss_in", ssm("in_proj_w"))
    give("ss_taps", _np.concatenate([ssm("conv_k").reshape(4, -1).T, ssm("conv_b").reshape(-1, 1)], axis=1))
    give("ss_theta", ssm("theta").reshape(2, P))
    give("ss_slopes", _np.concatenate([ssm("decay_slopes"), ssm("anchor_slopes")]))
    give("ss_scale", ssm("score_scale"))
    at = _np.arange(SEQ, dtype=_np.float32)
    give("ss_dist", _np.stack([SEQ - 1 - at] * 28 + [at] * 4))
    give("ss_logits", ssm("deriv_logits"))
    give("ss_w", _np.stack([_np.tile(ssm("W_re"), (16, 1)), _np.tile(ssm("W_im"), (16, 1))]))
    give("ss_norm", _np.stack([_np.tile(ssm("norm_scale")[:8], 16), _np.tile(ssm("norm_scale")[8:], 16)]))
    group = _np.arange(P) // 8
    spread = (_np.arange(32)[:, None, None] == 16 * _np.arange(2)[None, :, None] + group[None, None, :]).astype(_np.float32)
    give("ss_spread", _np.tile(spread, (4, 1, 1)))
    give("ss_gather", spread.transpose(2, 1, 0) / _np.float32(16))
    give("ss_eps_eye", _np.eye(32, dtype=_np.float32) * _np.float32(1e-5))
    give("ss_out", ssm("out_proj_w"))
    give("ones", _np.ones(SEQ, _np.float32))
    rw = lambda name: _np.asarray(inputs["L0_attn_a_" + name])
    give("rw_w", _np.stack([rw("W_" + n).T for n in "rwkvabgo"]))
    give("rw_mix", _np.stack([rw("x_" + n) for n in "rwkvabg"], axis=1))
    give("rw_bo", rw("b_o"))
    give("rw_gn", _np.stack([rw("gn_w"), rw("gn_b")], axis=1))
    same = (group[:, None] == group[None, :]).astype(_np.float32)
    give("rw_same", same)
    channel = (_np.arange(P)[None, None, :] % 8 == _np.arange(8)[None, :, None]).astype(_np.float32)
    pick = same[:, None, :] * channel
    give("rw_pick", pick)
    give("rw_give", pick.transpose(2, 1, 0))
    pool2 = (group[:, None, None] + 16 * _np.arange(2)[None, :, None] == _np.arange(32)[None, None, :]).astype(_np.float32)
    give("rw_pool2", pool2)
    give("rw_spread2", _np.tile(pool2.transpose(2, 1, 0), (4, 1, 1)))
    give("rw_eye", _np.tile(_np.eye(8, dtype=_np.float32), (16, 1)))
    dram["out"] = nc.dram_tensor("out", (BATCH, SEQ, P), _mybir.dt.float32, kind="ExternalOutput").ap()
    program(nc, dram)
    return _run(nc, [arrays], core_ids=[0]).results[0]["out"]
```

```python
from contextlib import ExitStack, contextmanager

import concourse.bass as bass
import numpy as np
from concourse import mybir

F32 = mybir.dt.float32
BF16 = mybir.dt.bfloat16
ALU = mybir.AluOpType
ACT = mybir.ActivationFunctionType
AX = mybir.AxisListType

P = 128
BATCH = 2
SEQ = 1024
TOKENS = BATCH * SEQ
TILES = TOKENS // P
CHUNK = 512
CHUNKS = TOKENS // CHUNK


class Chain:

    def __init__(self, eng, sem):
        self.eng, self.sem, self.n, self.at = eng, sem, 0, 0

    def __call__(self, ins):
        self.n += 1
        ins.then_inc(self.sem, 1)
        self.eng.wait_ge(self.sem, self.at + self.n)

    @contextmanager
    def loop(self, rounds, steps):
        before = self.n
        with self.eng.Fori(0, rounds) as i:
            self.at = i * steps
            yield i
        assert self.n == before + steps, (self.n - before, steps)
        self.n = before + rounds * steps
        self.at = 0


class Core:

    def __init__(self, nc, dram, ctx):
        self.nc, self.dram = nc, dram
        self.in_use = []
        sb = lambda name, shape, dt=F32: ctx.enter_context(nc.sbuf_tensor(name, shape, dt))
        self.x = sb("residual", [P, TILES, P])
        self.xn = sb("normed", [P, TILES, P])
        self.xt = sb("normed_t", [P, TOKENS])
        self.ident = sb("identity", [P, P])
        self.banks = ctx.enter_context(nc.psum_tensor("banks", [P, 8, CHUNK], F32))
        self.ps = [self.banks[:, i, :] for i in range(8)]

    def semaphore(self, ctx, name):
        handle = ctx.enter_context(self.nc.semaphore(name))
        self.in_use.append(handle)
        return handle

    def block(self, ctx):
        ctx.callback(self.clear)
        return ctx.enter_context(self.nc.Block())

    def clear(self):
        for handle in self.in_use:
            self.nc.gpsimd.sem_clear(handle)
        self.in_use = []
        self.nc.all_engine_barrier()

    def row(self, ap, tiles=TILES):
        return ap.unsqueeze(1).to_broadcast([P, tiles, ap.shape[-1]])

    def col(self, ap, n=P):
        return ap.unsqueeze(2).to_broadcast([P, ap.shape[1], n])


def dve_norm(core, step, src, dst, square, stat, eps, var_ready, rstd_ready, turn):
    v = core.nc.vector
    step(v.tensor_reduce(stat[:, 0], src[:], AX.X, ALU.add))
    step(v.tensor_scalar(stat[:, 0], stat[:, 0], 1.0 / P, None, ALU.mult))
    step(v.tensor_tensor(dst[:], src[:], core.col(stat[:, 0]), ALU.subtract))
    step(v.tensor_tensor(square[:], dst[:], dst[:], ALU.mult))
    step(v.tensor_reduce(stat[:, 1], square[:], AX.X, ALU.add))
    step(v.tensor_scalar(stat[:, 1], stat[:, 1], 1.0 / P, eps, ALU.mult, ALU.add))
    v.reciprocal(stat[:, 2], stat[:, 1]).then_inc(var_ready, 1)
    step.eng.wait_ge(rstd_ready, turn)
    return v.tensor_tensor(dst[:], dst[:], core.col(stat[:, 3]), ALU.mult)


def act_rstd(core, act, stat, var_ready, rstd_ready, turn):
    act.wait_ge(var_ready, turn)
    core.nc.scalar.activation(stat[:, 3], stat[:, 2], ACT.Sqrt).then_inc(rstd_ready, 1)


def pe_transpose_tiles(core, pe, src, ready, full, empty):
    pe.wait_ge(*ready)
    for g in range(CHUNKS):
        if g >= 2:
            pe.wait_ge(empty[0], empty[1] + g - 1)
        for t in range(4):
            ins = core.nc.tensor.transpose(core.ps[g % 2][:, t * P:(t + 1) * P], src[:, 4 * g + t, :],
                                           core.ident[:])
        ins.then_inc(full, 1)


def act_copy_transposed(core, act, dst, full, empty, turn=0):
    for g in range(CHUNKS):
        act.wait_ge(full, turn + g + 1)
        core.nc.scalar.copy(dst[:, g * CHUNK:(g + 1) * CHUNK], core.ps[g % 2][:]).then_inc(empty, 1)


def load_stage(core):
    nc = core.nc
    with ExitStack() as ctx:
        loaded = core.semaphore(ctx, "residual_in")
        block = core.block(ctx)

        @block.sync
        def _(sp):
            sp.dma_start(core.x[:], core.dram["x"].rearrange("b (t p) c -> p (b t) c", p=P)).then_inc(loaded, 16)
            sp.dma_start(core.ident[:], core.dram["identity"]).then_inc(loaded, 16)
            sp.wait_ge(loaded, 32)


def store_stage(core):
    nc = core.nc
    with nc.semaphore("result_out") as stored, nc.Block() as block:
        @block.sync
        def _(sp):
            sp.dma_start(core.dram["out"].rearrange("b (t p) c -> p (b t) c", p=P), core.x[:]).then_inc(stored, 16)
            sp.wait_ge(stored, 16)


def rwkv_stage(core):
    nc, d = core.nc, core.dram
    H, K = 16, 8
    STEPS = 64
    PER = SEQ // STEPS
    COLS = BATCH * PER
    ROWS = 2 * K
    BLOCK = 8
    PAD = STEPS + BLOCK
    SCAN = ("w", "k", "v", "a", "b", "r")
    ORDER = ("r", "w", "k", "v", "a", "b", "g")
    tag = "rw_"
    with ExitStack() as ctx:
        sb = lambda name, shape, dt=F32: ctx.enter_context(nc.sbuf_tensor(tag + name, shape, dt))
        sem = lambda name: core.semaphore(ctx, tag + name)
        weights = sb("weights", [P, 8, P])
        mix = sb("mix", [P, 7])
        bo, gn = sb("bo", [P, P]), sb("gn", [P, 2])
        head = sb("head", [P, H])
        same = sb("same", [P, P])
        pick = sb("pick", [P, K, P])
        give = sb("give", [P, K, P])
        pool2 = sb("pool2", [P, 2, 2 * H])
        spread2 = sb("spread2", [P, 2, P])
        eye = sb("eye", [P, K])
        seq = {n: sb(n, [P, COLS, PAD]) for n in SCAN}
        g_t = sb("g_t", [P, TOKENS])
        state = sb("state", [P, 2, COLS, ROWS])
        yr = sb("yr", [P, 2, BLOCK, COLS, ROWS])
        kv = sb("kv", [P, 2, K, COLS * BLOCK])
        ya, ub, x1 = sb("ya", [P, 2, PER, ROWS]), sb("ub", [P, 2, PER, ROWS]), sb("x1", [P, 2, PER, ROWS])
        o, yc = sb("o", [P, COLS, PAD]), sb("yc", [P, COLS, PAD])
        borders = sb("borders", [P, COLS, K])
        stat = sb("stat", [P, 4, TILES])
        inv = sb("inv", [P, CHUNK])
        flat_yr = yr[:].rearrange("p i s c r -> p (i s c r)")
        square = flat_yr[:, 0:2048].rearrange("p (t c) -> p t c", c=P)
        diff, mixed = flat_yr[:, 2048:4096], [flat_yr[:, 4096:6144], flat_yr[:, 6144:8192]]
        wide = flat_yr[:, 0:4096].rearrange("p (n c) -> p n c", c=P)
        tight = flat_yr[:, 4096:8192].rearrange("p (n c) -> p n c", c=P)

        loads = sem("loads")
        var_ready, rstd_ready, normed = sem("var_ready"), sem("rstd_ready"), sem("normed")
        xt_full, xt_copied = sem("xt_full"), sem("xt_copied")
        mixed_ready, proj_full, proj_ready = sem("mixed_ready"), sem("proj_full"), sem("proj_ready")
        sq_ready, sq_full, len_ready, inv_ready, inv_full, unit_ready = (sem(n) for n in (
            "sq_ready", "sq_full", "len_ready", "inv_ready", "inv_full", "unit_ready"))
        y_ready, u_full, x1_ready, x_ready = sem("y_ready"), sem("u_full"), sem("x1_ready"), sem("x_ready")
        yr_ready, v_full, kv_ready, o_full, o_copied = (sem(n) for n in ("yr_ready", "v_full", "kv_ready", "o_full", "o_copied"))
        wide_ready, wide_full, wide_copied, border_full, border_ready = (sem(n) for n in (
            "wide_ready", "wide_full", "wide_copied", "border_full", "border_ready"))
        fix_ready, fix_full = sem("fix_ready"), sem("fix_full")
        gn_in, gn_full = sem("gn_in"), sem("gn_full")
        res_ready, res_full = sem("res_ready"), sem("res_full")
        dve_step, pool_step = sem("dve_step"), sem("pool_step")
        LOADS = 13
        banks0 = core.banks[:, 0:4, :].rearrange("p k n -> p (k n)")
        banks4 = core.banks[:, 4:8, :].rearrange("p k n -> p (k n)")
        cols = lambda t, off: t[:, :, off:off + STEPS]
        block = core.block(ctx)

        @block.sync
        def _(sp):
            pairs = ((weights[:], d["rw_w"].rearrange("k c n -> c k n")), (mix[:], d["rw_mix"]), (bo[:], d["rw_bo"].partition_broadcast(P)),
                     (gn[:], d["rw_gn"]), (head[:], d["head_mask"]), (same[:], d["rw_same"]), (pick[:], d["rw_pick"]),
                     (give[:], d["rw_give"]), (pool2[:], d["rw_pool2"]), (spread2[:], d["rw_spread2"]), (eye[:], d["rw_eye"]))
            for dst, src in pairs:
                sp.dma_start(dst, src).then_inc(loads, 16)

        @block.tensor
        def _(pe):
            mm = nc.tensor.matmul
            pe_transpose_tiles(core, pe, core.xn, (normed, 1), xt_full, (xt_copied, 0))
            pe.wait_ge(loads, 11 * 16)
            pe.wait_ge(xt_copied, CHUNKS)
            for i in range(7):
                pe.wait_ge(mixed_ready, i + 1)
                for c in range(CHUNKS):
                    if i >= 2:
                        pe.wait_ge(proj_ready, (i - 2) * CHUNKS + c + 1)
                    mm(core.ps[4 * (i % 2) + c], weights[:, i, :], mixed[i % 2][:, c * CHUNK:(c + 1) * CHUNK], start=True,
                       stop=True).then_inc(proj_full, 1)
            pe.wait_ge(proj_ready, 7 * CHUNKS)
            for i, n in enumerate("ab"):
                pe.wait_ge(sq_ready, i + 1)
                for c in range(CHUNKS):
                    ins = mm(core.ps[0][32 * c:32 * c + 32, :], pool2[:, i, :], mixed[i][:, c * CHUNK:(c + 1) * CHUNK],
                             start=(i == 0), stop=(i == 1), tile_position=(0, 32 * c), skip_group_check=True)
            ins.then_inc(sq_full, 1)
            pe.wait_ge(inv_ready, 1)
            for i in range(2):
                if i:
                    pe.wait_ge(unit_ready, 1)
                for c in range(CHUNKS):
                    ins = mm(core.ps[4 + c], spread2[32 * c:32 * c + 32, i, :], inv[32 * c:32 * c + 32, :], start=True, stop=True)
                ins.then_inc(inv_full, 1)
            pe.wait_ge(unit_ready, 2)

            def spread_v(q, s):
                r = s // 2
                ins = mm(core.ps[2 + r % 2][:, (s % 2) * 256:(s % 2 + 1) * 256], give[:, s, :], seq["v"][:, :, bass.ds(q * BLOCK, BLOCK)],
                         start=True, stop=True)
                if s % 2:
                    ins.then_inc(v_full, 1)

            def output(i, row):
                ins = mm(core.ps[4 + row // K][:, 0:256], pick[:, row % K, :], yr[:, i, :, :, row].rearrange("p s c -> p c s"),
                         start=(row % K == 0), stop=(row % K == K - 1))
                if row % K == K - 1:
                    ins.then_inc(o_full, 1)

            for s in range(K):
                if s in (4, 6):
                    pe.wait_ge(kv_ready, s // 2 - 1)
                spread_v(0, s)
            pe.sem_inc(o_full, 4)
            with pe.Fori(0, STEPS // BLOCK // 2) as qq:
                for i in range(2):
                    q = qq * 2 + i
                    todo = list(range(ROWS))
                    for s in range(BLOCK):
                        n = q * BLOCK + s
                        for b in range(BATCH):
                            pe.wait_ge(y_ready, n * 2 + b + 1)
                            mm(core.ps[b][:, 0:256], same[:], ya[:, b].rearrange("p c r -> p (c r)"), start=True, stop=True).then_inc(u_full, 1)
                            if b == 0:
                                if s % 2 == 0:
                                    pe.wait_ge(kv_ready, q * 4 + s // 2 + 3)
                                spread_v(q + 1, s)
                            elif s:
                                if s == 1:
                                    pe.wait_ge(yr_ready, q * BLOCK + 1)
                                    pe.wait_ge(o_copied, q * 2 + 2)
                                for row in todo[:3 if s <= 2 else 2]:
                                    output(1 - i, row)
                                    todo.remove(row)
            pe.wait_ge(yr_ready, STEPS + 1)
            pe.wait_ge(o_copied, STEPS // BLOCK * 2 + 2)
            for row in range(ROWS):
                output(1, row)
            pe.wait_ge(wide_ready, 1)
            for m in range(COLS // 4):
                if m >= 2:
                    pe.wait_ge(wide_copied, m - 1)
                for t in range(4):
                    ins = nc.tensor.transpose(core.ps[m % 2][:, t * P:(t + 1) * P], wide[:, 4 * m + t, :], core.ident[:])
                ins.then_inc(wide_full, 1)
            pe.wait_ge(wide_copied, COLS // 4)
            for c in range(PER - 1):
                pe.wait_ge(border_ready, c + 1)
                for b in range(BATCH):
                    ins = mm(core.ps[2 + c % 2][:, b * K:(b + 1) * K], tight[:, b * PER + c, :], borders[:, b * PER + c, :],
                             start=True, stop=True)
                ins.then_inc(border_full, 1)
            pe.wait_ge(fix_ready, 1)
            pe.wait_ge(o_copied, STEPS // BLOCK * 2 + 4)
            for c in range(COLS):
                ins = mm(core.ps[4 + c // 8][:, (c % 8) * STEPS:(c % 8 + 1) * STEPS], wide[:, c, :], yc[:, c, BLOCK:BLOCK + STEPS],
                         start=True, stop=True)
            ins.then_inc(fix_full, 1)
            pe.wait_ge(gn_in, 1)
            for c in range(CHUNKS):
                ins = mm(core.ps[c], same[:], mixed[0][:, c * CHUNK:(c + 1) * CHUNK], start=True, stop=True)
            ins.then_inc(gn_full, 1)
            pe.wait_ge(gn_in, 2)
            for c in range(CHUNKS):
                ins = mm(core.ps[0][32 * c:32 * c + 32, :], pool2[:, 0, :], mixed[1][:, c * CHUNK:(c + 1) * CHUNK],
                         start=True, stop=True, tile_position=(0, 32 * c), skip_group_check=True)
            ins.then_inc(gn_full, 1)
            pe.wait_ge(inv_ready, 2)
            for c in range(CHUNKS):
                ins = mm(core.ps[4 + c], spread2[32 * c:32 * c + 32, 0, :], inv[32 * c:32 * c + 32, :], start=True, stop=True)
            ins.then_inc(gn_full, 1)
            pe.wait_ge(res_ready, 1)
            for t in range(TILES):
                ins = mm(core.ps[t // 4][:, (t % 4) * P:(t % 4 + 1) * P], mixed[0][:, t * P:(t + 1) * P], weights[:, 7, :],
                         start=True, stop=True)
            ins.then_inc(res_full, 1)

        @block.scalar
        def _(act):
            act_rstd(core, act, stat, var_ready, rstd_ready, 1)
            act_copy_transposed(core, act, core.xt, xt_full, xt_copied)
            func = {"w": (ACT.Sigmoid, -1.0), "k": (ACT.Tanh, 1.0), "g": (ACT.Sigmoid, 1.0)}
            for i, n in enumerate(ORDER):
                for c in range(CHUNKS):
                    act.wait_ge(proj_full, i * CHUNKS + c + 1)
                    src = core.ps[4 * (i % 2) + c]
                    if n == "g":
                        dst = g_t[:, c * CHUNK:(c + 1) * CHUNK]
                    else:
                        off = 1 if n == "r" else 0
                        dst = seq[n][:, 8 * c:8 * c + 8, off:off + STEPS]
                        src = src.rearrange("p (c s) -> p c s", s=STEPS)
                    f, scale = func.get(n, (ACT.Copy, 1.0))
                    nc.scalar.activation(dst, src, f, scale=scale).then_inc(proj_ready, 1)
            act.wait_ge(sq_full, 1)
            nc.scalar.activation(inv[:], core.ps[0], ACT.Sqrt).then_inc(len_ready, 1)
            act.sem_inc(o_copied, 2)

            def copy_outputs(q):
                for i, dst in enumerate((o, yc)):
                    act.wait_ge(o_full, q * 2 + i + 5)
                    nc.scalar.copy(dst[:, :, bass.ds(q * BLOCK, BLOCK)], core.ps[4 + i][:, 0:256].rearrange("p (c s) -> p c s", s=BLOCK)).then_inc(o_copied, 1)

            with act.Fori(0, STEPS // BLOCK) as q:
                copy_outputs(q)
            copy_outputs(STEPS // BLOCK)
            for m in range(COLS // 4):
                act.wait_ge(wide_full, m + 1)
                nc.scalar.copy(tight[:, 4 * m:4 * m + 4, :], core.ps[m % 2].rearrange("p (t c) -> p t c", c=P)).then_inc(wide_copied, 1)
            act.wait_ge(len_ready, 2)
            nc.scalar.activation(inv[:], inv[:], ACT.Sqrt).then_inc(inv_ready, 1)

        @block.gpsimd
        def _(pool):
            g = nc.gpsimd
            pool.wait_ge(inv_ready, 1)
            step = Chain(pool, pool_step)
            with step.loop(STEPS // BLOCK // 2, 2 * BLOCK * 2) as qq:
                for i in range(2):
                    q = qq * 2 + i
                    pool.wait_ge(kv_ready, q * 4 + 4)
                    for s in range(BLOCK):
                        n = q * BLOCK + s
                        before = state[:, 1 - s % 2]
                        for b in range(BATCH):
                            mine = slice(b * PER, (b + 1) * PER)
                            pool.wait_ge(x_ready, n * 2 + b + 1)
                            step(g.tensor_tensor(x1[:, b], before[:, mine], seq["w"][:, mine, bass.ds(n, 1)].to_broadcast([P, PER, ROWS]), ALU.mult))
                            g.tensor_tensor(x1[:, b, :, 0:K], x1[:, b, :, 0:K],
                                            kv[:, i].rearrange("p v (c s) -> p c v s", s=BLOCK)[:, mine, :, s], ALU.add).then_inc(x1_ready, 1)
                        if s == 1:
                            pool.wait_ge(o_full, q * 2 + 2)
                        j, slot = (i, s - 1) if s else (1 - i, BLOCK - 1)
                        g.tensor_tensor(yr[:, j, slot], before, seq["r"][:, :, bass.ds(n, 1)].to_broadcast([P, COLS, ROWS]),
                                        ALU.mult).then_inc(yr_ready, 1)
            pool.wait_ge(x_ready, STEPS * 2 + 2)
            g.tensor_tensor(yr[:, 1, BLOCK - 1], state[:, 1], seq["r"][:, :, STEPS:STEPS + 1].to_broadcast([P, COLS, ROWS]),
                            ALU.mult).then_inc(yr_ready, 1)

        @block.vector
        def _(dve):
            v = nc.vector
            step = Chain(dve, dve_step)
            step(dve_norm(core, step, core.x, core.xn, square, stat, 1e-5, var_ready, rstd_ready, 1))
            dve.sem_inc(normed, 1)
            dve.wait_ge(xt_copied, CHUNKS)
            dve.wait_ge(loads, 11 * 16)
            x_t = core.xt[:].rearrange("p (b s) -> p b s", b=BATCH)
            df = diff.rearrange("p (b s) -> p b s", b=BATCH)
            step(v.tensor_tensor(df[:, :, 1:SEQ], x_t[:, :, 0:SEQ - 1], x_t[:, :, 1:SEQ], ALU.subtract))
            step(v.tensor_scalar(df[:, :, 0:1], x_t[:, :, 0:1], -1.0, None, ALU.mult))
            for i in range(7):
                if i >= 2:
                    dve.wait_ge(proj_full, (i - 1) * CHUNKS)
                v.scalar_tensor_tensor(out=mixed[i % 2], in0=diff, scalar=mix[:, i:i + 1], in1=core.xt[:], op0=ALU.mult,
                                       op1=ALU.add).then_inc(mixed_ready, 1)
            for n in ("k", "v", "a"):
                step(v.memset(seq[n][:, :, STEPS:PAD], 0.0))
            step(v.memset(seq["r"][:, :, 0:1], 0.0))
            step(v.memset(state[:, 1, :, 0:K], 0.0))
            step(v.tensor_copy(state[:, 1, :, K:ROWS], eye[:].unsqueeze(1).to_broadcast([P, COLS, K])))
            dve.wait_ge(proj_ready, 7 * CHUNKS)
            for i, n in enumerate("ab"):
                step(v.tensor_tensor(mixed[i].rearrange("p (c s) -> p c s", s=STEPS), cols(seq[n], 0), cols(seq[n], 0), ALU.mult))
                dve.sem_inc(sq_ready, 1)
            dve.wait_ge(len_ready, 1)
            step(v.tensor_scalar(inv[:], inv[:], 1e-6, None, ALU.max))
            step(v.reciprocal(inv[:], inv[:]))
            dve.sem_inc(inv_ready, 1)
            for i, n in enumerate("ab"):
                dve.wait_ge(inv_full, i + 1)
                step(v.tensor_tensor(cols(seq[n], 0), cols(seq[n], 0), banks4.rearrange("p (c s) -> p c s", s=STEPS), ALU.mult))
                dve.sem_inc(unit_ready, 1)
            step(v.memset(yr[:, 1], 0.0))

            def key_values(q, r, i):
                v.tensor_tensor(kv[:, i, 2 * r:2 * r + 2].rearrange("p v (c s) -> p v c s", s=BLOCK),
                                core.ps[2 + r % 2].rearrange("p (v c s) -> p v c s", v=2, s=BLOCK),
                                seq["k"][:, :, bass.ds(q * BLOCK, BLOCK)].unsqueeze(1).to_broadcast([P, 2, COLS, BLOCK]),
                                ALU.mult).then_inc(kv_ready, 1)

            def times_a(n, b, src):
                mine = slice(b * PER, (b + 1) * PER)
                v.tensor_tensor(ya[:, b], src[:, mine], seq["a"][:, mine, bass.ds(n, 1)].to_broadcast([P, PER, ROWS]),
                                ALU.mult).then_inc(y_ready, 1)

            for r in range(4):
                dve.wait_ge(v_full, r + 1)
                key_values(0, r, 0)
            for b in range(BATCH):
                times_a(0, b, state[:, 1])
            dve.sem_inc(x_ready, 2)
            with step.loop(STEPS // BLOCK // 2, 2 * BLOCK * 2) as qq:
                for i in range(2):
                    q = qq * 2 + i
                    for s in range(BLOCK):
                        n = q * BLOCK + s
                        for b in range(BATCH):
                            mine = slice(b * PER, (b + 1) * PER)
                            dve.wait_ge(u_full, n * 2 + b + 1)
                            step(v.tensor_tensor(ub[:, b], core.ps[b][:, 0:256].rearrange("p (c r) -> p c r", r=ROWS),
                                                 seq["b"][:, mine, bass.ds(n, 1)].to_broadcast([P, PER, ROWS]), ALU.mult))
                            dve.wait_ge(x1_ready, n * 2 + b + 1)
                            v.tensor_tensor(state[:, s % 2, mine], ub[:, b], x1[:, b], ALU.add).then_inc(x_ready, 1)
                            dve.wait_ge(x_ready, n * 2 + b + 3)
                            times_a(n + 1, b, state[:, s % 2])
                        if s % 2:
                            dve.wait_ge(v_full, q * 4 + s // 2 + 5)
                            key_values(q + 1, s // 2, 1 - i)
            last = state[:, 1]
            dve.wait_ge(o_full, STEPS // BLOCK * 2 + 6)
            step(v.tensor_tensor(wide.rearrange("p n (h k) -> p n h k", k=K), last[:, :, K:ROWS].unsqueeze(2).to_broadcast([P, COLS, H, K]),
                                 head[:].unsqueeze(1).unsqueeze(3).to_broadcast([P, COLS, H, K]), ALU.mult))
            dve.sem_inc(wide_ready, 1)
            border = borders[:].rearrange("p (b c) k -> p b c k", b=BATCH)
            own = last.rearrange("p (b c) r -> p b c r", b=BATCH)
            step(v.memset(border[:, :, 0], 0.0))
            dve.sem_inc(border_ready, 1)
            for c in range(PER - 1):
                dve.wait_ge(border_full, c + 1)
                v.tensor_tensor(border[:, :, c + 1], core.ps[2 + c % 2][:, 0:BATCH * K].rearrange("p (b k) -> p b k", b=BATCH),
                                own[:, :, c, 0:K], ALU.add).then_inc(border_ready, 1)
            dve.wait_ge(border_ready, PER)
            step(v.tensor_tensor(wide.rearrange("p n (h k) -> p n h k", k=K), borders[:].unsqueeze(2).to_broadcast([P, COLS, H, K]),
                                 head[:].unsqueeze(1).unsqueeze(3).to_broadcast([P, COLS, H, K]), ALU.mult))
            dve.sem_inc(fix_ready, 1)
            dve.wait_ge(fix_full, 1)
            out, dev = mixed
            step(v.tensor_tensor(out.rearrange("p (c s) -> p c s", s=STEPS), cols(o, BLOCK), banks4.rearrange("p (c s) -> p c s", s=STEPS), ALU.add))
            dve.sem_inc(gn_in, 1)
            dve.wait_ge(gn_full, 1)
            step(v.scalar_tensor_tensor(out=out, in0=banks0, scalar=-1.0 / K, in1=out, op0=ALU.mult, op1=ALU.add))
            step(v.tensor_tensor(dev, out, out, ALU.mult))
            dve.sem_inc(gn_in, 1)
            dve.wait_ge(gn_full, 2)
            step(v.tensor_scalar(inv[:], core.ps[0], 1.0 / K, 0.00064, ALU.mult, ALU.add))
            step(v.reciprocal(inv[:], inv[:]))
            dve.sem_inc(len_ready, 1)
            dve.wait_ge(gn_full, 3)
            step(v.tensor_tensor(out, out, banks4, ALU.mult))
            step(v.tensor_scalar(out, out, gn[:, 0:1], gn[:, 1:2], ALU.mult, ALU.add))
            step(v.tensor_tensor(out, out, g_t[:], ALU.mult))
            dve.sem_inc(res_ready, 1)
            step(v.tensor_tensor(core.x[:], core.x[:], core.row(bo[:]), ALU.add))
            dve.wait_ge(res_full, 1)
            step(v.tensor_tensor(core.x[:], core.x[:], banks0.rearrange("p (t c) -> p t c", c=P), ALU.add))


def routed_ffn_stage(core, tag):
    nc, d = core.nc, core.dram
    E, I = 4, 512
    IB = I // P
    with ExitStack() as ctx:
        sb = lambda name, shape, dt=F32: ctx.enter_context(nc.sbuf_tensor(tag + name, shape, dt))
        sem = lambda name: core.semaphore(ctx, tag + name)
        w_router = sb("w_router", [P, E])
        w1 = sb("w1", [P, E, I])
        b1 = sb("b1", [E, I])
        wo = sb("wo", [P, IB, P])
        bo, gamma, beta = sb("bo", [P, P]), sb("gamma", [P, P]), sb("beta", [P, P])
        square = sb("square", [P, TILES, P])
        stat = sb("stat", [P, 4, TILES])
        best, left = sb("best", [P, TILES]), sb("left", [P, TILES])
        hot = sb("hot", [P, TILES, E])
        hot_t = sb("hot_t", [E, TOKENS])
        xe = [sb(f"xe{e}", [P, TILES, P]) for e in range(E)]
        xe_t = sb("xe_t", [P, E, TOKENS])
        hidden = sb("hidden", [P, IB, CHUNK])
        y = sb("y", [P, TILES, P])

        loads = sem("loads")
        var_ready, rstd_ready, normed = sem("var_ready"), sem("rstd_ready"), sem("normed")
        xt_full, xt_copied = sem("xt_full"), sem("xt_copied")
        logits_full, hot_ready, hot_full, hot_copied = sem("logits_full"), sem("hot_ready"), sem("hot_full"), sem("hot_copied")
        xe_ready = [sem(f"xe_ready{e}") for e in range(E)]
        h_full, h_free, hidden_free = sem("h_full"), sem("h_free"), sem("hidden_free")
        y_full, y_free = sem("y_full"), sem("y_free")
        dve_step, act_step = sem("dve_step"), sem("act_step")
        logits, hot_ps, y_ps = core.ps[2], core.ps[3], core.ps[4]

        block = core.block(ctx)

        @block.sync
        def _(sp):
            for dst, src in ((w_router[:], d["W_router"]), (w1[:], d["W1"].rearrange("e c i -> c e i")), (b1[:], d["b1"]),
                             (wo[:], d["Wo"].rearrange("(j p) c -> p j c", p=P)), (bo[:], d["bo"].partition_broadcast(P)),
                             (gamma[:], d["gamma"].partition_broadcast(P)), (beta[:], d["beta"].partition_broadcast(P))):
                sp.dma_start(dst, src).then_inc(loads, 16)

        @block.tensor
        def _(pe):
            pe_transpose_tiles(core, pe, core.xn, (normed, 1), xt_full, (xt_copied, 0))
            pe.wait_ge(loads, 7 * 16)
            pe.wait_ge(xt_copied, CHUNKS)
            for t in range(TILES):
                ins = nc.tensor.matmul(logits[:, t * E:(t + 1) * E], core.xt[:, t * P:(t + 1) * P], w_router[:],
                                       start=True, stop=True)
            ins.then_inc(logits_full, 1)
            pe.wait_ge(hot_ready, 1)
            for g in range(CHUNKS):
                if g:
                    pe.wait_ge(hot_copied, g)
                for t in range(4):
                    ins = nc.tensor.transpose(hot_ps[0:E, t * P:(t + 1) * P], hot[:, 4 * g + t, :], core.ident[:])
                ins.then_inc(hot_full, 1)
            for e in range(E):
                pe_transpose_tiles(core, pe, xe[e], (xe_ready[e], 1), xt_full, (xt_copied, CHUNKS * (e + 1)))
                pe.wait_ge(xt_copied, CHUNKS * (e + 2))
            with pe.Fori(0, CHUNKS) as c:
                for j in range(IB):
                    pe.wait_ge(h_free, c * IB + j + 1)
                    h = core.ps[j % 2]
                    for e in range(E):
                        nc.tensor.matmul(h[:], w1[:, e, j * P:(j + 1) * P], xe_t[:, e, bass.ds(c * CHUNK, CHUNK)],
                                         start=(e == 0), stop=False)
                    nc.tensor.matmul(h[:], b1[:, j * P:(j + 1) * P], hot_t[:, bass.ds(c * CHUNK, CHUNK)],
                                     start=False, stop=True).then_inc(h_full, 1)
                pe.wait_ge(y_free, c + 1)
                pe.wait_ge(act_step, c * IB + IB)
                for t in range(4):
                    for j in range(IB):
                        ins = nc.tensor.matmul(y_ps[:, t * P:(t + 1) * P], hidden[:, j, t * P:(t + 1) * P], wo[:, j, :],
                                               start=(j == 0), stop=(j == IB - 1))
                ins.then_inc(y_full, 1)

        @block.scalar
        def _(act):
            act_rstd(core, act, stat, var_ready, rstd_ready, 1)
            act_copy_transposed(core, act, core.xt, xt_full, xt_copied)
            for g in range(CHUNKS):
                act.wait_ge(hot_full, g + 1)
                nc.scalar.copy(hot_t[:, g * CHUNK:(g + 1) * CHUNK], hot_ps[0:E, :]).then_inc(hot_copied, 1)
            for e in range(E):
                act_copy_transposed(core, act, xe_t[:, e], xt_full, xt_copied, CHUNKS * (e + 1))
            act.sem_inc(h_free, 2)
            with act.Fori(0, CHUNKS) as c:
                for j in range(IB):
                    act.wait_ge(h_full, c * IB + j + 1)
                    if j == 0:
                        act.wait_ge(hidden_free, c + 1)
                    nc.scalar.activation(hidden[:, j, :], core.ps[j % 2][:], ACT.Gelu).then_inc(act_step, 1)
                    act.wait_ge(act_step, c * IB + j + 1)
                    act.sem_inc(h_free, 1)
            act_rstd(core, act, stat, var_ready, rstd_ready, 2)

        @block.gpsimd
        def _(pool):
            pool.wait_ge(hot_ready, 1)
            for e in (2, 3):
                nc.gpsimd.tensor_tensor(xe[e][:], core.xn[:], core.col(hot[:, :, e]), ALU.mult).then_inc(xe_ready[e], 1)

        @block.vector
        def _(dve):
            v = nc.vector
            step = Chain(dve, dve_step)
            step(dve_norm(core, step, core.x, core.xn, square, stat, 1e-5, var_ready, rstd_ready, 1))
            dve.sem_inc(normed, 1)
            dve.wait_ge(logits_full, 1)
            scores = logits[:, 0:TILES * E].rearrange("p (t e) -> p t e", e=E)
            step(v.tensor_reduce(best[:], scores, AX.X, ALU.max))
            step(v.tensor_tensor(hot[:], scores, core.col(best[:], E), ALU.is_equal))
            step(v.tensor_scalar(left[:], hot[:, :, 0], -1.0, 1.0, ALU.mult, ALU.add))
            for e in range(1, E):
                step(v.tensor_tensor(hot[:, :, e], hot[:, :, e], left[:], ALU.mult))
                step(v.tensor_tensor(left[:], left[:], hot[:, :, e], ALU.subtract))
            dve.sem_inc(hot_ready, 1)
            for e in (0, 1):
                v.tensor_tensor(xe[e][:], core.xn[:], core.col(hot[:, :, e]), ALU.mult).then_inc(xe_ready[e], 1)
            dve.wait_ge(loads, 7 * 16)
            dve.sem_inc(y_free, 1)
            dve.sem_inc(hidden_free, 1)
            with step.loop(CHUNKS, 2) as c:
                dve.wait_ge(y_full, c + 1)
                part = y[:, bass.ds(c * 4, 4), :]
                step(v.tensor_tensor(part, y_ps[:].rearrange("p (t c) -> p t c", c=P), core.xn[:, bass.ds(c * 4, 4), :],
                                     ALU.add))
                dve.sem_inc(y_free, 1)
                dve.sem_inc(hidden_free, 1)
                step(v.tensor_tensor(part, part, core.row(bo[:], 4), ALU.add))
            step(dve_norm(core, step, y, y, square, stat, 1e-12, var_ready, rstd_ready, 2))
            step(v.tensor_tensor(y[:], y[:], core.row(gamma[:]), ALU.mult))
            step(v.tensor_tensor(y[:], y[:], core.row(beta[:]), ALU.add))
            step(v.tensor_tensor(core.x[:], core.x[:], y[:], ALU.add))


def linear_attention_stage(core):
    nc, d = core.nc, core.dram
    H, M, F = 16, 8, 512
    FB = F // P
    STAB = 0.001
    KV = P + H
    tag = "la_"
    with ExitStack() as ctx:
        sb = lambda name, shape, dt=F32: ctx.enter_context(nc.sbuf_tensor(tag + name, shape, dt))
        sem = lambda name: core.semaphore(ctx, tag + name)
        wq, wkv, wo = sb("wq", [P, P]), sb("wkv", [P, 2 * P]), sb("wo", [P, P])
        w1, b1, w2, b2 = sb("w1", [P, F]), sb("b1", [P, FB]), sb("w2", [P, FB, P]), sb("b2", [P, P])
        gamma, beta, head = sb("gamma", [P, P]), sb("beta", [P, P]), sb("head", [P, H])
        square = sb("square", [P, TILES, P])
        stat = sb("stat", [P, 4, TILES])
        ln = sb("ln", [P, TILES, P])
        q_t = sb("q_t", [P, TOKENS])
        k = sb("k", [P, TILES, P])
        v1 = sb("v1", [P, TILES, P + 1])
        kv = sb("kv", [P, BATCH, KV])
        recip = sb("recip", [P, TILES, H])
        att = sb("att", [P, TILES, P])
        add1 = sb("add1", [P, TILES, P])
        hidden = sb("hidden", [P, FB, CHUNK])
        y = sb("y", [P, TILES, P])

        loads = sem("loads")
        var_ready, rstd_ready, ln_ready = sem("var_ready"), sem("rstd_ready"), sem("ln_ready")
        xt_full, xt_copied = sem("xt_full"), sem("xt_copied")
        q_full, q_ready = sem("q_full"), sem("q_ready")
        kv_full, k_ready, v_ready = sem("kv_full"), sem("k_ready"), sem("v_ready")
        sums_full, sums_ready = sem("sums_full"), sem("sums_ready")
        att_full, att_ready = sem("att_full"), sem("att_ready")
        out_full, add_ready = sem("out_full"), sem("add_ready")
        h_full, h_ready = sem("h_full"), sem("h_ready")
        y_full, y_ready, y_read = sem("y_full"), sem("y_ready"), sem("y_read")
        dve_step, out_gelu = sem("dve_step"), sem("out_gelu")
        block = core.block(ctx)

        @block.sync
        def _(sp):
            for dst, src in ((wq[:], d["la_wq"]), (wkv[:, 0:P], d["la_wk"]), (wkv[:, P:2 * P], d["la_wv"]), (wo[:], d["la_wo"]),
                             (w1[:], d["la_w1"]), (b1[:], d["la_b1"].rearrange("(j p) -> p j", p=P)),
                             (w2[:], d["la_w2"].rearrange("(j p) c -> p j c", p=P)), (b2[:], d["la_b2"].partition_broadcast(P)),
                             (gamma[:], d["la_gamma"].partition_broadcast(P)), (beta[:], d["la_beta"].partition_broadcast(P)),
                             (head[:], d["head_mask"])):
                with nc.allow_non_contiguous_dma("a bias per partition"):
                    sp.dma_start(dst, src).then_inc(loads, 16)

        @block.tensor
        def _(pe):
            pe_transpose_tiles(core, pe, ln, (ln_ready, 1), xt_full, (xt_copied, 0))
            pe.wait_ge(xt_copied, CHUNKS)
            pe.wait_ge(loads, 11 * 16)
            for g in range(CHUNKS):
                if g >= 2:
                    pe.wait_ge(q_ready, g - 1)
                nc.tensor.matmul(core.ps[2 + g % 2], wq[:], core.xt[:, g * CHUNK:(g + 1) * CHUNK], start=True,
                                 stop=True).then_inc(q_full, 1)
            for g in range(TILES // 2):
                if g >= 2:
                    pe.wait_ge(k_ready, g - 1)
                    pe.wait_ge(v_ready, g - 1)
                for t in range(2):
                    at = (2 * g + t) * P
                    ins = nc.tensor.matmul(core.ps[4 + g % 2][:, t * 2 * P:(t + 1) * 2 * P], core.xt[:, at:at + P], wkv[:],
                                           start=True, stop=True)
                ins.then_inc(kv_full, 1)
            for b in range(BATCH):
                pe.wait_ge(k_ready, (b + 1) * TILES // 4)
                pe.wait_ge(v_ready, (b + 1) * TILES // 4)
                for t in range(TILES // 2):
                    ins = nc.tensor.matmul(core.ps[6 + b][:, 0:P + 1], k[:, b * 8 + t, :], v1[:, b * 8 + t, :],
                                           start=(t == 0), stop=(t == 7))
                ins.then_inc(sums_full, 1)
            pe.wait_ge(q_ready, CHUNKS)
            for g in range(TILES // 2):
                pe.wait_ge(sums_ready, g // 4 + 1)
                if g >= 2:
                    pe.wait_ge(att_ready, g - 1)
                for t in range(2):
                    at = (2 * g + t) * P
                    ins = nc.tensor.matmul(core.ps[2 + g % 2][:, t * KV:(t + 1) * KV], q_t[:, at:at + P], kv[:, g // 4, :],
                                           start=True, stop=True)
                ins.then_inc(att_full, 1)
            pe_transpose_tiles(core, pe, att, (att_ready, TILES // 2), xt_full, (xt_copied, CHUNKS))
            pe.wait_ge(xt_copied, 2 * CHUNKS)
            for g in range(CHUNKS):
                if g >= 2:
                    pe.wait_ge(add_ready, g - 1)
                for t in range(4):
                    at = (4 * g + t) * P
                    ins = nc.tensor.matmul(core.ps[4 + g % 2][:, t * P:(t + 1) * P], core.xt[:, at:at + P], wo[:],
                                           start=True, stop=True)
                ins.then_inc(out_full, 1)
            pe_transpose_tiles(core, pe, ln, (ln_ready, 2), xt_full, (xt_copied, 2 * CHUNKS))
            pe.wait_ge(xt_copied, 3 * CHUNKS)
            with pe.Fori(0, CHUNKS) as c:
                for j in range(FB):
                    pe.wait_ge(h_ready, c * FB + j + 1)
                    nc.tensor.matmul(core.ps[j % 2], w1[:, j * P:(j + 1) * P], core.xt[:, bass.ds(c * CHUNK, CHUNK)],
                                     start=True, stop=True).then_inc(h_full, 1)
                pe.wait_ge(h_ready, c * FB + FB + 2)
                pe.wait_ge(y_read, c + 1)
                for t in range(4):
                    for j in range(FB):
                        ins = nc.tensor.matmul(core.ps[2][:, t * P:(t + 1) * P], hidden[:, j, t * P:(t + 1) * P], w2[:, j, :],
                                               start=(j == 0), stop=(j == FB - 1))
                ins.then_inc(y_full, 1)

        @block.scalar
        def _(act):
            act_rstd(core, act, stat, var_ready, rstd_ready, 1)
            act_rstd(core, act, stat, var_ready, rstd_ready, 2)
            act_copy_transposed(core, act, core.xt, xt_full, xt_copied)
            for g in range(TILES // 2):
                act.wait_ge(kv_full, g + 1)
                nc.scalar.copy(v1[:, 2 * g:2 * g + 2, 0:P],
                               core.ps[4 + g % 2].rearrange("p (t k c) -> p t k c", t=2, k=2)[:, :, 1]).then_inc(v_ready, 1)
            act_copy_transposed(core, act, core.xt, xt_full, xt_copied, CHUNKS)
            act_rstd(core, act, stat, var_ready, rstd_ready, 3)
            act_copy_transposed(core, act, core.xt, xt_full, xt_copied, 2 * CHUNKS)
            act.sem_inc(h_ready, 2)
            with act.Fori(0, CHUNKS) as c:
                act.wait_ge(y_read, c + 1)
                for j in range(FB):
                    act.wait_ge(h_full, c * FB + j + 1)
                    nc.scalar.activation(hidden[:, j, :], core.ps[j % 2], ACT.Gelu, bias=b1[:, j:j + 1]).then_inc(h_ready, 1)
            for g in range(CHUNKS):
                act.wait_ge(y_ready, g + 1)
                part = y[:, 4 * g:4 * g + 4, :]
                nc.scalar.activation(part, part, ACT.Gelu).then_inc(out_gelu, 1)

        @block.vector
        def _(dve):
            v = nc.vector
            step = Chain(dve, dve_step)
            step(v.memset(v1[:, :, P:P + 1], 1.0))
            step(dve_norm(core, step, core.x, core.xn, square, stat, 1e-5, var_ready, rstd_ready, 1))
            step(dve_norm(core, step, core.xn, ln, square, stat, 1e-6, var_ready, rstd_ready, 2))
            dve.wait_ge(loads, 11 * 16)
            step(v.tensor_tensor(ln[:], ln[:], core.row(gamma[:]), ALU.mult))
            step(v.tensor_tensor(ln[:], ln[:], core.row(beta[:]), ALU.add))
            dve.sem_inc(ln_ready, 1)
            for g in range(CHUNKS):
                dve.wait_ge(q_full, g + 1)
                v.tensor_scalar(q_t[:, g * CHUNK:(g + 1) * CHUNK], core.ps[2 + g % 2], 0.0, STAB, ALU.max, ALU.add).then_inc(q_ready, 1)
            for g in range(TILES // 2):
                dve.wait_ge(v_ready, g + 1)
                v.tensor_scalar(k[:, 2 * g:2 * g + 2, :], core.ps[4 + g % 2].rearrange("p (t k c) -> p t k c", t=2, k=2)[:, :, 0],
                                0.0, STAB, ALU.max, ALU.add).then_inc(k_ready, 1)
            for b in range(BATCH):
                dve.wait_ge(sums_full, b + 1)
                step(v.tensor_tensor(kv[:, b, 0:P].rearrange("p (h c) -> p h c", c=M), core.ps[6 + b][:, 0:P].rearrange("p (h c) -> p h c", c=M),
                                     head[:].unsqueeze(2).to_broadcast([P, H, M]), ALU.mult))
                step(v.tensor_tensor(kv[:, b, P:KV], head[:], core.ps[6 + b][:, P:P + 1].to_broadcast([P, H]), ALU.mult))
                dve.sem_inc(sums_ready, 1)
            for g in range(TILES // 2):
                dve.wait_ge(att_full, g + 1)
                part = core.ps[2 + g % 2][:, 0:2 * KV].rearrange("p (t n) -> p t n", t=2)
                step(v.reciprocal(recip[:, 2 * g:2 * g + 2], part[:, :, P:KV]))
                v.tensor_tensor(att[:, 2 * g:2 * g + 2, :].rearrange("p t (h c) -> p t h c", c=M), part[:, :, 0:P].rearrange("p t (h c) -> p t h c", c=M),
                                recip[:, 2 * g:2 * g + 2].unsqueeze(3).to_broadcast([P, 2, H, M]), ALU.mult).then_inc(att_ready, 1)
            for g in range(CHUNKS):
                dve.wait_ge(out_full, g + 1)
                v.tensor_tensor(add1[:, 4 * g:4 * g + 4, :], core.ps[4 + g % 2].rearrange("p (t c) -> p t c", c=P),
                                core.xn[:, 4 * g:4 * g + 4, :], ALU.add).then_inc(add_ready, 1)
            dve.wait_ge(add_ready, CHUNKS)
            step(dve_norm(core, step, add1, ln, square, stat, 1e-6, var_ready, rstd_ready, 3))
            step(v.tensor_tensor(ln[:], ln[:], core.row(gamma[:]), ALU.mult))
            step(v.tensor_tensor(ln[:], ln[:], core.row(beta[:]), ALU.add))
            dve.sem_inc(ln_ready, 1)
            step(v.tensor_tensor(core.x[:], core.x[:], add1[:], ALU.add))
            dve.sem_inc(y_read, 1)
            for g in range(CHUNKS):
                dve.wait_ge(y_full, g + 1)
                part = y[:, 4 * g:4 * g + 4, :]
                v.tensor_tensor(part, core.ps[2].rearrange("p (t c) -> p t c", c=P), core.row(b2[:], 4), ALU.add).then_inc(y_read, 1)
                dve.wait_ge(y_read, g + 2)
                dve.sem_inc(y_ready, 1)
            for g in range(CHUNKS):
                dve.wait_ge(out_gelu, g + 1)
                part = slice(4 * g, 4 * g + 4)
                step(v.tensor_tensor(core.x[:, part], core.x[:, part], y[:, part], ALU.add))


class HeadStream:
    T = SEQ // P
    SLOTS = 2 * T

    def __init__(self, core, ctx, tag, turn_banks):
        nc = self.nc = core.nc
        self.core = core
        self.turned = (core.ps[4], core.ps[3 + turn_banks])
        self.halves_before = 3 - turn_banks
        sb = lambda name, shape, dt=F32: ctx.enter_context(nc.sbuf_tensor(tag + name, shape, dt))
        sem = lambda name: core.semaphore(ctx, tag + name)
        self.qz, self.kt = sb("q_z", [P, 2, 2, SEQ]), sb("k_t", [P, 2, SEQ])
        self.v = sb("v", [P, self.T, 2, 65])
        self.v_hi, self.v_lo = sb("v_hi", [P, 2, self.T, 2, 65], BF16), sb("v_lo", [P, 2, self.T, 2, 65], BF16)
        self.negmax = sb("negmax", [P, 2])
        self.p = sb("p", [P, 2, SEQ])
        self.p_hi, self.p_lo = sb("p_hi", [P, 2, SEQ], BF16), sb("p_lo", [P, 2, SEQ], BF16)
        self.recip = sb("recip", [P, 2])
        self.o = sb("o", [P, 2, self.T, 2, 64])
        self.filled = sem("filled")
        self.s_full = sem("s_full")
        self.max_ready = sem("max_ready")
        self.exp_done = sem("exp_done")
        self.pt_full = sem("pt_full")
        self.hi_ready = sem("hi_ready")
        self.lo_ready = sem("lo_ready")
        self.av_done = sem("av_done")
        self.o_ready = sem("o_ready")
        self.recip_ready = sem("recip_ready")
        self.v_split_hi = sem("v_split_hi")
        self.v_split = sem("v_split")

    def fill(self, pool):
        g = self.nc.gpsimd
        for ap, value in ((self.v[:, :, :, 64:65], 1.0), (self.qz[:], 0.0), (self.o[:], 0.0), (self.p[:], 1.0),
                          (self.p_hi[:], 1.0), (self.p_lo[:], 0.0), (self.v_hi[:, 1, :, :, 0:64], 0.0),
                          (self.v_hi[:, 1, :, :, 64:65], 1.0), (self.v_lo[:, 1], 0.0)):
            g.memset(ap, value).then_inc(self.filled, 1)
    FILLS = 9

    def pe_seed(self, pe):
        pe.wait_ge(self.filled, self.FILLS)
        pe.sem_inc(self.pt_full, 2)
        pe.sem_inc(self.av_done, 1)

    def act_seed(self, act):
        act.wait_ge(self.filled, self.FILLS)
        act.sem_inc(self.exp_done, 2)

    def dve_seed(self, dve):
        dve.wait_ge(self.filled, self.FILLS)
        dve.sem_inc(self.lo_ready, 2)
        dve.sem_inc(self.o_ready, 1)

    def scores(self, pe, unit, b, i):
        s, t, h = unit * self.SLOTS + i, i // 2, i % 2
        pe.wait_ge(self.exp_done, s + 1)
        for half in range(2):
            ins = self.nc.tensor.matmul(self.core.ps[2 * h + half], self.qz[:, b, h, t * P:(t + 1) * P],
                                        self.kt[:, b, half * CHUNK:(half + 1) * CHUNK], start=True, stop=True)
        ins.then_inc(self.s_full, 1)

    def transpose(self, pe, unit, i, g):
        s, h = unit * self.SLOTS + i, (i - 1) % 2
        if g == 0:
            pe.wait_ge(self.exp_done, s + 2)
        pe.wait_ge(self.lo_ready, s * 2 + g + self.halves_before)
        for j in range(4):
            k = 4 * g + j
            ins = self.nc.tensor.transpose(self.turned[g][:, j * P:(j + 1) * P], self.p[:, h, k * P:(k + 1) * P],
                                           self.core.ident[:])
        ins.then_inc(self.pt_full, 1)

    def values(self, pe, unit, b, i):
        s, t, h = unit * self.SLOTS + i, (i - 2) // 2, i % 2
        own = b if i >= 2 else 1 - b
        pe.wait_ge(self.lo_ready, s * 2 + 2)
        if h == 0:
            pe.wait_ge(self.o_ready, unit * self.T + i // 2 + 1)
        if i == 2:
            pe.wait_ge(self.v_split, unit + 1)
        at = (t % 2) * 130 + h * 65
        for k in range(self.T):
            block = slice(k * P, (k + 1) * P)
            for n, (p, v) in enumerate(((self.p_hi, self.v_hi), (self.p_hi, self.v_lo), (self.p_lo, self.v_hi))):
                ins = self.nc.tensor.matmul(self.core.ps[6][:, at:at + 65], p[:, h, block], v[:, own, k, h, :],
                                            start=(k == 0 and n == 0), stop=(k == self.T - 1 and n == 2))
        ins.then_inc(self.av_done, 1)

    def act_hi(self, act, unit, i, g):
        s, h = unit * self.SLOTS + i, (i - 1) % 2
        if g == 0:
            act.wait_ge(self.av_done, s + 1)
        act.wait_ge(self.pt_full, s * 2 + g + 3)
        self.nc.scalar.copy(self.p_hi[:, h, g * CHUNK:(g + 1) * CHUNK], self.turned[g]).then_inc(self.hi_ready, 1)

    def act_exp(self, act, unit, i):
        s, h = unit * self.SLOTS + i, i % 2
        act.wait_ge(self.max_ready, s + 1)
        act.wait_ge(self.pt_full, s * 2 + 2)
        self.nc.scalar.activation(self.p[:, h, :], self.core.banks[:, 2 * h:2 * h + 2, :], ACT.Exp,
                                  bias=self.negmax[:, h:h + 1]).then_inc(self.exp_done, 1)

    def dve_max(self, dve, unit, i):
        h = i % 2
        dve.wait_ge(self.s_full, unit * self.SLOTS + i + 1)
        self.nc.vector.tensor_reduce(self.negmax[:, h:h + 1], self.core.banks[:, 2 * h:2 * h + 2, :], AX.XY, ALU.max,
                                     negate=True).then_inc(self.max_ready, 1)

    def dve_lo(self, dve, unit, i, g):
        s, h = unit * self.SLOTS + i, (i - 1) % 2
        part = slice(g * CHUNK, (g + 1) * CHUNK)
        dve.wait_ge(self.hi_ready, s * 2 + g + 1)
        self.nc.vector.tensor_tensor(self.p_lo[:, h, part], self.turned[g], self.p_hi[:, h, part],
                                     ALU.subtract).then_inc(self.lo_ready, 1)

    def dve_normalise(self, dve, unit, b, i):
        t = (i - 3) // 2
        own = b if i >= 3 else 1 - b
        dve.wait_ge(self.av_done, unit * self.SLOTS + i + 2)
        o = self.core.ps[6][:, (t % 2) * 130:(t % 2 + 1) * 130].rearrange("p (h c) -> p h c", h=2)
        self.nc.vector.reciprocal(self.recip[:], o[:, :, 64]).then_inc(self.recip_ready, 1)
        dve.wait_ge(self.recip_ready, unit * self.T + t + 2)
        self.nc.vector.tensor_tensor(self.o[:, own, t % self.T], o[:, :, 0:64], self.core.col(self.recip[:], 64),
                                     ALU.mult).then_inc(self.o_ready, 1)

    def act_split_values(self, act, unit, b, ready):
        act.wait_ge(*ready)
        self.nc.scalar.copy(self.v_hi[:, b], self.v[:]).then_inc(self.v_split_hi, 1)

    def pool_split_values(self, pool, unit, b):
        pool.wait_ge(self.v_split_hi, unit + 1)
        self.nc.gpsimd.tensor_tensor(self.v_lo[:, b], self.v[:], self.v_hi[:, b], ALU.subtract).then_inc(self.v_split, 1)


def attention_stage(core):
    nc, d = core.nc, core.dram
    PAIRS = 8
    UNITS = PAIRS * BATCH
    tag = "at_"
    with ExitStack() as ctx:
        sb = lambda name, shape, dt=F32: ctx.enter_context(nc.sbuf_tensor(tag + name, shape, dt))
        sem = lambda name: core.semaphore(ctx, tag + name)
        w = sb("w", [P, 5, (PAIRS + 1) * P], BF16)
        bias_all, bias = sb("bias_all", [P, PAIRS + 1, 4], BF16), sb("bias", [P, 4])
        bv = sb("bv", [P, (PAIRS + 1) * P], BF16)
        wo_all = sb("wo_all", [P, PAIRS, P], BF16)
        wo = sb("wo", [P, PAIRS + 1, P])
        bo = sb("bo", [P, P], BF16)
        rope = sb("rope", [P, 4, SEQ])
        xt_parts = sb("xt_parts", [P, 3, TOKENS], BF16)
        turned = sb("turned", [P, 2, CHUNK])
        o_t = sb("o_t", [P, SEQ])
        stat = sb("stat", [P, 4, TILES])
        square = sb("square", [P, TILES, P])
        rest = square[:].rearrange("p t c -> p (t c)")
        hs = HeadStream(core, ctx, tag, turn_banks=2)

        loads, padded = sem("loads"), sem("padded")
        var_ready, rstd_ready, normed = sem("var_ready"), sem("rstd_ready"), sem("normed")
        xt_full, xt_copied = sem("xt_full"), sem("xt_copied")
        part_ready, rest_ready = sem("part_ready"), sem("rest_ready")
        proj_full = sem("proj_full")
        terms_ready = sem("terms_ready")
        bias_ready = sem("bias_ready")
        qk_ready = sem("qk_ready")
        v_full, v_ready = sem("v_full"), sem("v_ready")
        ot_full, ot_ready = sem("ot_full"), sem("ot_ready")
        y_full, y_added = sem("y_full"), sem("y_added")
        dve_step = sem("dve_step")
        spare = core.ps[7]
        LOADS = 9
        block = core.block(ctx)

        @block.sync
        def _(sp):
            biases = tuple((bias_all[:, 0:PAIRS, k], d["at_bias"][k].rearrange("g p -> p g")) for k in range(4))
            for dst, src in ((w[:, :, 0:PAIRS * P], d["at_w"].rearrange("k c n -> c k n")),
                             (bv[:, 0:PAIRS * P], d["at_bv"].partition_broadcast(P)), (wo_all[:], d["at_wo"].rearrange("(g p) c -> p g c", p=P)),
                             (bo[:], d["at_bo"].partition_broadcast(P)), (rope[:], d["rope"].rearrange("k p s -> p k s"))) + biases:
                with nc.allow_non_contiguous_dma("head-major weights"):
                    sp.dma_start(dst, src).then_inc(loads, 16)

        @block.tensor
        def _(pe):
            pe_transpose_tiles(core, pe, core.xn, (normed, 1), xt_full, (xt_copied, 0))
            pe.wait_ge(loads, LOADS * 16)
            pe.wait_ge(padded, 5)
            pe.wait_ge(part_ready, 2)
            pe.wait_ge(rest_ready, 2)

            def project(unit, pair, b, n, first=False):
                if n == 0:
                    if not first:
                        pe.wait_ge(v_ready, unit * 2)
                        pe.wait_ge(y_added, unit * 2 - 1)
                elif n <= 8:
                    pe.wait_ge(terms_ready, unit * 8 + n)
                else:
                    pe.wait_ge(v_ready, unit * 2 + 1)
                if n < 8:
                    kind, at = 2 * (n // 4) + n % 2, b * SEQ + (n // 2 % 2) * CHUNK
                    for j in range(3):
                        ins = nc.tensor.matmul(spare, w[:, kind, bass.ds(pair * P, P)], xt_parts[:, j, at:at + CHUNK],
                                               start=(j == 0), stop=(j == 2))
                    ins.then_inc(proj_full, 1)
                else:
                    for t in range(4):
                        at = b * SEQ + (4 * (n - 8) + t) * P
                        for j in range(3):
                            ins = nc.tensor.matmul(spare[:, t * P:(t + 1) * P], xt_parts[:, j, at:at + P],
                                                   w[:, 4, bass.ds(pair * P, P)], start=(j == 0), stop=(j == 2))
                    ins.then_inc(v_full, 1)

            def output(unit, b, at, n, v_count):
                if n == 0:
                    pe.wait_ge(v_ready, v_count)
                    pe.wait_ge(hs.o_ready, unit * hs.T + 2)
                else:
                    pe.wait_ge(ot_ready, unit * 2 + min(n, 2))
                if n == 3:
                    pe.wait_ge(y_added, unit * 2 + 2)
                for t in range(4):
                    tile = 4 * (n % 2) + t
                    if n < 2:
                        ins = nc.tensor.transpose(spare[:, t * P:(t + 1) * P], hs.o[:, 1 - b, tile].rearrange("p h c -> p (h c)"),
                                                  core.ident[:])
                    else:
                        ins = nc.tensor.matmul(spare[:, t * P:(t + 1) * P], o_t[:, tile * P:(tile + 1) * P],
                                               wo[:, bass.ds(at, 1), :].rearrange("p a b -> p (a b)"), start=True, stop=True)
                ins.then_inc(ot_full if n < 2 else y_full, 1)

            for n in range(10):
                project(0, 0, 0, n, True)
            hs.pe_seed(pe)
            with pe.Fori(0, PAIRS) as pair:
                for b in range(BATCH):
                    u = pair * BATCH + b
                    for i in range(hs.SLOTS):
                        if i == 0:
                            pe.wait_ge(qk_ready, u * 4 + 5)
                        hs.scores(pe, u, b, i)
                        for g in range(2):
                            hs.transpose(pe, u, i, g)
                        hs.values(pe, u, b, i)
                        if i < 10:
                            project(u + 1, pair + b, 1 - b, i)
                        elif i < 14:
                            output(u, b, pair + b, i - 10, u * 2 + 4)
            for g in range(2):
                hs.transpose(pe, UNITS, 0, g)
            hs.values(pe, UNITS, 0, 0)
            hs.values(pe, UNITS, 0, 1)
            for n in range(4):
                output(UNITS, 0, PAIRS, n, UNITS * 2 + 2)

        @block.scalar
        def _(act):
            act_rstd(core, act, stat, var_ready, rstd_ready, 1)
            act_copy_transposed(core, act, core.xt, xt_full, xt_copied)
            act.wait_ge(xt_copied, CHUNKS)
            nc.scalar.copy(xt_parts[:, 0, :], core.xt[:]).then_inc(part_ready, 1)
            act.wait_ge(rest_ready, 1)
            nc.scalar.copy(xt_parts[:, 1, :], rest).then_inc(part_ready, 1)
            hs.act_seed(act)

            def copy_outputs(u, n):
                act.wait_ge(ot_full, u * 2 + n + 1)
                nc.scalar.copy(o_t[:, n * CHUNK:(n + 1) * CHUNK], spare).then_inc(ot_ready, 1)

            hs.act_split_values(act, 0, 0, (v_ready, 2))
            with act.Fori(0, PAIRS) as pair:
                for b in range(BATCH):
                    u = pair * BATCH + b
                    for i in range(hs.SLOTS):
                        for g in range(2):
                            hs.act_hi(act, u, i, g)
                        hs.act_exp(act, u, i)
                        if i in (10, 11):
                            copy_outputs(u, i - 10)
                        if i == 12:
                            hs.act_split_values(act, u + 1, 1 - b, (v_ready, u * 2 + 4))
            for g in range(2):
                hs.act_hi(act, UNITS, 0, g)
            for n in range(2):
                copy_outputs(UNITS, n)

        @block.gpsimd
        def _(pool):
            g = nc.gpsimd
            hs.fill(pool)
            for ap in (w[:, :, PAIRS * P:], bias_all[:, PAIRS, :], bv[:, PAIRS * P:], wo[:, 0]):
                g.memset(ap, 0.0).then_inc(padded, 1)
            pool.wait_ge(loads, LOADS * 16)
            g.tensor_copy(wo[:, 1:], wo_all[:]).then_inc(padded, 1)

            def sum_keys(unit, b):
                for c in range(2):
                    pool.wait_ge(terms_ready, unit * 8 + 2 * c + 6)
                    g.tensor_tensor(hs.kt[:, b, c * CHUNK:(c + 1) * CHUNK], turned[:, 0, :], turned[:, 1, :],
                                    ALU.add).then_inc(qk_ready, 1)
                hs.pool_split_values(pool, unit, b)

            sum_keys(0, 0)
            with pool.Fori(0, PAIRS) as pair:
                for b in range(BATCH):
                    sum_keys(pair * BATCH + b + 1, 1 - b)

        @block.vector
        def _(dve):
            v = nc.vector
            step = Chain(dve, dve_step)
            step(dve_norm(core, step, core.x, core.xn, square, stat, 1e-5, var_ready, rstd_ready, 1))
            dve.sem_inc(normed, 1)
            dve.wait_ge(loads, LOADS * 16)
            step(v.tensor_tensor(core.x[:], core.x[:], core.row(bo[:]), ALU.add))
            dve.wait_ge(part_ready, 1)
            v.tensor_tensor(rest, core.xt[:], xt_parts[:, 0, :], ALU.subtract).then_inc(rest_ready, 1)
            dve.wait_ge(part_ready, 2)
            v.tensor_tensor(xt_parts[:, 2, :], rest, xt_parts[:, 1, :], ALU.subtract).then_inc(rest_ready, 1)
            dve.wait_ge(padded, 5)

            def rotate(unit, pair, b, n, first=False):
                if n < 8:
                    g, term = n // 2, n % 2
                    kind, chunk = 2 * (g // 2) + term, slice((g % 2) * CHUNK, (g % 2 + 1) * CHUNK)
                    dve.wait_ge(proj_full, unit * 8 + n + 1)
                    if term == 0:
                        dve.wait_ge(qk_ready, unit * 4 + g + 1)
                    if n == 0:
                        v.tensor_copy(bias[:], bias_all[:, bass.ds(pair, 1), :].rearrange("p a b -> p (a b)")).then_inc(bias_ready, 1)
                        dve.wait_ge(bias_ready, unit + 1)
                    v.scalar_tensor_tensor(out=turned[:, term, :], in0=spare, scalar=bias[:, kind:kind + 1],
                                           in1=rope[:, kind, chunk], op0=ALU.add, op1=ALU.mult).then_inc(terms_ready, 1)
                    if n in (1, 3):
                        dve.wait_ge(terms_ready, unit * 8 + n + 1)
                        for h in range(2):
                            rows = slice(64 * h, 64 * h + 64)
                            ins = v.tensor_tensor(hs.qz[rows, b, h, chunk], turned[rows, 0, :], turned[rows, 1, :], ALU.add)
                        ins.then_inc(qk_ready, 1)
                    return
                if n == 8 and not first:
                    dve.wait_ge(hs.v_split, unit)
                dve.wait_ge(v_full, unit * 2 + n - 7)
                v.tensor_tensor(hs.v[:, 4 * (n - 8):4 * (n - 7), :, 0:64], spare.rearrange("p (t h c) -> p t h c", t=4, h=2),
                                bv[:, bass.ds(pair * P, P)].rearrange("p (h c) -> p h c", h=2).unsqueeze(1).to_broadcast([P, 4, 2, 64]),
                                ALU.add).then_inc(v_ready, 1)

            def add_outputs(u, b, n):
                dve.wait_ge(y_full, u * 2 + n + 1)
                at = b * hs.T + 4 * n
                v.tensor_tensor(core.x[:, at:at + 4, :], core.x[:, at:at + 4, :], spare.rearrange("p (t c) -> p t c", c=P),
                                ALU.add).then_inc(y_added, 1)

            dve.sem_inc(qk_ready, 1)
            dve.sem_inc(y_added, 1)
            hs.dve_seed(dve)
            for n in range(10):
                rotate(0, 0, 0, n, True)
            with dve.Fori(0, PAIRS) as pair:
                for b in range(BATCH):
                    u = pair * BATCH + b
                    for i in range(hs.SLOTS):
                        hs.dve_max(dve, u, i)
                        for g in range(2):
                            hs.dve_lo(dve, u, i, g)
                        if i % 2:
                            hs.dve_normalise(dve, u, b, i)
                        if i < 10:
                            rotate(u + 1, pair + b, 1 - b, i)
                        elif 12 <= i < 14:
                            add_outputs(u, 1 - b, i - 12)
            for g in range(2):
                hs.dve_lo(dve, UNITS, 0, g)
            hs.dve_normalise(dve, UNITS, 0, 1)
            for n in range(2):
                add_outputs(UNITS, 1, n)


def expert_attention_stage(core, tag):
    nc, d = core.nc, core.dram
    H, E, D, TOP = 8, 5, 64, 3
    PAIRS = H // 2
    UNITS = PAIRS * BATCH
    ED = E * D
    ROWS_OUT = (P, P, ED - 2 * P)
    T = SEQ // P
    PIECES = T * 6
    PER_SLOT = 4
    DONE = {(6 * t + 5) // PER_SLOT: t for t in range(T)}
    with ExitStack() as ctx:
        sb = lambda name, shape, dt=F32: ctx.enter_context(nc.sbuf_tensor(tag + name, shape, dt))
        sem = lambda name: core.semaphore(ctx, tag + name)
        w = sb("w", [P, 3 * H + 2, ED])
        w_gate = sb("w_gate", [P, 2 * H * E])
        wo = sb("wo", [P, 3, P])
        stat = sb("stat", [P, 4, TILES])
        gate = sb("gate", [P, 2 * TILES * H, E])
        mask = sb("mask", [P, 2 * TILES * H, E])
        scratch = sb("scratch", [P, 6 * 2 * ED])
        qk_product = scratch[:, 0:4 * 2 * ED].rearrange("p (t k h e c) -> p t k h e c", t=2, k=2, h=2, e=E)
        v_product = scratch[:, 4 * 2 * ED:6 * 2 * ED].rearrange("p (t h e c) -> p t h e c", t=2, h=2, e=E)
        square = scratch[:, 0:TILES * P].rearrange("p (t c) -> p t c", c=P)
        beats = scratch[:, 0:2 * TILES * H * E].rearrange("p (n e) -> p n e", e=E)
        lost = sb("lost", [P, 2 * TILES * H])
        tok = sb("tok", [P, 2, T, 2, D])
        routed = sb("routed", [P, 2, E, D])
        z = sb("z", [P, TILES, ED])
        z_t = sb("z_t", [P, 2, 3, P])
        hs = HeadStream(core, ctx, tag, turn_banks=1)
        by_which = lambda t: t[:].rearrange("p (w n) e -> p w (n e)", w=2)

        loads, padded = sem("loads"), sem("padded")
        var_ready, rstd_ready, normed = sem("var_ready"), sem("rstd_ready"), sem("normed")
        xt_full, xt_copied = sem("xt_full"), sem("xt_copied")
        gates_full, gates_ready = sem("gates_full"), sem("gates_ready")
        proj_full = sem("proj_full")
        product_ready = sem("product_ready")
        tok_ready = sem("tok_ready")
        v_ready = sem("v_ready")
        qk_full, qk_ready = sem("qk_full"), sem("qk_ready")
        zt_full, zt_ready = sem("zt_full"), sem("zt_ready")
        y_full, y_added = sem("y_full"), sem("y_added")
        dve_step, pool_step, z_ready = sem("dve_step"), sem("pool_step"), sem("z_ready")
        spare = (core.ps[5], core.ps[7])
        GB = 6
        block = core.block(ctx)

        @block.sync
        def _(sp):
            for dst, src in ((w[:, 0:3 * H, :].rearrange("p (k h) n -> p k (h n)", k=3), d["ex_w"].rearrange("k c n -> c k n")), (w_gate[:], d["ex_gate"]),
                             (wo[:, 0:2, :], d["ex_wo"][0:256, :].rearrange("(j p) c -> p j c", p=P)),
                             (wo[0:64, 2, :], d["ex_wo"][256:320, :])):
                sp.dma_start(dst, src).then_inc(loads, 16)

        @block.tensor
        def _(pe):
            pe_transpose_tiles(core, pe, core.xn, (normed, 1), xt_full, (xt_copied, 0))
            pe.wait_ge(xt_copied, CHUNKS)
            pe.wait_ge(loads, 4 * 16)
            for t in range(TILES):
                ins = nc.tensor.matmul(core.ps[2 + t // GB][:, (t % GB) * 80:(t % GB + 1) * 80], core.xt[:, t * P:(t + 1) * P],
                                       w_gate[:], start=True, stop=True)
            ins.then_inc(gates_full, 1)
            pe.wait_ge(gates_ready, 3)
            pe.wait_ge(padded, 1)

            def project(unit, pair, b, n, out):
                t, kind, h = n // 6, n // 2 % 3, n % 2
                ins = nc.tensor.matmul(out[:, 0:ED], core.xt[:, b * SEQ + t * P:b * SEQ + (t + 1) * P],
                                       w[:, bass.ds(pair * 2 + (kind * H + h), 1), :].rearrange("p a n -> p (a n)"),
                                       start=True, stop=True)
                ins.then_inc(proj_full, 1)

            def turn(unit, m, out):
                pe.wait_ge(tok_ready, unit * 16 + 8 * (m // 2 + 1))
                for t in range(4):
                    ins = nc.tensor.transpose(out[:, t * P:(t + 1) * P], tok[:, m % 2, 4 * (m // 2) + t].rearrange("p h c -> p (h c)"),
                                              core.ident[:])
                ins.then_inc(qk_full, 1)

            for n in range(PIECES):
                if n >= 4:
                    pe.wait_ge(product_ready, n - 3)
                project(0, 0, 0, n, core.ps[n % 4])
            for m in range(4):
                turn(0, m, core.ps[4 + m])
            hs.pe_seed(pe)
            with pe.Fori(0, PAIRS) as pair:
                for b in range(BATCH):
                    u = pair * BATCH + b
                    for i in range(hs.SLOTS):

                        def piece(k):
                            n = i * PER_SLOT + k
                            if n < PIECES:
                                if n >= 2:
                                    pe.wait_ge(product_ready, (u + 1) * PIECES + n - 1)
                                project(u + 1, pair + b, 1 - b, n, spare[n % 2])
                            elif k == 0:
                                m = i - PIECES // PER_SLOT
                                if m < 2:
                                    pe.wait_ge(product_ready, (u + 2) * PIECES)
                                else:
                                    pe.wait_ge(qk_ready, (u + 1) * 4 + m - 1)
                                turn(u + 1, m, spare[m % 2])

                        if i == 0:
                            pe.wait_ge(qk_ready, u * 4 + 4)
                        hs.scores(pe, u, b, i)
                        piece(0)
                        hs.transpose(pe, u, i, 0)
                        piece(1)
                        hs.values(pe, u, b, i)
                        piece(2)
                        hs.transpose(pe, u, i, 1)
                        piece(3)
            for g in range(2):
                hs.transpose(pe, UNITS, 0, g)
            hs.values(pe, UNITS, 0, 0)
            hs.values(pe, UNITS, 0, 1)
            pe.wait_ge(z_ready, 1)
            for t in range(TILES + 1):
                if t < TILES:
                    if t >= 2:
                        pe.wait_ge(zt_ready, t - 1)
                    for j, n in enumerate(ROWS_OUT):
                        ins = nc.tensor.transpose(core.ps[t % 2][0:n, j * P:(j + 1) * P], z[:, t, j * P:j * P + n], core.ident[:])
                    ins.then_inc(zt_full, 1)
                if t >= 1:
                    pe.wait_ge(zt_ready, t)
                    if t >= 3:
                        pe.wait_ge(y_added, t - 2)
                    for j, n in enumerate(ROWS_OUT):
                        ins = nc.tensor.matmul(core.ps[2 + (t - 1) % 2][:, 0:P], z_t[0:n, (t - 1) % 2, j, :], wo[0:n, j, :],
                                               start=(j == 0), stop=(j == 2))
                    ins.then_inc(y_full, 1)

        @block.scalar
        def _(act):
            act_rstd(core, act, stat, var_ready, rstd_ready, 1)
            act_copy_transposed(core, act, core.xt, xt_full, xt_copied)
            act.wait_ge(gates_full, 1)
            for i in range(3):
                n = min(GB, TILES - i * GB)
                for which in range(2):
                    ins = nc.scalar.activation(gate[:].rearrange("p (w t h) e -> p w t h e", w=2, h=H)[:, which, i * GB:i * GB + n],
                                               core.ps[2 + i][:, 0:n * 80].rearrange("p (t w h e) -> p t w h e", w=2, h=H, e=E)[:, :, which],
                                               ACT.Sigmoid)
                ins.then_inc(gates_ready, 1)
            hs.act_seed(act)

            def place(unit, b, m, src):
                chunk = slice((m // 2) * CHUNK, (m // 2 + 1) * CHUNK)
                act.wait_ge(qk_full, unit * 4 + m + 1)
                if m % 2 == 0:
                    for h in range(2):
                        rows = slice(64 * h, 64 * h + 64)
                        ins = nc.scalar.copy(hs.qz[rows, b, h, chunk], src[rows, :])
                else:
                    ins = nc.scalar.copy(hs.kt[:, b, chunk], src)
                ins.then_inc(qk_ready, 1)

            for m in range(4):
                place(0, 0, m, core.ps[4 + m])
            hs.act_split_values(act, 0, 0, (v_ready, T))
            with act.Fori(0, PAIRS) as pair:
                for b in range(BATCH):
                    u = pair * BATCH + b
                    for i in range(hs.SLOTS):
                        if i >= 12:
                            place(u + 1, 1 - b, i - 12, spare[i % 2])
                        hs.act_hi(act, u, i, 0)
                        hs.act_exp(act, u, i)
                        hs.act_hi(act, u, i, 1)
                        if i == 13:
                            hs.act_split_values(act, u + 1, 1 - b, (v_ready, (u + 2) * T))
            for g in range(2):
                hs.act_hi(act, UNITS, 0, g)
            for t in range(TILES):
                act.wait_ge(zt_full, t + 1)
                if t >= 2:
                    act.wait_ge(y_full, t - 1)
                nc.scalar.copy(z_t[:, t % 2, 0:2].rearrange("p j c -> p (j c)"), core.ps[t % 2][:, 0:2 * P])
                n = ROWS_OUT[2]
                nc.scalar.copy(z_t[0:n, t % 2, 2], core.ps[t % 2][0:n, 2 * P:3 * P]).then_inc(zt_ready, 1)

        @block.gpsimd
        def _(pool):
            g = nc.gpsimd
            hs.fill(pool)
            g.memset(w[:, 3 * H:, :], 0.0).then_inc(padded, 1)
            step = Chain(pool, pool_step)
            step(g.memset(z[:], 0.0))

            def sum_tile(unit, t, first=False):
                if t == 0 and not first:
                    pool.wait_ge(qk_full, unit * 4)
                for kind in range(2):
                    pool.wait_ge(product_ready, unit * PIECES + t * 6 + kind * 2 + 2)
                    part = qk_product[:, t % 2, kind]
                    step(g.tensor_tensor(part[:, :, 0:2], part[:, :, 0:2], part[:, :, 2:4], ALU.add))
                    step(g.tensor_tensor(part[:, :, 0], part[:, :, 0], part[:, :, 1], ALU.add))
                    g.tensor_tensor(tok[:, kind, t], part[:, :, 0], part[:, :, 4], ALU.add).then_inc(tok_ready, 1)

            def route(unit, pair, b, i):
                t = (i - 3) // 2
                own, of_pair = (b, pair) if i >= 3 else (1 - b, pair - 1 + b)
                tile = own * T + t % T
                pool.wait_ge(hs.o_ready, unit * T + t + 3)
                step(g.tensor_tensor(routed[:], hs.o[:, own, t % T].unsqueeze(2).to_broadcast([P, 2, E, D]),
                                     mask[:, bass.ds(of_pair * 2 + (TILES + tile) * H, 2), :].unsqueeze(3).to_broadcast([P, 2, E, D]),
                                     ALU.mult))
                for h in range(2):
                    step(g.tensor_tensor(z[:, tile, :], z[:, tile, :], routed[:, h].rearrange("p e c -> p (e c)"), ALU.add))

            for t in range(T):
                sum_tile(0, t, True)
            hs.pool_split_values(pool, 0, 0)
            with step.loop(PAIRS, BATCH * (T * 4 + T * 3)) as pair:
                for b in range(BATCH):
                    u = pair * BATCH + b
                    for i in range(hs.SLOTS):
                        if i % 2:
                            route(u, pair, b, i)
                        if i in DONE:
                            sum_tile(u + 1, DONE[i])
                        if i == 13:
                            hs.pool_split_values(pool, u + 1, 1 - b)
            route(UNITS, PAIRS, 0, 1)
            pool.sem_inc(z_ready, 1)

        @block.vector
        def _(dve):
            v = nc.vector
            step = Chain(dve, dve_step)
            step(dve_norm(core, step, core.x, core.xn, square, stat, 1e-5, var_ready, rstd_ready, 1))
            dve.sem_inc(normed, 1)
            for e in range(E):
                step(v.memset(mask[:, :, e], float(E - 1 - e)))
            dve.wait_ge(gates_ready, 3)
            n = 2 * TILES * H
            for e in range(E - 1):
                rest = E - 1 - e
                step(v.tensor_tensor(beats[:, :, 0:rest], gate[:, :, e].unsqueeze(2).to_broadcast([P, n, rest]), gate[:, :, e + 1:E],
                                     ALU.is_ge))
                step(v.tensor_tensor(mask[:, :, e + 1:E], mask[:, :, e + 1:E], beats[:, :, 0:rest], ALU.add))
                step(v.tensor_reduce(lost[:], beats[:, :, 0:rest], AX.X, ALU.add))
                step(v.tensor_tensor(mask[:, :, e], mask[:, :, e], lost[:], ALU.subtract))
            step(v.tensor_scalar(mask[:], mask[:], float(TOP), None, ALU.is_lt))
            step(v.tensor_tensor(gate[:], gate[:], mask[:], ALU.mult))
            step(v.tensor_scalar(by_which(gate)[:, 1], by_which(gate)[:, 1], float(D) ** -0.5, None, ALU.mult))

            def apply_gates(unit, pair, b, n, src, first=False):
                t, kind, h = n // 6, n // 2 % 3, n % 2
                dve.wait_ge(proj_full, unit * PIECES + n + 1)
                if h == 0 and not (first and t < 2):
                    if kind < 2:
                        dve.wait_ge(tok_ready, unit * 16 + (t - 2) * 2 + kind + 1)
                    else:
                        dve.wait_ge(v_ready, unit * T + t - 1)
                product = qk_product[:, t % 2, kind, h] if kind < 2 else v_product[:, t % 2, h]
                at = ((TILES if kind == 0 else 0) + b * T + t) * H + h
                v.tensor_tensor(product, src[:, 0:ED].rearrange("p (e c) -> p e c", c=D),
                                gate[:, bass.ds(pair * 2 + at, 1), :].rearrange("p a e -> p (a e)").unsqueeze(2).to_broadcast([P, E, D]),
                                ALU.mult).then_inc(product_ready, 1)

            def sum_values(unit, t, first=False):
                if t == 0 and not first:
                    dve.wait_ge(hs.v_split, unit)
                dve.wait_ge(product_ready, unit * PIECES + t * 6 + 6)
                v.tensor_reduce(hs.v[:, t, :, 0:D], v_product[:, t % 2].rearrange("p h e c -> p h c e"), AX.X,
                                ALU.add).then_inc(v_ready, 1)

            hs.dve_seed(dve)
            for n in range(PIECES):
                if n % 6 == 2 and n >= 6:
                    sum_values(0, n // 6 - 1, True)
                apply_gates(0, 0, 0, n, core.ps[n % 4], True)
            sum_values(0, T - 1, True)
            with dve.Fori(0, PAIRS) as pair:
                for b in range(BATCH):
                    u = pair * BATCH + b
                    for i in range(hs.SLOTS):

                        def piece(k):
                            if i * PER_SLOT + k < PIECES:
                                apply_gates(u + 1, pair + b, 1 - b, i * PER_SLOT + k, spare[k % 2])

                        hs.dve_max(dve, u, i)
                        piece(0)
                        hs.dve_lo(dve, u, i, 0)
                        piece(1)
                        piece(2)
                        if i % 2:
                            hs.dve_normalise(dve, u, b, i)
                        hs.dve_lo(dve, u, i, 1)
                        piece(3)
                        if i - 1 in DONE:
                            sum_values(u + 1, DONE[i - 1])
            for g in range(2):
                hs.dve_lo(dve, UNITS, 0, g)
            hs.dve_normalise(dve, UNITS, 0, 1)
            for t in range(TILES):
                dve.wait_ge(y_full, t + 1)
                v.tensor_tensor(core.x[:, t], core.x[:, t], core.ps[2 + t % 2][:, 0:P], ALU.add).then_inc(y_added, 1)


def ssm_stage(core):
    nc, d = core.nc, core.dram
    K, H = 32, 8
    TAPS = 4
    BLOCKS = 2
    ORDER = (4, 0, 1, 2, 3)
    TURN_HI = 6.28125
    TURN_LO = 2 * np.pi - TURN_HI
    ROUND = 1.5 * 2.0 ** 23
    tag = "ss_"
    with ExitStack() as ctx:
        sb = lambda name, shape, dt=F32: ctx.enter_context(nc.sbuf_tensor(tag + name, shape, dt))
        sem = lambda name: core.semaphore(ctx, tag + name)
        w_in = sb("w_in", [P, 4 * P + K])
        taps, taps_s = sb("taps", [P, 4, TAPS + 1]), sb("taps_s", [K, TAPS + 1])
        theta = sb("theta", [P, BLOCKS])
        slopes, scale, dist = sb("slopes", [K, 8]), sb("scale", [K, 1]), sb("dist", [K, SEQ])
        logits = sb("logits", [P, 3])
        mix = sb("mix", [P, 8])
        w_rep, norm = sb("w_rep", [P, 2, H]), sb("norm", [P, 2])
        w_diag = sb("w_diag", [P, 2, P])
        head = sb("head", [P, 16])
        spread, gather, eps_eye = sb("spread", [P, BLOCKS, P]), sb("gather", [P, BLOCKS, K]), sb("eps_eye", [K, K])
        w_out = sb("w_out", [P, BLOCKS, P])
        square = sb("square", [P, TILES, P])
        stat = sb("stat", [P, 4, TILES])
        raw = [sb(f"raw{i}", [P, BATCH, SEQ + TAPS - 1]) for i in range(2)]
        score = sb("score", [K, BATCH, SEQ])
        weight = sb("weight", [K, SEQ])
        den = sb("den", [K, BATCH, SEQ])
        value = [sb(f"value{j}", [P, BATCH, SEQ]) for j in range(BLOCKS)]
        gate = [sb(f"gate{j}", [P, BATCH, SEQ]) for j in range(BLOCKS)]
        angle, poly = square[:].rearrange("p t c -> p (t c)"), sb("poly", [P, TOKENS])
        sin, cos = sb("sin", [P, TOKENS]), sb("cos", [P, TOKENS])
        num = [[sb(f"num{j}{i}", [P, BATCH, SEQ]) for i in range(2)] for j in range(BLOCKS)]
        factor = sb("factor", [P, CHUNK])
        ones = sb("ones", [P, SEQ])
        flat = lambda t: t[:].rearrange("p b s -> p (b s)")

        loads = sem("loads")
        var_ready, rstd_ready, normed = sem("var_ready"), sem("rstd_ready"), sem("normed")
        xt_full, xt_copied = sem("xt_full"), sem("xt_copied")
        raw_full, raw_ready, conv_done = sem("raw_full"), sem("raw_ready"), sem("conv_done")
        small_ready, small_exp, small_ln = sem("small_ready"), sem("small_exp"), sem("small_ln")
        score_ready, weights_ready, pw_ready = sem("score_ready"), sem("weights_ready"), sem("pw_ready")
        spread_full, spread_used = sem("spread_full"), sem("spread_used")
        angle_ready, waves_ready, num_ready, squares_ready = sem("angle_ready"), sem("waves_ready"), sem("num_ready"), sem("squares_ready")
        squares_used, power_full, power_inv, factor_ready = sem("squares_used"), sem("power_full"), sem("power_inv"), sem("factor_ready")
        gates_ready, mixed_full, mixed_read, gated_ready = sem("gates_ready"), sem("mixed_full"), sem("mixed_read"), sem("gated_ready")
        out_full = sem("out_full")
        dve_step, act_step = sem("dve_step"), sem("act_step")
        banks4 = core.banks[:, 4:8, :].rearrange("p k n -> p (k n)")
        banks0 = core.banks[:, 0:4, :].rearrange("p k n -> p (k n)")
        block = core.block(ctx)
        LOADS = 16

        @block.sync
        def _(sp):
            pairs = ((w_in[:], d["ss_in"]), (taps[:], d["ss_taps"][0:512, :].rearrange("(m p) k -> p m k", p=P)),
                     (taps_s[:], d["ss_taps"][512:544, :]), (theta[:], d["ss_theta"].rearrange("j p -> p j")),
                     (slopes[:, 0:1], d["ss_slopes"].unsqueeze(1)), (scale[:], d["ss_scale"].unsqueeze(1)), (dist[:], d["ss_dist"]),
                     (logits[:], d["ss_logits"].partition_broadcast(P)), (w_rep[:], d["ss_w"].rearrange("i p h -> p i h")),
                     (norm[:], d["ss_norm"].rearrange("i p -> p i")), (head[:], d["head_mask"]),
                     (spread[:], d["ss_spread"]), (gather[:], d["ss_gather"]), (eps_eye[:], d["ss_eps_eye"]),
                     (w_out[:], d["ss_out"].rearrange("(j p) c -> p j c", p=P)), (ones[:], d["ones"].partition_broadcast(P)))
            assert len(pairs) == LOADS
            for dst, src in pairs:
                with nc.allow_non_contiguous_dma("small constants"):
                    sp.dma_start(dst, src).then_inc(loads, 16)

        @block.tensor
        def _(pe):
            pe_transpose_tiles(core, pe, core.xn, (normed, 1), xt_full, (xt_copied, 0))
            pe.wait_ge(xt_copied, CHUNKS)
            pe.wait_ge(loads, LOADS * 16)
            for i, m in enumerate(ORDER):
                n = K if m == 4 else P
                for c in range(CHUNKS):
                    if i:
                        pe.wait_ge(raw_ready, (i - 1) * CHUNKS + c + 1)
                    nc.tensor.matmul(core.ps[c][0:n, :], w_in[:, m * P:m * P + n], core.xt[:, c * CHUNK:(c + 1) * CHUNK],
                                     start=True, stop=True).then_inc(raw_full, 1)
            pe.wait_ge(pw_ready, 1)
            for j in range(BLOCKS):
                if j:
                    pe.wait_ge(spread_used, 1)
                for c in range(CHUNKS):
                    ins = nc.tensor.matmul(core.ps[4 + c], spread[0:K, j, :], flat(score)[:, c * CHUNK:(c + 1) * CHUNK],
                                           start=True, stop=True)
                ins.then_inc(spread_full, 1)
            pe.wait_ge(raw_ready, len(ORDER) * CHUNKS)
            for j in range(BLOCKS):
                pe.wait_ge(squares_ready, j + 1)
                for c in range(CHUNKS):
                    out = core.ps[0][K * c:K * (c + 1), :]
                    for i, sq in enumerate((sin, cos)):
                        ins = nc.tensor.matmul(out, gather[:, j, :], sq[:, c * CHUNK:(c + 1) * CHUNK],
                                               start=(j == 0 and i == 0), stop=False, tile_position=(0, K * c),
                                               skip_group_check=True)
                    if j == BLOCKS - 1:
                        ins = nc.tensor.matmul(out, eps_eye[:], flat(den)[:, c * CHUNK:(c + 1) * CHUNK], start=False, stop=True,
                                               tile_position=(0, K * c), skip_group_check=True)
                ins.then_inc(squares_used, 1)
            pe.wait_ge(factor_ready, 1)
            pe.wait_ge(spread_used, 2)
            for j in range(BLOCKS):
                if j:
                    pe.wait_ge(mixed_read, 1)
                for c in range(CHUNKS):
                    nc.tensor.matmul(core.ps[4 + c], spread[K * c:K * (c + 1), j, :], factor[K * c:K * (c + 1), :], start=True, stop=True)
                    for i in range(2):
                        ins = nc.tensor.matmul(core.ps[c], w_diag[:, i, :], flat(num[j][i])[:, c * CHUNK:(c + 1) * CHUNK],
                                               start=(i == 0), stop=(i == 1))
                ins.then_inc(mixed_full, 1)
            pe.wait_ge(mixed_read, 2)
            for t in range(TILES):
                for j in range(BLOCKS):
                    ins = nc.tensor.matmul(core.ps[4 + t // 4][:, (t % 4) * P:(t % 4 + 1) * P], flat(gate[j])[:, t * P:(t + 1) * P],
                                           w_out[:, j, :], start=(j == 0), stop=(j == 1))
            ins.then_inc(out_full, 1)

        @block.scalar
        def _(act):
            act_rstd(core, act, stat, var_ready, rstd_ready, 1)
            step = Chain(act, act_step)
            act_copy_transposed(core, act, core.xt, xt_full, xt_copied)
            act.wait_ge(small_ready, 1)
            nc.scalar.activation(slopes[:, 2:3], slopes[:, 1:2], ACT.Exp)
            nc.scalar.activation(mix[:, 0:3], mix[:, 0:3], ACT.Exp).then_inc(small_exp, 1)
            act.wait_ge(small_ready, 2)
            nc.scalar.activation(slopes[:, 4:5], slopes[:, 3:4], ACT.Ln).then_inc(small_ln, 1)
            act.wait_ge(small_ready, 3)
            nc.scalar.activation(weight[:], dist[:], ACT.Exp, scale=slopes[:, 7:8]).then_inc(weights_ready, 1)
            for i, m in enumerate(ORDER):
                n = K if m == 4 else P
                if i >= 2:
                    act.wait_ge(conv_done, i - 1)
                for c in range(CHUNKS):
                    act.wait_ge(raw_full, i * CHUNKS + c + 1)
                    at = TAPS - 1 + (c % 2) * CHUNK
                    nc.scalar.copy(raw[i % 2][0:n, c // 2, at:at + CHUNK], core.ps[c][0:n, :]).then_inc(raw_ready, 1)
                if i == 0:
                    act.wait_ge(score_ready, 1)
                    nc.scalar.activation(flat(score), flat(score), ACT.Exp).then_inc(weights_ready, 1)
            for j in range(BLOCKS):
                act.wait_ge(angle_ready, j + 1)
                if j:
                    act.wait_ge(squares_used, 1)
                nc.scalar.activation(sin[:], angle, ACT.Sin)
                step(nc.scalar.activation(cos[:], angle, ACT.Sin, scale=0.5))
                nc.scalar.activation(cos[:], cos[:], ACT.Square).then_inc(waves_ready, 1)
                act.wait_ge(num_ready, j + 1)
                for i, sq in enumerate((sin, cos)):
                    ins = nc.scalar.activation(sq[:], flat(num[j][i]), ACT.Square)
                ins.then_inc(squares_ready, 1)
            act.wait_ge(power_inv, 1)
            nc.scalar.activation(factor[:], factor[:], ACT.Sqrt).then_inc(factor_ready, 1)
            for j in range(BLOCKS):
                act.wait_ge(conv_done, 4 + j)
                nc.scalar.activation(flat(gate[j]), flat(gate[j]), ACT.Silu).then_inc(gates_ready, 1)

        @block.vector
        def _(dve):
            v = nc.vector
            step = Chain(dve, dve_step)
            for i in range(2):
                step(v.memset(raw[i][:, :, 0:TAPS - 1], 0.0))
            step(dve_norm(core, step, core.x, core.xn, square, stat, 1e-5, var_ready, rstd_ready, 1))
            dve.sem_inc(normed, 1)
            dve.wait_ge(loads, LOADS * 16)
            step(v.tensor_scalar(slopes[:, 1:2], slopes[:, 0:1], -1.0, None, ALU.mult))
            step(v.tensor_tensor(slopes[:, 1:2], slopes[:, 1:2], slopes[:, 0:1], ALU.min))
            step(v.tensor_reduce(mix[:, 3:4], logits[:], AX.X, ALU.max))
            step(v.tensor_scalar(mix[:, 0:3], logits[:], mix[:, 3:4], None, ALU.subtract))
            dve.sem_inc(small_ready, 1)
            dve.wait_ge(small_exp, 1)
            step(v.tensor_reduce(mix[:, 3:4], mix[:, 0:3], AX.X, ALU.add))
            step(v.reciprocal(mix[:, 4:5], mix[:, 3:4]))
            step(v.tensor_scalar(mix[:, 0:3], mix[:, 0:3], mix[:, 4:5], None, ALU.mult))
            step(v.tensor_scalar(mix[:, 5:6], mix[:, 2:3], -1.0, None, ALU.mult))
            step(v.tensor_scalar(slopes[:, 3:4], slopes[:, 2:3], 1.0, None, ALU.add))
            dve.sem_inc(small_ready, 1)
            step(v.tensor_scalar(slopes[:, 5:6], slopes[:, 3:4], -1.0, None, ALU.add))
            step(v.tensor_scalar(slopes[:, 6:7], slopes[:, 5:6], 0.0, None, ALU.is_equal))
            step(v.tensor_tensor(slopes[:, 6:7], slopes[:, 6:7], slopes[:, 2:3], ALU.mult))
            step(v.tensor_scalar(slopes[:, 5:6], slopes[:, 5:6], 1e-20, None, ALU.max))
            step(v.reciprocal(slopes[:, 7:8], slopes[:, 5:6]))
            step(v.tensor_tensor(slopes[:, 7:8], slopes[:, 7:8], slopes[:, 2:3], ALU.mult))
            dve.wait_ge(small_ln, 1)
            step(v.tensor_tensor(slopes[:, 7:8], slopes[:, 7:8], slopes[:, 4:5], ALU.mult))
            step(v.tensor_tensor(slopes[:, 7:8], slopes[:, 7:8], slopes[:, 6:7], ALU.add))
            step(v.tensor_scalar(slopes[:, 5:6], slopes[:, 0:1], 0.0, None, ALU.max))
            step(v.tensor_tensor(slopes[:, 7:8], slopes[:, 7:8], slopes[:, 5:6], ALU.add))
            step(v.tensor_scalar(slopes[:, 7:8], slopes[:, 7:8], -1.0, None, ALU.mult))
            dve.sem_inc(small_ready, 1)
            for i in range(2):
                step(v.tensor_tensor(w_diag[:, i].rearrange("p (k h) -> p k h", h=H), head[:].unsqueeze(2).to_broadcast([P, 16, H]),
                                     w_rep[:, i].unsqueeze(1).to_broadcast([P, 16, H]), ALU.mult))
                step(v.tensor_scalar(w_diag[:, i], w_diag[:, i], norm[:, i:i + 1], None, ALU.mult))
            targets = {4: score, 0: value[0], 1: value[1], 2: gate[0], 3: gate[1]}

            def convolve(i):
                m = ORDER[i]
                out, tap = targets[m], (taps_s if m == 4 else taps[:, m])
                n = K if m == 4 else P
                dve.wait_ge(raw_ready, (i + 1) * CHUNKS)
                step(v.tensor_scalar(out[:], raw[i % 2][0:n, :, 0:SEQ], tap[:, 0:1], tap[:, TAPS:TAPS + 1], ALU.mult, ALU.add))
                for k in range(1, TAPS):
                    step(v.scalar_tensor_tensor(out=out[:], in0=raw[i % 2][0:n, :, k:k + SEQ], scalar=tap[:, k:k + 1], in1=out[:],
                                                op0=ALU.mult, op1=ALU.add))
                dve.sem_inc(conv_done, 1)

            convolve(0)
            step(v.tensor_scalar(score[:], score[:], scale[:], -20.0, ALU.mult, ALU.max))
            step(v.tensor_scalar(score[:], score[:], 20.0, None, ALU.min))
            dve.sem_inc(score_ready, 1)
            convolve(1)
            dve.wait_ge(weights_ready, 2)
            step(v.tensor_tensor(score[:], score[:], weight[:].unsqueeze(1).to_broadcast([K, BATCH, SEQ]), ALU.mult))
            dve.sem_inc(pw_ready, 1)
            for b in range(BATCH):
                step(v.tensor_tensor_scan(den[:, b], ones[0:K, :], score[:, b], 0.0, ALU.mult, ALU.add))
            step(v.tensor_scalar(den[:], den[:], 1e-4, None, ALU.max))
            step(v.tensor_tensor(den[:], den[:], den[:], ALU.mult))
            for j in range(BLOCKS):
                x = flat(value[j])
                step(v.tensor_scalar(angle, x, theta[:, j:j + 1], None, ALU.mult))
                step(v.tensor_scalar(poly[:], angle, 1.0 / (2 * np.pi), ROUND, ALU.mult, ALU.add))
                step(v.tensor_scalar(poly[:], poly[:], -ROUND, None, ALU.add))
                step(v.scalar_tensor_tensor(out=angle, in0=poly[:], scalar=-TURN_HI, in1=angle, op0=ALU.mult, op1=ALU.add))
                step(v.scalar_tensor_tensor(out=angle, in0=poly[:], scalar=-TURN_LO, in1=angle, op0=ALU.mult, op1=ALU.add))
                step(v.tensor_scalar(angle, angle, 3.1415925, -3.1415925, ALU.min, ALU.max))
                dve.sem_inc(angle_ready, 1)
                step(v.tensor_scalar(poly[:], x, mix[:, 5:6], mix[:, 1:2], ALU.mult, ALU.add))
                step(v.tensor_tensor(poly[:], poly[:], x, ALU.mult))
                step(v.tensor_scalar(poly[:], poly[:], mix[:, 0:1], None, ALU.add))
                dve.wait_ge(spread_full, j + 1)
                step(v.tensor_tensor(poly[:], poly[:], banks4, ALU.mult))
                dve.sem_inc(spread_used, 1)
                convolve(2 + j)
                dve.wait_ge(waves_ready, j + 1)
                step(v.tensor_scalar(cos[:], cos[:], -2.0, 1.0, ALU.mult, ALU.add))
                step(v.tensor_tensor(cos[:], cos[:], poly[:], ALU.mult))
                step(v.tensor_tensor(sin[:], sin[:], poly[:], ALU.mult))
                for i, wave in enumerate((cos, sin)):
                    for b in range(BATCH):
                        step(v.tensor_tensor_scan(num[j][i][:, b], ones[:], wave[:, b * SEQ:(b + 1) * SEQ], 0.0, ALU.mult, ALU.add))
                dve.sem_inc(num_ready, 1)
            convolve(4)
            dve.wait_ge(squares_used, 2)
            step(v.reciprocal(factor[:], core.ps[0]))
            dve.sem_inc(power_inv, 1)
            for j in range(BLOCKS):
                dve.wait_ge(gates_ready, j + 1)
                dve.wait_ge(mixed_full, j + 1)
                step(v.tensor_tensor(flat(gate[j]), flat(gate[j]), banks4, ALU.mult))
                step(v.tensor_tensor(flat(gate[j]), flat(gate[j]), banks0, ALU.mult))
                dve.sem_inc(mixed_read, 1)
            dve.wait_ge(out_full, 1)
            step(v.tensor_tensor(core.x[:], core.x[:], banks4.rearrange("p (t c) -> p t c", c=P), ALU.add))


def program(nc, dram):
    with ExitStack() as ctx:
        core = Core(nc, dram, ctx)
        load_stage(core)
        rwkv_stage(core)
        routed_ffn_stage(core, "f0_")
        linear_attention_stage(core)
        routed_ffn_stage(core, "f1_")
        attention_stage(core)
        expert_attention_stage(core, "g0_")
        ssm_stage(core)
        expert_attention_stage(core, "g1_")
        store_stage(core)


def kernel(**inputs):
    import numpy as _np
    import concourse.bacc as _bacc
    from concourse import mybir as _mybir
    from concourse.bass_utils import run_bass_kernel_spmd as _run

    nc = _bacc.Bacc("TRN2", target_bir_lowering=False, num_devices=1)
    arrays, dram = {}, {}

    def give(name, a):
        a = _np.ascontiguousarray(a)
        arrays[f"in_{name}"] = a
        dram[name] = nc.dram_tensor(f"in_{name}", a.shape, _mybir.dt.from_np(a.dtype), kind="ExternalInput").ap()

    give("x", inputs["L0_attn_a_x"])
    give("identity", _np.eye(P, dtype=_np.float32))
    for name in ("W_router", "W1", "b1", "Wo", "bo"):
        give(name, inputs["L0_ffn_" + name])
    give("gamma", inputs["L0_ffn_ln_gamma"])
    give("beta", inputs["L0_ffn_ln_beta"])
    def pair_swapped(a):
        return a.reshape((16, 2, 32) + a.shape[1:])[:, ::-1].reshape(a.shape)

    wq, wk, wv = (_np.asarray(inputs["L1_attn_a_W" + n]) for n in "qkv")
    bq, bk = (_np.asarray(inputs["L1_attn_a_b" + n]) for n in "qk")
    give("at_w", _np.stack([a.T for a in (wq, pair_swapped(wq), wk, pair_swapped(wk), wv)]))
    give("at_bias", _np.stack([a.reshape(8, P) for a in (bq, pair_swapped(bq), bk, pair_swapped(bk))]))
    give("at_bv", inputs["L1_attn_a_bv"])
    give("at_wo", _np.asarray(inputs["L1_attn_a_Wo"]).T)
    give("at_bo", inputs["L1_attn_a_bo"])
    freq = (1.0 / _np.float32(10000.0) ** (_np.arange(0, 64, 2, dtype=_np.float32) / _np.float32(64))).astype(_np.float32)
    angle = (freq[:, None] * _np.arange(SEQ, dtype=_np.float32)[None, :]).astype(_np.float32)
    cos = _np.tile(_np.cos(angle), (4, 1)).astype(_np.float32)
    sin = _np.concatenate([-_np.sin(angle), _np.sin(angle)] * 2).astype(_np.float32)
    give("rope", _np.stack([cos / 8, sin / 8, cos, sin]).astype(_np.float32))


    wkv = _np.asarray(inputs["L1_ffn_Wkv"])
    half = wkv.shape[1] // 2
    give("ex_w", _np.stack([_np.asarray(inputs["L1_ffn_Wq"]), wkv[:, :half], wkv[:, half:]]))
    give("ex_gate", _np.concatenate([_np.asarray(inputs["L1_ffn_Ws"]), _np.asarray(inputs["L1_ffn_Wd"])], axis=1))
    give("ex_wo", _np.asarray(inputs["L1_ffn_Wo"]).reshape(64, 5, P).transpose(1, 0, 2).reshape(320, P))
    for name in ("wq", "wk", "wv", "wo"):
        give("la_" + name, _np.asarray(inputs["L0_attn_b_" + name]).reshape(P, P))
    for name in ("w1", "b1", "w2", "b2"):
        give("la_" + name, inputs["L0_attn_b_" + name])
    give("la_gamma", inputs["L0_attn_b_gamma1"])
    give("la_beta", inputs["L0_attn_b_beta1"])
    give("head_mask", (_np.arange(P)[:, None] // 8 == _np.arange(16)[None, :]).astype(_np.float32))
    ssm = lambda name: _np.asarray(inputs["L1_attn_b_" + name])
    give("ss_in", ssm("in_proj_w"))
    give("ss_taps", _np.concatenate([ssm("conv_k").reshape(4, -1).T, ssm("conv_b").reshape(-1, 1)], axis=1))
    give("ss_theta", ssm("theta").reshape(2, P))
    give("ss_slopes", _np.concatenate([ssm("decay_slopes"), ssm("anchor_slopes")]))
    give("ss_scale", ssm("score_scale"))
    at = _np.arange(SEQ, dtype=_np.float32)
    give("ss_dist", _np.stack([SEQ - 1 - at] * 28 + [at] * 4))
    give("ss_logits", ssm("deriv_logits"))
    give("ss_w", _np.stack([_np.tile(ssm("W_re"), (16, 1)), _np.tile(ssm("W_im"), (16, 1))]))
    give("ss_norm", _np.stack([_np.tile(ssm("norm_scale")[:8], 16), _np.tile(ssm("norm_scale")[8:], 16)]))
    group = _np.arange(P) // 8
    spread = (_np.arange(32)[:, None, None] == 16 * _np.arange(2)[None, :, None] + group[None, None, :]).astype(_np.float32)
    give("ss_spread", _np.tile(spread, (4, 1, 1)))
    give("ss_gather", spread.transpose(2, 1, 0) / _np.float32(16))
    give("ss_eps_eye", _np.eye(32, dtype=_np.float32) * _np.float32(1e-5))
    give("ss_out", ssm("out_proj_w"))
    give("ones", _np.ones(SEQ, _np.float32))
    rw = lambda name: _np.asarray(inputs["L0_attn_a_" + name])
    give("rw_w", _np.stack([rw("W_" + n).T for n in "rwkvabgo"]))
    give("rw_mix", _np.stack([rw("x_" + n) for n in "rwkvabg"], axis=1))
    give("rw_bo", rw("b_o"))
    give("rw_gn", _np.stack([rw("gn_w"), rw("gn_b")], axis=1))
    same = (group[:, None] == group[None, :]).astype(_np.float32)
    give("rw_same", same)
    channel = (_np.arange(P)[None, None, :] % 8 == _np.arange(8)[None, :, None]).astype(_np.float32)
    pick = same[:, None, :] * channel
    give("rw_pick", pick)
    give("rw_give", pick.transpose(2, 1, 0))
    pool2 = (group[:, None, None] + 16 * _np.arange(2)[None, :, None] == _np.arange(32)[None, None, :]).astype(_np.float32)
    give("rw_pool2", pool2)
    give("rw_spread2", _np.tile(pool2.transpose(2, 1, 0), (4, 1, 1)))
    give("rw_eye", _np.tile(_np.eye(8, dtype=_np.float32), (16, 1)))
    dram["out"] = nc.dram_tensor("out", (BATCH, SEQ, P), _mybir.dt.float32, kind="ExternalOutput").ap()
    program(nc, dram)
    return _run(nc, [arrays], core_ids=[0]).results[0]["out"]
```
